# Optimizing a Trainium2 kernel written in Bass

```python
import numpy as np
import jax
import jax.numpy as jnp

def _softmax(x, axis=-1):
    return jax.nn.softmax(x, axis=axis)

def _gelu(x):
    return jax.nn.gelu(x, approximate=True)

def _silu(x):
    return jax.nn.silu(x)

def _sigmoid(x):
    return jax.nn.sigmoid(x)

def _layernorm(x, axis=-1, eps=1e-05):
    m = jnp.mean(x, axis=axis, keepdims=True)
    v = jnp.var(x, axis=axis, keepdims=True)
    return (x - m) / jnp.sqrt(v + eps)

def _scatter_add(tgt, idx, src, axis=0):
    return tgt.at[idx].add(src)

def _segment_sum(src, seg, n):
    return jax.ops.segment_sum(src, seg, n)
kernel_name = 'mk_adj_resnorm_d2_adj_r2_4d058d'

def setup_inputs(seed: int=0):
    np.random.seed(seed)
    _w = jnp.asarray

    def _rec_inputs():
        import jax
        import jax.numpy as jnp
        _gk = jax.random.key(seed)
        x = -0.0005207 + 1.001 * jax.random.normal(jax.random.fold_in(_gk, 1), (3327, 256), jnp.float32)
        _a = jax.random.bernoulli(jax.random.fold_in(_gk, 2), 0.00120228, (3327, 3327))
        _af = _a.astype(jnp.float32)
        adj = _af
        return (x, adj)
    x, adj = _rec_inputs()

    def _L0_gnn_setup():
        import jax, jax.numpy as jnp
        import numpy as np
        N = 2048
        INPUT_DIM = 256
        KEY_DIM = 64
        OUT_DIM = 256
        N_HEADS = 8
        IDENTITY_BIAS = 0.01
        MASK_VAL = 1e+16

        def _xavier(key, shape, gain=np.sqrt(2.0)):
            std = gain * np.sqrt(2.0 / (shape[-2] + shape[-1]))
            return jax.random.normal(key, shape, dtype=jnp.float32) * np.float32(std)
        key = jax.random.key(seed)
        kx, ka, kk, kq, kv, ko = jax.random.split(key, 6)
        node_matrix = jax.random.normal(kx, (N, INPUT_DIM), dtype=jnp.float32)
        adjacency_matrix = jax.random.bernoulli(ka, 0.01, (N, N)).astype(jnp.float32)
        Wks = _xavier(kk, (N_HEADS, INPUT_DIM, KEY_DIM))
        Wqs = _xavier(kq, (N_HEADS, INPUT_DIM, KEY_DIM))
        Wvs = _xavier(kv, (N_HEADS, INPUT_DIM, KEY_DIM))
        Wo = _xavier(ko, (N_HEADS, KEY_DIM, OUT_DIM))
        return {'node_matrix': node_matrix, 'adjacency_matrix': adjacency_matrix, 'Wks': Wks, 'Wqs': Wqs, 'Wvs': Wvs, 'Wo': Wo}
    _L0_gnn_all = _L0_gnn_setup()
    _L0_gnn_in = {k: v for k, v in _L0_gnn_all.items() if k in ('Wks', 'Wqs', 'Wvs', 'Wo')}
    del _L0_gnn_all

    def _L1_gnn_setup():
        import jax, jax.numpy as jnp
        import numpy as np
        N = 3072
        D_IN = 256
        D_OUT = 256
        DENSITY = 0.005
        key = jax.random.key(seed)
        ks = jax.random.split(key, 12)
        x = jax.random.normal(ks[0], (N, D_IN), dtype=jnp.float32)
        adj_a = (jax.random.uniform(ks[1], (N, N)) < DENSITY).astype(jnp.float32)
        adj_b = (jax.random.uniform(ks[2], (N, N)) < DENSITY).astype(jnp.float32)
        W_sa = jax.random.normal(ks[3], (D_IN, D_OUT), dtype=jnp.float32) * (1.414 / np.sqrt(D_IN + D_OUT))
        a_sa = jax.random.normal(ks[4], (1, 2 * D_OUT), dtype=jnp.float32) * (1.414 / np.sqrt(1 + 2 * D_OUT))
        stdv = 1.0 / np.sqrt(D_OUT)
        W_gcnb = jax.random.uniform(ks[5], (D_IN, D_OUT), minval=-stdv, maxval=stdv, dtype=jnp.float32)
        b_gcnb = jax.random.uniform(ks[6], (D_OUT,), minval=-stdv, maxval=stdv, dtype=jnp.float32)
        s = 1.0 / np.sqrt(2 * D_IN)
        Wa = jax.random.uniform(ks[7], (1, 2 * D_IN), minval=-s, maxval=s, dtype=jnp.float32)
        ba = jax.random.uniform(ks[8], (1,), minval=-s, maxval=s, dtype=jnp.float32)
        Wb = jax.random.uniform(ks[9], (1, 2 * D_IN), minval=-s, maxval=s, dtype=jnp.float32)
        bb = jax.random.uniform(ks[10], (1,), minval=-s, maxval=s, dtype=jnp.float32)
        return {'x': x, 'adj_a': adj_a, 'adj_b': adj_b, 'W_sa': W_sa, 'a_sa': a_sa, 'W_gcnb': W_gcnb, 'b_gcnb': b_gcnb, 'Wa': Wa, 'ba': ba, 'Wb': Wb, 'bb': bb}
    _L1_gnn_all = _L1_gnn_setup()
    _L1_gnn_in = {k: v for k, v in _L1_gnn_all.items() if k in ('W_sa', 'a_sa', 'W_gcnb', 'b_gcnb', 'Wa', 'ba', 'Wb', 'bb')}
    del _L1_gnn_all
    return {'x': x, 'adj': adj, 'L0_gnn_Wks': _L0_gnn_in['Wks'], 'L0_gnn_Wqs': _L0_gnn_in['Wqs'], 'L0_gnn_Wvs': _L0_gnn_in['Wvs'], 'L0_gnn_Wo': _L0_gnn_in['Wo'], 'L1_gnn_W_sa': _L1_gnn_in['W_sa'], 'L1_gnn_a_sa': _L1_gnn_in['a_sa'], 'L1_gnn_W_gcnb': _L1_gnn_in['W_gcnb'], 'L1_gnn_b_gcnb': _L1_gnn_in['b_gcnb'], 'L1_gnn_Wa': _L1_gnn_in['Wa'], 'L1_gnn_ba': _L1_gnn_in['ba'], 'L1_gnn_Wb': _L1_gnn_in['Wb'], 'L1_gnn_bb': _L1_gnn_in['bb']}

def reference(x, adj, L0_gnn_Wks, L0_gnn_Wqs, L0_gnn_Wvs, L0_gnn_Wo, L1_gnn_W_sa, L1_gnn_a_sa, L1_gnn_W_gcnb, L1_gnn_b_gcnb, L1_gnn_Wa, L1_gnn_ba, L1_gnn_Wb, L1_gnn_bb):
    import jax
    import jax.numpy as jnp

    def _L0_gnn_ref(node_matrix, adjacency_matrix, Wks, Wqs, Wvs, Wo):
        import jax, jax.numpy as jnp
        import numpy as np
        N = 2048
        INPUT_DIM = 256
        KEY_DIM = 64
        OUT_DIM = 256
        N_HEADS = 8
        IDENTITY_BIAS = 0.01
        MASK_VAL = 1e+16

        def _xavier(key, shape, gain=np.sqrt(2.0)):
            std = gain * np.sqrt(2.0 / (shape[-2] + shape[-1]))
            return jax.random.normal(key, shape, dtype=jnp.float32) * np.float32(std)
        n = node_matrix.shape[0]
        kd = Wks.shape[-1]
        eye = jnp.eye(n, dtype=node_matrix.dtype)
        adj = jnp.maximum(adjacency_matrix, eye)
        q = jnp.einsum('nd,hdk->hnk', node_matrix, Wqs)
        k = jnp.einsum('nd,hdk->hnk', node_matrix, Wks)
        v = jnp.einsum('nd,hdk->hnk', node_matrix, Wvs)
        scores = jnp.einsum('hqk,hmk->hqm', q, k) * kd ** (-0.5)
        scores = scores + IDENTITY_BIAS * eye - MASK_VAL * (1.0 - adj)
        att = jax.nn.softmax(scores, axis=-1)
        return jnp.einsum('hqm,hmk,hko->qo', att, v, Wo)

    def _L1_gnn_ref(x, adj_a, adj_b, W_sa, a_sa, W_gcnb, b_gcnb, Wa, ba, Wb, bb):
        import jax, jax.numpy as jnp
        import numpy as np
        N = 3072
        D_IN = 256
        D_OUT = 256
        DENSITY = 0.005
        type_sum_a = adj_a @ x
        type_sum_b = adj_b @ x
        attn_a = jax.nn.sigmoid(jnp.concatenate([type_sum_a, x], axis=1) @ Wa.T + ba)
        attn_b = jax.nn.sigmoid(jnp.concatenate([type_sum_b, x], axis=1) @ Wb.T + bb)
        h = x @ W_sa
        Hd = h.shape[1]
        s_left = h @ a_sa[0, :Hd]
        s_right = h @ a_sa[0, Hd:]
        scores = s_left[:, None] + s_right[None, :]
        e = jnp.where(adj_a != 0, jnp.exp(-jax.nn.leaky_relu(scores, 0.01)), 0.0)
        attn = e / (jnp.sum(e, axis=1, keepdims=True) + 1e-05)
        x_a = attn @ h
        x_b = adj_b @ (x @ W_gcnb) + b_gcnb
        return jax.nn.sigmoid(attn_a * x_a + attn_b * x_b)
    x = _layernorm(x + _L0_gnn_ref(x, adj, L0_gnn_Wks, L0_gnn_Wqs, L0_gnn_Wvs, L0_gnn_Wo), axis=-1)
    x = _layernorm(x + _L1_gnn_ref(x, adj, adj, L1_gnn_W_sa, L1_gnn_a_sa, L1_gnn_W_gcnb, L1_gnn_b_gcnb, L1_gnn_Wa, L1_gnn_ba, L1_gnn_Wb, L1_gnn_bb), axis=-1)
    return x

_drawn_inputs = setup_inputs


def setup_inputs(seed=0):
    import zlib

    import numpy as np

    out = dict(_drawn_inputs(seed))
    spreads = {}
    factors = {'L1_gnn_b_gcnb': 8.0}
    for name, (base, spread) in spreads.items():
        noise = np.random.default_rng([zlib.crc32(name.encode()), seed]).standard_normal(out[name].shape)
        drawn = base * np.exp(spread * noise) if base else spread * noise
        out[name] = jnp.asarray(drawn.astype(out[name].dtype))
    for name, factor in factors.items():
        out[name] = (out[name] * factor).astype(out[name].dtype)
    return out
```

```python
from contextlib import ExitStack

import concourse.bass as bass
from concourse import mybir

F32 = mybir.dt.float32
ALU = mybir.AluOpType
ACT = mybir.ActivationFunctionType
AX_X = mybir.AxisListType.X
P = 128
BIG = 1e16


def adj_resnorm(nc, x, xT, adj, Wq, Wk, Wv, Wo, W_sa, W_saT, a_sa, W_gcn, b_gcn, Wab, bab, out):
    NP, D = x.shape
    NT = NP // P
    HK = Wq.shape[1]
    KD = 64
    NHP = HK // P
    DC = D // P
    NCH = 8
    CW = NP // NCH
    GROUPS = [4, 3, 3, 3, 4, 3, 3, 3]
    START = [sum(GROUPS[:g]) for g in range(8)]
    assert sum(GROUPS) == NT and NT % 2 == 0 and CW <= 512
    PROJ = 3 * NCH
    PER_HP = PROJ + NT * 2 * NCH
    EPS = 1e-5
    NORM0 = 3 * NT + 1
    HEAD1 = NORM0 + 5
    STEPS = 12
    LAST = HEAD1 + NT * STEPS + NORM0

    with ExitStack() as ctx:
        def sb(name, shape):
            return ctx.enter_context(nc.sbuf_tensor(name, shape, F32))

        def pb(name, shape):
            return ctx.enter_context(nc.psum_tensor(name, shape, F32))

        def sem(name):
            return ctx.enter_context(nc.semaphore(name))

        ident = sb("ident", [P, P])
        eye_bias = sb("eye_bias", [P, P])
        xs = sb("xs", [P, NT, D])
        big = sb("big", [P, 2 * NP])
        xTs = big[:, :].rearrange("p (c n) -> p c n", c=DC)
        wpair = sb("wpair", [P, 3, DC, P])
        wo_s = sb("wo_s", [P, D])
        QK = sb("QK", [P, 2 * NP])
        QT, KT = QK[:, 0:NP], QK[:, NP:2 * NP]
        V = sb("V", [P, NT, P])
        SR = V[:].rearrange("p t m -> p (t m)")
        qtile = sb("qtile", [P, P])
        bias = [sb(f"bias{u}", [P, NP]) for u in range(2)]
        prob = [sb(f"prob{h}", [P, NP]) for h in range(2)]
        PT = [sb(f"PT{h}", [P, NP]) for h in range(2)]
        negmax = sb("negmax", [P, 2])
        rowmax = sb("rowmax", [P, 2])
        rowsum = sb("rowsum", [P, 2])
        rinv = sb("rinv", [P, 2])
        oT = sb("oT", [P, P])
        stats = sb("stats", [P, NT, 6])
        mv = sb("mv", [P, NT, 2])
        std = sb("std", [P, NT])
        rstd = sb("rstd", [P, NT])
        wsa = sb("wsa", [P, DC, D])
        wsaT = sb("wsaT", [P, DC, D])
        asa = sb("asa", [P, DC, 2])
        wgcn = sb("wgcn", [P, DC, D])
        wab = sb("wab", [P, 2 * DC, 2])
        bab_b = sb("bab_b", [P, 2])
        bg_b = sb("bg_b", [P, D])
        coef = sb("coef", [P, DC, 4])
        ones = sb("ones", [P, P])
        wr_b = sb("wr_b", [P, DC, P])
        node = sb("node", [P, NT, 4])
        zs = sb("zs", [P, 2, D])
        zT = sb("zT", [P, 4, P])
        gate = sb("gate", [P, 2])
        esum = sb("esum", [P, 1])
        yt = sb("yt", [P, D])
        ys = QK[:, :].rearrange("p (t d) -> p t d", d=D)

        S = [pb(f"S{b}", [P, 512]) for b in range(4)]
        T = [pb(f"T{b}", [P, 512]) for b in range(2)]
        O = pb("O", [P, 512])
        R = pb("R", [P, 512])

        s_id = sem("s_id")
        s_x = sem("s_x")
        s_w = sem("s_w")
        s_adj = [sem(f"s_adj{u}") for u in range(2)]
        s_bias = [sem(f"s_bias{u}") for u in range(2)]
        s_bias_used = [sem(f"s_bias_used{u}") for u in range(2)]
        s_chunk = sem("s_chunk")
        s_taken = sem("s_taken")
        s_q = sem("s_q")
        s_max = sem("s_max")
        s_dve = sem("s_dve")
        s_exp = sem("s_exp")
        s_tr = [sem(f"s_tr{b}") for b in range(2)]
        s_cp = [sem(f"s_cp{b}") for b in range(2)]
        s_pv = sem("s_pv")
        s_oT = sem("s_oT")
        s_res = sem("s_res")
        s_acc = sem("s_acc")
        s_att = sem("s_att")
        s_v = sem("s_v")
        s_w1 = sem("s_w1")
        s_var = sem("s_var")
        s_std = sem("s_std")
        s_coef = sem("s_coef")
        s_xT = sem("s_xT")
        s_xTc = sem("s_xTc")
        s_sr = sem("s_sr")
        s_node = sem("s_node")
        s_adj1 = [sem(f"s_adj1{u}") for u in range(2)]
        s_leak = sem("s_leak")
        s_ee = sem("s_ee")
        s_z = sem("s_z")
        s_zs = sem("s_zs")
        s_zT = sem("s_zT")
        s_zTc = sem("s_zTc")
        s_f = sem("s_f")
        s_gz = sem("s_gz")
        s_ge = sem("s_ge")
        s_y = sem("s_y")
        s_ye = sem("s_ye")
        s_out = sem("s_out")

        with nc.Block() as block:
            @block.sync
            def _(sp):
                sp.dma_start(xs[:], x.rearrange("(t p) d -> p t d", p=P)).then_inc(s_x, 16)
                sp.dma_start(xTs, xT.rearrange("(c p) n -> p c n", p=P)).then_inc(s_x, 16)
                with sp.Fori(0, NHP) as hp:
                    sp.wait_ge(s_acc, hp * (2 * NT))
                    for w, W in enumerate((Wq, Wk, Wv)):
                        sp.dma_start(wpair[:, w], W.rearrange("(c p) (h m) -> h p c m", p=P, m=P)[bass.ds(hp, 1)].rearrange("h p c m -> (h p) c m")).then_inc(s_w, 16)
                    sp.dma_start(wo_s[:], Wo.rearrange("(h p) d -> h p d", p=P)[bass.ds(hp, 1)].rearrange("h p d -> (h p) d")).then_inc(s_w, 16)
                    with sp.Fori(0, NT // 2) as t2:
                        for u in range(2):
                            sp.wait_ge(s_bias_used[u], hp * (NT // 2) + t2)
                            sp.dma_start(bias[u][:], adj[bass.ds((t2 * 2 + u) * P, P), :]).then_inc(s_adj[u], 16)

                for dst, src in ((wsa[:], W_sa.rearrange("(c p) n -> p c n", p=P)), (wsaT[:], W_saT.rearrange("(c p) n -> p c n", p=P)),
                                 (asa[:], a_sa.rearrange("(c p) n -> p c n", p=P)), (wgcn[:], W_gcn.rearrange("(c p) n -> p c n", p=P)),
                                 (wab[:], Wab.rearrange("(c p) n -> p c n", p=P)), (bab_b[:], bab.partition_broadcast(P)),
                                 (bg_b[:], b_gcn.partition_broadcast(P))):
                    sp.dma_start(dst, src).then_inc(s_w1, 16)
                sp.wait_ge(s_acc, NHP * NT * 2)
                with sp.Fori(0, NT // 2) as t2:
                    for u in range(2):
                        sp.wait_ge(s_z, t2 * 4)
                        sp.dma_start(bias[u][:], adj[bass.ds((t2 * 2 + u) * P, P), :]).then_inc(s_adj1[u], 16)
                sp.wait_ge(s_var, 2)
                sp.wait_ge(s_v, LAST)
                sp.dma_start(out.rearrange("(t p) d -> p t d", p=P), ys[:]).then_inc(s_out, 16)
                sp.wait_ge(s_out, 16)

            @block.gpsimd
            def _(pool):
                pool.memset(ident[:], 0.0).then_inc(s_id, 1)
                pool.memset(eye_bias[:], -BIG).then_inc(s_id, 1)
                pool.wait_ge(s_id, 2)
                for m, one in ((ident, 1.0), (eye_bias, 0.01)):
                    pool.affine_select(out=m[:], in_=m[:], compare_op=ALU.not_equal, fill=one, base=0,
                                       pattern=[[-1, P]], channel_multiplier=1).then_inc(s_id, 1)

            @block.tensor
            def _(pe):
                pe.wait_ge(s_id, 4)
                pe.wait_ge(s_x, 32)
                with pe.Fori(0, NHP) as hp:
                    pe.wait_ge(s_w, hp * 64 + 64)
                    n = 0
                    for w in range(2):
                        for c in range(NCH):
                            pe.wait_ge(s_taken, hp * PER_HP + n + 1)
                            for dc in range(DC):
                                mm = nc.tensor.matmul(S[n % 4][:, 0:CW], wpair[:, w, dc, :], xTs[:, dc, c * CW:(c + 1) * CW],
                                                      start=dc == 0, stop=dc == DC - 1)
                            mm.then_inc(s_chunk, 1)
                            n += 1
                    for g in range(8):
                        pe.wait_ge(s_taken, hp * PER_HP + n + 1)
                        for b in range(GROUPS[g]):
                            k = START[g] + b
                            for dc in range(DC):
                                mm = nc.tensor.matmul(S[n % 4][:, b * P:(b + 1) * P], xTs[:, dc, k * P:(k + 1) * P],
                                                      wpair[:, 2, dc, :], start=dc == 0, stop=dc == DC - 1)
                        mm.then_inc(s_chunk, 1)
                        n += 1
                    with pe.Fori(0, NT) as i:
                        it = hp * NT + i
                        pe.wait_ge(s_q, it + 1)
                        for h in range(2):
                            for c in range(NCH):
                                m = h * NCH + c
                                pe.wait_ge(s_taken, hp * PER_HP + i * (2 * NCH) + PROJ + m + 1)
                                nc.tensor.matmul(S[m % 4][:, 0:CW], qtile[h * KD:(h + 1) * KD, :],
                                                 KT[h * KD:(h + 1) * KD, c * CW:(c + 1) * CW],
                                                 start=True, stop=True).then_inc(s_chunk, 1)
                        for h in range(2):
                            pe.wait_ge(s_exp, it * 2 + h + 1)

                            def pv(g):
                                pe.wait_ge(s_cp[g % 2], it * 8 + h * 4 + g // 2 + 1)
                                for b in range(GROUPS[g]):
                                    k = START[g] + b
                                    mm = nc.tensor.matmul(O[h * KD:(h + 1) * KD, 0:P], V[:, k, h * KD:(h + 1) * KD],
                                                          PT[h][:, k * P:(k + 1) * P], start=k == 0, stop=k == NT - 1)
                                return mm

                            for g in range(8):
                                pe.wait_ge(s_cp[g % 2], it * 8 + h * 4 + g // 2)
                                for b in range(GROUPS[g]):
                                    k = START[g] + b
                                    mm = nc.tensor.transpose(T[g % 2][:, b * P:(b + 1) * P], prob[h][:, k * P:(k + 1) * P], ident[:])
                                mm.then_inc(s_tr[g % 2], 1)
                                if g:
                                    pv(g - 1)
                            pv(7).then_inc(s_pv, 1)
                            pe.wait_ge(s_oT, it * 2 + h + 1)
                            pe.wait_ge(s_acc, it * 2 + h)
                            nc.tensor.matmul(R[:, 0:D], oT[h * KD:(h + 1) * KD, :], wo_s[h * KD:(h + 1) * KD, :],
                                             start=True, stop=True).then_inc(s_res, 1)

                pe.wait_ge(s_w1, 16 * 7)
                pe.wait_ge(s_acc, NHP * NT * 2)
                for dc in range(DC):
                    for oc in range(DC):
                        mm = nc.tensor.matmul(R[:, dc * 2:dc * 2 + 2], wsaT[:, oc, dc * P:(dc + 1) * P], asa[:, oc, :],
                                              start=oc == 0, stop=oc == DC - 1)
                mm.then_inc(s_coef, 1)
                pe.wait_ge(s_v, NORM0)
                for t in range(NT):
                    if t:
                        pe.wait_ge(s_xTc, t)
                    for dc in range(DC):
                        mm = nc.tensor.transpose(S[0][:, dc * P:(dc + 1) * P], xs[:, t, dc * P:(dc + 1) * P], ident[:])
                    mm.then_inc(s_xT, 1)
                pe.wait_ge(s_xTc, NT)
                pe.wait_ge(s_coef, 3)
                for c in range(NCH):
                    if c:
                        pe.wait_ge(s_xTc, NT + c)
                    for dc in range(DC):
                        mm = nc.tensor.matmul(S[1][:, 0:CW], wr_b[:, dc, :], xTs[:, dc, c * CW:(c + 1) * CW],
                                              start=dc == 0, stop=dc == DC - 1)
                    mm.then_inc(s_sr, 1)
                for t in range(NT):
                    for dc in range(DC):
                        mm = nc.tensor.matmul(S[2][:, t * 4:t * 4 + 4], xTs[:, dc, t * P:(t + 1) * P], coef[:, dc, :],
                                              start=dc == 0, stop=dc == DC - 1)
                mm.then_inc(s_node, 1)
                pe.wait_ge(s_node, 2)
                with pe.Fori(0, NT // 2) as t2:
                    for u in range(2):
                        i = t2 * 2 + u
                        it = NHP * NT + t2 * 2 + u
                        for h in range(2):
                            if h == 0:
                                pe.wait_ge(s_adj1[u], t2 * 16 + 16)
                                src = bias[u]
                            else:
                                pe.wait_ge(s_ee, i * 2 + 2)
                                src = prob[0]

                            def agg(g):
                                pe.wait_ge(s_cp[g % 2], it * 8 + h * 4 + g // 2 + 1)
                                for b in range(GROUPS[g]):
                                    k = START[g] + b
                                    mm = nc.tensor.matmul(S[h][:, 0:D], PT[h][:, k * P:(k + 1) * P], xs[:, k, :],
                                                          start=k == 0, stop=k == NT - 1)
                                return mm

                            for g in range(8):
                                pe.wait_ge(s_cp[g % 2], it * 8 + h * 4 + g // 2)
                                for b in range(GROUPS[g]):
                                    k = START[g] + b
                                    mm = nc.tensor.transpose(T[g % 2][:, b * P:(b + 1) * P], src[:, k * P:(k + 1) * P], ident[:])
                                mm.then_inc(s_tr[g % 2], 1)
                                if g:
                                    agg(g - 1)
                            agg(7).then_inc(s_z, 1)
                        pe.wait_ge(s_zs, i + 1)
                        for q in range(4):
                            mm = nc.tensor.transpose(S[2][:, q * P:(q + 1) * P], zs[:, q // 2, (q % 2) * P:(q % 2 + 1) * P], ident[:])
                        mm.then_inc(s_zT, 1)
                        pe.wait_ge(s_zTc, i + 1)
                        pe.wait_ge(s_y, i)
                        for dc in range(DC):
                            nc.tensor.matmul(R[:, 0:D], zT[:, 2 + dc, :], wsa[:, dc, :], start=dc == 0, stop=dc == DC - 1)
                        for dc in range(DC):
                            nc.tensor.matmul(R[:, D:2 * D], zT[:, dc, :], wgcn[:, dc, :], start=dc == 0, stop=dc == DC - 1)
                        for dc in range(DC):
                            mm = nc.tensor.matmul(O[:, 0:2], zT[:, dc, :], wab[:, dc, :], start=dc == 0, stop=dc == DC - 1)
                        mm.then_inc(s_f, 1)

            @block.scalar
            def _(act):
                with act.Fori(0, NHP) as hp:
                    act.wait_ge(s_taken, hp * PER_HP + PROJ + 4)
                    with act.Fori(0, NT) as i:
                        it = hp * NT + i
                        act.wait_ge(s_chunk, hp * PER_HP + i * (2 * NCH) + PROJ)
                        nc.scalar.activation(qtile[:], QT[:, bass.ds(i * P, P)], ACT.Copy, scale=KD ** -0.5).then_inc(s_q, 1)
                        for h in range(2):
                            act.wait_ge(s_max, it * 2 + h + 1)
                            nc.scalar.activation(prob[h][:], prob[h][:], ACT.Exp, bias=negmax[:, h:h + 1],
                                                 accum_out=rowsum[:, h:h + 1]).then_inc(s_exp, 1)
                        for h in range(2):
                            for g in range(0, 8, 2):
                                act.wait_ge(s_tr[0], it * 8 + h * 4 + g // 2 + 1)
                                w = GROUPS[g] * P
                                nc.scalar.activation(PT[h][:, START[g] * P:START[g] * P + w], T[0][:, 0:w], ACT.Copy).then_inc(s_cp[0], 1)
                            act.wait_ge(s_pv, it * 2 + h + 1)
                            nc.scalar.activation(oT[h * KD:(h + 1) * KD, :], O[h * KD:(h + 1) * KD, 0:P], ACT.Copy).then_inc(s_oT, 1)

                act.wait_ge(s_var, 1)
                nc.scalar.activation(std[:], std[:], ACT.Sqrt).then_inc(s_std, 1)
                with act.Fori(0, NT // 2) as t2:
                    for u in range(2):
                        i = t2 * 2 + u
                        it = NHP * NT + t2 * 2 + u
                        for h in range(2):
                            if h == 1:
                                act.wait_ge(s_leak, i + 1)
                                nc.scalar.activation(prob[1][:], prob[1][:], ACT.Exp, scale=-1.0).then_inc(s_ee, 1)
                            for g in range(0, 8, 2):
                                act.wait_ge(s_tr[0], it * 8 + h * 4 + g // 2 + 1)
                                w = GROUPS[g] * P
                                nc.scalar.activation(PT[h][:, START[g] * P:START[g] * P + w], T[0][:, 0:w], ACT.Copy).then_inc(s_cp[0], 1)
                        act.wait_ge(s_zT, i + 1)
                        nc.scalar.activation(zT[:].rearrange("p a b -> p (a b)"), S[2][:], ACT.Copy).then_inc(s_zTc, 1)
                        act.wait_ge(s_gz, i + 1)
                        nc.scalar.activation(gate[:], gate[:], ACT.Exp, scale=-1.0).then_inc(s_ge, 1)
                        act.wait_ge(s_y, i + 1)
                        nc.scalar.activation(yt[:], yt[:], ACT.Exp, scale=-1.0).then_inc(s_ye, 1)
                act.wait_ge(s_var, 2)
                nc.scalar.activation(std[:], std[:], ACT.Sqrt).then_inc(s_std, 1)

            @block.vector
            def _(dve):
                for b in range(4):
                    nc.vector.memset(S[b][:], 0.0).then_inc(s_taken, 1)
                dve.wait_ge(s_x, 32)
                dve.wait_ge(s_id, 4)
                with dve.Fori(0, NHP) as hp:
                    n = 0
                    for buf in (QT, KT):
                        for c in range(NCH):
                            dve.wait_ge(s_chunk, hp * PER_HP + n + 1)
                            nc.vector.tensor_copy(buf[:, c * CW:(c + 1) * CW], S[n % 4][:, 0:CW]).then_inc(s_taken, 1)
                            n += 1
                    for g in range(8):
                        dve.wait_ge(s_chunk, hp * PER_HP + n + 1)
                        w = GROUPS[g] * P
                        nc.vector.tensor_copy(V[:, START[g]:START[g] + GROUPS[g], :].rearrange("p a b -> p (a b)"),
                                              S[n % 4][:, 0:w]).then_inc(s_taken, 1)
                        n += 1
                    with dve.Fori(0, NT // 2) as t2:
                        for u in range(2):
                            it = hp * NT + t2 * 2 + u
                            base = hp * PER_HP + t2 * (4 * NCH) + u * 2 * NCH + PROJ
                            it2 = hp * (NT // 2) + t2
                            dve.wait_ge(s_adj[u], it2 * 16 + 16)
                            nc.vector.tensor_scalar(bias[u][:], bias[u][:], BIG, -BIG, ALU.mult, ALU.add).then_inc(s_bias[u], 1)
                            dve.wait_ge(s_bias[u], it2 * 2 + 1)
                            diag = bias[u][:, bass.ds((t2 * 2 + u) * P, P)]
                            nc.vector.tensor_tensor(diag, diag, eye_bias[:], ALU.max).then_inc(s_bias[u], 1)
                            dve.wait_ge(s_bias[u], it2 * 2 + 2)
                            for h in range(2):
                                for c in range(NCH):
                                    m = h * NCH + c
                                    dve.wait_ge(s_chunk, base + m + 1)
                                    nc.vector.tensor_tensor(prob[h][:, c * CW:(c + 1) * CW], S[m % 4][:, 0:CW],
                                                            bias[u][:, c * CW:(c + 1) * CW], ALU.add).then_inc(s_taken, 1)
                                dve.wait_ge(s_taken, base + h * NCH + NCH + 4)
                                top = nc.vector.reduce_max(rowmax[:, h:h + 1], prob[h][:], AX_X)
                                if h == 0:
                                    top.then_inc(s_dve, 1)
                                    dve.wait_ge(s_dve, it + 1)
                                else:
                                    top.then_inc(s_bias_used[u], 1)
                                    dve.wait_ge(s_bias_used[u], hp * (NT // 2) + t2 + 1)
                                nc.vector.tensor_scalar(negmax[:, h:h + 1], rowmax[:, h:h + 1], -1.0, None,
                                                        ALU.mult).then_inc(s_max, 1)
                            for h in range(2):
                                for g in range(1, 8, 2):
                                    dve.wait_ge(s_tr[1], it * 8 + h * 4 + g // 2 + 1)
                                    w = GROUPS[g] * P
                                    nc.vector.tensor_copy(PT[h][:, START[g] * P:START[g] * P + w], T[1][:, 0:w]).then_inc(s_cp[1], 1)
                                dve.wait_ge(s_exp, it * 2 + h + 1)
                                nc.vector.reciprocal(rinv[:, h:h + 1], rowsum[:, h:h + 1]).then_inc(s_att, 1)
                                dve.wait_ge(s_att, it * 2 + h + 1)
                                dve.wait_ge(s_res, it * 2 + h + 1)
                                row = xs[:, bass.ds(t2 * 2 + u, 1), :].rearrange("p a d -> p (a d)")
                                nc.vector.scalar_tensor_tensor(out=row, in0=R[:, 0:D], scalar=rinv[:, h:h + 1], in1=row,
                                                               op0=ALU.mult, op1=ALU.add).then_inc(s_acc, 1)
                                dve.wait_ge(s_acc, it * 2 + h + 1)

                def layernorm(buf, n0, k):
                    with dve.Fori(0, NT) as t:
                        nc.vector.bn_stats(stats[:, bass.ds(t, 1), :].rearrange("p a d -> p (a d)"),
                                           buf[:, bass.ds(t, 1), :].rearrange("p a d -> p (a d)")).then_inc(s_v, 1)
                    dve.wait_ge(s_v, n0 + NT)
                    for t in range(NT):
                        nc.vector.bn_aggr(mv[:, t, :], stats[:, t, :]).then_inc(s_v, 1)
                    dve.wait_ge(s_v, n0 + 2 * NT)
                    nc.vector.tensor_scalar(std[:], mv[:, :, 1], EPS, None, ALU.add).then_inc(s_var, 1)
                    dve.wait_ge(s_std, k + 1)
                    nc.vector.reciprocal(rstd[:], std[:]).then_inc(s_v, 1)
                    dve.wait_ge(s_v, n0 + 2 * NT + 1)
                    with dve.Fori(0, NT) as t:
                        row = buf[:, bass.ds(t, 1), :].rearrange("p a d -> p (a d)")
                        nc.vector.tensor_scalar(row, row, mv[:, bass.ds(t, 1), 0], rstd[:, bass.ds(t, 1)], ALU.subtract,
                                                ALU.mult).then_inc(s_v, 1)

                layernorm(xs, 0, 0)
                dve.wait_ge(s_coef, 1)
                nc.vector.tensor_copy(coef[:, :, 0:2], R[:, 0:2 * DC].rearrange("p (c k) -> p c k", k=2)).then_inc(s_v, 1)
                nc.vector.tensor_copy(coef[:, :, 2:4], wab[:, DC:2 * DC, :]).then_inc(s_v, 1)
                nc.vector.memset(ones[:], 1.0).then_inc(s_v, 1)
                dve.wait_ge(s_v, NORM0 + 3)
                for dc in range(DC):
                    nc.vector.tensor_scalar(wr_b[:, dc, :], ones[:], coef[:, dc, 1:2], None, ALU.mult).then_inc(s_coef, 1)
                for t in range(NT):
                    dve.wait_ge(s_xT, t + 1)
                    nc.vector.tensor_copy(xTs[:, :, t * P:(t + 1) * P],
                                          S[0][:, 0:D].rearrange("p (c n) -> p c n", c=DC)).then_inc(s_xTc, 1)
                for c in range(NCH):
                    dve.wait_ge(s_sr, c + 1)
                    nc.vector.tensor_copy(SR[:, c * CW:(c + 1) * CW], S[1][:, 0:CW]).then_inc(s_xTc, 1)
                dve.wait_ge(s_node, 1)
                nc.vector.tensor_copy(node[:].rearrange("p t k -> p (t k)"), S[2][:, 0:NT * 4]).then_inc(s_node, 1)
                dve.wait_ge(s_node, 2)
                for k in range(2):
                    nc.vector.tensor_scalar(node[:, :, 2 + k], node[:, :, 2 + k], bab_b[:, k:k + 1], None, ALU.add).then_inc(s_v, 1)
                dve.wait_ge(s_v, HEAD1)
                dve.wait_ge(s_xTc, NT + NCH)
                with dve.Fori(0, NT // 2) as t2:
                    for u in range(2):
                        i = t2 * 2 + u
                        it = NHP * NT + t2 * 2 + u
                        n = 0

                        def step(ins):
                            nonlocal n
                            n += 1
                            ins.then_inc(s_v, 1)
                            dve.wait_ge(s_v, i * STEPS + (HEAD1 + n))

                        def copies(h):
                            for g in range(1, 8, 2):
                                dve.wait_ge(s_tr[1], it * 8 + h * 4 + g // 2 + 1)
                                w = GROUPS[g] * P
                                nc.vector.tensor_copy(PT[h][:, START[g] * P:START[g] * P + w], T[1][:, 0:w]).then_inc(s_cp[1], 1)

                        step(nc.vector.tensor_scalar(prob[1][:], SR[:], node[:, bass.ds(i, 1), 0], None, ALU.add))
                        step(nc.vector.scalar_tensor_tensor(out=prob[1][:], in0=prob[1][:], scalar=0.01, in1=prob[1][:],
                                                            op0=ALU.mult, op1=ALU.max))
                        dve.wait_ge(s_adj1[u], t2 * 16 + 16)
                        nc.vector.tensor_tensor(prob[1][:], prob[1][:], bias[u][:], ALU.mult).then_inc(s_leak, 1)
                        copies(0)
                        dve.wait_ge(s_ee, i * 2 + 1)
                        nc.vector.tensor_tensor_reduce(out=prob[0][:], in0=prob[1][:], in1=bias[u][:], scale=1.0, scalar=0.0,
                                                       op0=ALU.mult, op1=ALU.add, accum_out=esum[:]).then_inc(s_ee, 1)
                        copies(1)
                        dve.wait_ge(s_ee, i * 2 + 2)
                        step(nc.vector.tensor_scalar(esum[:], esum[:], 1e-5, None, ALU.add))
                        step(nc.vector.reciprocal(esum[:], esum[:]))
                        dve.wait_ge(s_z, i * 2 + 2)
                        step(nc.vector.tensor_copy(zs[:, 0, :], S[0][:, 0:D]))
                        nc.vector.tensor_scalar(zs[:, 1, :], S[1][:, 0:D], esum[:, 0:1], None, ALU.mult).then_inc(s_zs, 1)
                        dve.wait_ge(s_f, i + 1)
                        nc.vector.tensor_tensor(gate[:], O[:, 0:2], node[:, bass.ds(i, 1), 2:4].rearrange("p a k -> p (a k)"),
                                                ALU.add).then_inc(s_gz, 1)
                        step(nc.vector.tensor_tensor(yt[:], R[:, D:2 * D], bg_b[:], ALU.add))
                        dve.wait_ge(s_ge, i + 1)
                        step(nc.vector.tensor_scalar(gate[:], gate[:], 1.0, None, ALU.add))
                        step(nc.vector.reciprocal(gate[:], gate[:]))
                        step(nc.vector.tensor_scalar(yt[:], yt[:], gate[:, 1:2], None, ALU.mult))
                        nc.vector.scalar_tensor_tensor(out=yt[:], in0=R[:, 0:D], scalar=gate[:, 0:1], in1=yt[:],
                                                       op0=ALU.mult, op1=ALU.add).then_inc(s_y, 1)
                        dve.wait_ge(s_ye, i + 1)
                        step(nc.vector.tensor_scalar(yt[:], yt[:], 1.0, None, ALU.add))
                        step(nc.vector.reciprocal(yt[:], yt[:]))
                        step(nc.vector.tensor_tensor(ys[:, bass.ds(i, 1), :].rearrange("p a d -> p (a d)"), yt[:],
                                                     xs[:, bass.ds(i, 1), :].rearrange("p a d -> p (a d)"), ALU.add))
                        assert n == STEPS
                layernorm(ys, HEAD1 + NT * STEPS, 1)




def kernel(**inputs):
    import numpy as _np
    import concourse.bacc as _bacc
    from concourse import mybir as _mybir
    from concourse.bass_utils import run_bass_kernel_spmd as _run

    a = {k: _np.asarray(v) for k, v in inputs.items()}
    N, D = a["x"].shape
    NP = -(-N // 128) * 128
    x = _np.zeros((NP, D), a["x"].dtype)
    x[:N] = a["x"]
    adj = _np.zeros((NP, NP), a["adj"].dtype)
    adj[:N, :N] = a["adj"]

    def heads_last(w):
        return w.transpose(1, 0, 2).reshape(D, -1)

    laid = {
        "x": x, "xT": x.T, "adj": adj,
        "Wq": heads_last(a["L0_gnn_Wqs"]), "Wk": heads_last(a["L0_gnn_Wks"]), "Wv": heads_last(a["L0_gnn_Wvs"]),
        "Wo": a["L0_gnn_Wo"].reshape(-1, D),
        "W_sa": a["L1_gnn_W_sa"], "W_saT": a["L1_gnn_W_sa"].T, "a_sa": a["L1_gnn_a_sa"].reshape(2, D).T,
        "W_gcn": a["L1_gnn_W_gcnb"], "b_gcn": a["L1_gnn_b_gcnb"],
        "Wab": _np.concatenate([a["L1_gnn_Wa"], a["L1_gnn_Wb"]], 0).T,
        "bab": _np.concatenate([a["L1_gnn_ba"], a["L1_gnn_bb"]]),
    }
    nc = _bacc.Bacc("TRN2", target_bir_lowering=False, num_devices=1)
    arrays, args = {}, []
    for name, v in laid.items():
        v = _np.ascontiguousarray(v)
        arrays[f"in_{name}"] = v
        args.append(nc.dram_tensor(f"in_{name}", v.shape, _mybir.dt.from_np(v.dtype), kind="ExternalInput").ap())
    args.append(nc.dram_tensor("out_0", (NP, D), _mybir.dt.float32, kind="ExternalOutput").ap())
    adj_resnorm(nc, *args)
    r = _run(nc, [arrays], core_ids=[0])
    return r.results[0]["out_0"][:N]
```

```python
from contextlib import ExitStack

import concourse.bass as bass
from concourse import mybir

F32 = mybir.dt.float32
BF16 = mybir.dt.bfloat16
U32 = mybir.dt.uint32
I32 = mybir.dt.int32
ALU = mybir.AluOpType
ACT = mybir.ActivationFunctionType
AX_X = mybir.AxisListType.X
P = 128
KD = 64
BIG = 1e16
EPS = 1e-5
SEGS = 4
RANKS = 16
ET = 5
OFF = 8192.0
NONE = -3e4


class Tile:

    def __init__(self, u, b, count):
        self.u, self.b, self.count = u, b, count
        self.t = u * 2 + b

    def at(self, k):
        s = self.b + k
        return Tile(self.u + s // 2, s % 2, self.count)

    def has(self, k):
        return not isinstance(self.u, int) or 0 <= self.t + k < self.count


def sweep(eng, count, lag, body):
    first = max(1, (lag + 1) // 2)
    for t in range(2 * first):
        body(Tile(t // 2, t % 2, count))
    with eng.Fori(first, count // 2 - 1) as u:
        for b in range(2):
            body(Tile(u, b, count))
    for t in range(count - 2, count + lag):
        body(Tile(t // 2, t % 2, count))


def wait(eng, sem, value):
    if not isinstance(value, int) or value > 0:
        eng.wait_ge(sem, value)


class Chain:

    def __init__(self, eng, sem, tile, per):
        self.eng, self.sem, self.per, self.base, self.n = eng, sem, per, tile.t * per, 0

    def __call__(self, ins, then=True):
        self.n += 1
        assert self.n <= self.per
        ins.then_inc(self.sem, 1)
        if then:
            self.eng.wait_ge(self.sem, self.base + self.n)

    def join(self):
        self.eng.wait_ge(self.sem, self.base + self.n)


def flat(ap):
    return ap.rearrange("p a b -> p (a b)")


def row(buf, t, n=1):
    return buf[:, bass.ds(t * n, n)]


def sparse_path(nc, dram, scratch, flag, out):
    x, xT, adj = dram["x"], dram["xT"], dram["adj"]
    NP, D = x.shape
    NT = NP // P
    HK = dram["Wq"].shape[1]
    H = HK // KD
    DC = D // P
    HC = HK // P
    SW = NP // SEGS
    SB = SW + 8
    NS = SEGS * 8
    EW = ET * P
    GC = 2 * NS + 2
    XW = D + 4
    kv_table, x_table = scratch
    assert SW * SEGS == NP and NT % 2 == 0 and NT >= 6

    with ExitStack() as ctx:
        def sb(name, shape, dt=F32):
            return ctx.enter_context(nc.sbuf_tensor(name, shape, dt))

        def sem(name):
            return ctx.enter_context(nc.semaphore(name))

        s_passed = sem("f_passed")

        def passed(eng):
            eng.sem_inc(s_passed, 1)

        ident = sb("f_ident", [P, P])
        ones = sb("f_ones", [P, P])
        tri = sb("f_tri", [P, P])
        iota_e = sb("f_iota_e", [P, EW])
        iota_i = sb("f_iota_i", [P, P])
        iota_r = sb("f_iota_r", [P, RANKS])
        edge1 = sb("f_edge1", [P, ET])
        tile0 = sb("f_tile0", [P, NT])
        seg0 = sb("f_seg0", [P, NS])
        xs = sb("f_xs", [P, NT, D])
        Q = sb("f_Q", [P, NT, HK])
        deg_all = sb("f_deg", [P, NT])
        end_all = sb("f_end", [P, NT])
        full_all = sb("f_full", [P, NT * SEGS])
        idx_all = sb("f_idx", [P, NT * ET], U32)
        row1_all = sb("f_row1", [P, NT * ET])
        rank1_all = sb("f_rank1", [P, NT * ET])
        skip_all = sb("f_skip", [P, NT * ET])
        sel_all = sb("f_sel", [P, NT * EW], BF16)
        sel = [sb(f"f_sel{b}", [P, EW]) for b in range(2)]
        selT = [sb(f"f_selT{b}", [P, ET, P]) for b in range(2)]
        idx = [sb(f"f_idx{b}", [P, ET], U32) for b in range(2)]
        ring = sb("f_ring", [P, 2 * ET * 2 * HK])
        stats = sb("f_stats", [P, NT, 6])
        mv = sb("f_mv", [P, NT, 2])
        std = sb("f_std", [P, NT])
        rstd = sb("f_rstd", [P, NT])
        s_const = sem("f_const")
        s_load = sem("f_load")

        with ExitStack() as ph:
            def pb(name, shape):
                return ph.enter_context(nc.psum_tensor(name, shape, F32))

            def sb1(name, shape, dt=F32):
                return ph.enter_context(nc.sbuf_tensor(name, shape, dt))

            adjb = [ring[:, b * SEGS * SB:(b + 1) * SEGS * SB].rearrange("p (s w) -> p s w", s=SEGS) for b in range(2)]
            w0 = 2 * SEGS * SB
            wqkv = ring[:, w0:w0 + 3 * DC * HK].rearrange("p (w c m) -> p w c m", w=3, c=DC)
            ones8 = sb1("f_ones8", [P, 8])
            xt = [sb1(f"f_xt{b}", [P, DC, P]) for b in range(2)]
            kvrow = [sb1(f"f_kvrow{b}", [P, 2 * HK]) for b in range(2)]
            found = sb1("f_found", [P, NS], U32)
            valid = sb1("f_valid", [P, NS])
            count = sb1("f_count", [P, NS])
            end2 = [sb1(f"f_end2{b}", [P, 1]) for b in range(2)]
            G_in = [sb1(f"f_Gin{b}", [P, GC]) for b in range(2)]
            G = sb1("f_G", [P, ET, GC])
            after = sb1("f_after", [P, EW])
            before = sb1("f_before", [P, EW])
            pick = sb1("f_pick", [P, ET, NS])
            node = sb1("f_node", [P, ET])
            same = sb1("f_same", [P, ET])
            beat = sb1("f_beat", [P, 1])
            Bqkv = [pb(f"f_B{w}", [P, 512]) for w in range(3)]
            BG = pb("f_BG", [P, 512])
            BO = pb("f_BO", [P, 512])

            s_ones = sem("f_ones")
            s_adj = [sem(f"f_adj{b}") for b in range(2)]
            s_xt = [sem(f"f_xt{b}") for b in range(2)]
            s_beat = sem("f_beat")
            s_find = sem("f_find")
            s_proj = sem("f_proj")
            s_pcopy = sem("f_pcopy")
            s_kvout = [sem(f"f_kvout{b}") for b in range(2)]
            s_row = sem("f_row")
            s_off = sem("f_off")
            s_end = sem("f_end")
            s_sel = sem("f_sel")
            s_selp = sem("f_selp")
            s_keep = sem("f_keep")
            s_g = sem("f_g")
            s_gcopy = sem("f_gcopy")
            s_edge = sem("f_edge")
            ROWSTEPS, EDGESTEPS = 6, 8
            s_xs = sem("f_xs")

            with nc.Block() as block:
                @block.sync
                def _(sp):
                    for w, W in enumerate(("Wq", "Wk", "Wv")):
                        sp.dma_start(wqkv[:, w], dram[W].rearrange("(c p) m -> p c m", p=P)).then_inc(s_load, 16)

                    def body(tl):
                        u, b, t = tl.u, tl.b, tl.t
                        if tl.has(0):
                            wait(sp, s_find, t - 1)
                            sp.dma_start(adjb[b][:, :, 0:SW], adj[bass.ds(t * P, P), :].rearrange("p (s w) -> p s w", s=SEGS)).then_inc(s_adj[b], 16)
                            wait(sp, s_proj, (t - 1) * 3)
                            passed(sp)
                            sp.dma_start(xt[b][:], xT[:, bass.ds(t * P, P)].rearrange("(c p) n -> p c n", p=P)).then_inc(s_xt[b], 16)
                        if tl.has(-1):
                            q = tl.at(-1)
                            sp.wait_ge(s_pcopy, q.t * 3 + 3)
                            sp.dma_start(kv_table[bass.ds(q.t * P, P), :], kvrow[q.b][:]).then_inc(s_kvout[q.b], 16)

                    sweep(sp, NT, 1, body)
                    sp.dma_start(xs[:], x.rearrange("(t p) d -> p t d", p=P)).then_inc(s_xs, 16)
                    sp.wait_ge(s_xs, 16)
                    for b in range(2):
                        sp.wait_ge(s_kvout[b], 16 * (NT // 2))

                @block.gpsimd
                def _(pool):
                    for m, v in ((ident, 0.0), (ones, 1.0), (tri, 1.0)):
                        pool.memset(m[:], v).then_inc(s_const, 1)
                    pool.wait_ge(s_const, 3)
                    pool.affine_select(out=ident[:], in_=ident[:], compare_op=ALU.not_equal, fill=1.0, base=0,
                                       pattern=[[-1, P]], channel_multiplier=1).then_inc(s_const, 1)
                    pool.affine_select(out=tri[:], in_=tri[:], compare_op=ALU.is_gt, fill=0.0, base=0,
                                       pattern=[[1, P]], channel_multiplier=-1).then_inc(s_const, 1)
                    for out_, pattern, base, cm in (
                            (iota_e[:], [[1, EW]], 0, 0), (iota_i[:], [[1, P]], 1, 0), (iota_r[:], [[1, RANKS]], 1, 0),
                            (edge1[:], [[P, ET]], 1, 1), (tile0[:], [[P, NT]], -int(OFF) - 1, 0),
                            (seg0[:].rearrange("p (s k) -> p s k", k=8), [[SW, SEGS], [0, 8]], -int(OFF), 0),
                            (G_in[0][:, GC - 1:GC], [[1, 1]], 1, 1), (G_in[1][:, GC - 1:GC], [[1, 1]], 1, 1)):
                        pool.iota(out_, pattern, base=base, channel_multiplier=cm,
                                  allow_small_or_imprecise_dtypes=True).then_inc(s_const, 1)

                    def body(tl):
                        t, b = tl.t, tl.b
                        wait(pool, s_keep, t - 1)
                        pool.wait_ge(s_end, t * 3 + 3)
                        passed(pool)
                        off = G_in[b][:, GC - 2:GC - 1]
                        pool.tensor_scalar(after[:], iota_e[:], off, None, ALU.is_ge).then_inc(s_selp, 1)
                        pool.tensor_scalar(before[:], iota_e[:], end2[b][:], None, ALU.is_lt).then_inc(s_selp, 1)
                        pool.wait_ge(s_selp, t * 2 + 2)
                        pool.tensor_tensor(sel[b][:], after[:], before[:], ALU.mult).then_inc(s_sel, 1)
                        pool.wait_ge(s_sel, t + 1)
                        passed(pool)

                    sweep(pool, NT, 0, body)

                @block.tensor
                def _(pe):
                    pe.wait_ge(s_load, 48)
                    pe.wait_ge(s_const, 13)

                    def proj(tl, w):
                        for dc in range(DC):
                            mm = nc.tensor.matmul(Bqkv[w][:, 0:HK], xt[tl.b][:, dc, :], wqkv[:, w, dc, :],
                                                  start=dc == 0, stop=dc == DC - 1)
                        mm.then_inc(s_proj, 1)

                    def body(tl):
                        u, b, t = tl.u, tl.b, tl.t
                        if tl.has(0):
                            pe.wait_ge(s_xt[b], u * 16 + 16)
                            wait(pe, s_pcopy, t * 3 - 1)
                            proj(tl, 0)
                            proj(tl, 1)
                            wait(pe, s_pcopy, t * 3)
                            proj(tl, 2)
                            pe.wait_ge(s_row, t * ROWSTEPS + ROWSTEPS)
                            wait(pe, s_end, t * 3)
                            nc.tensor.matmul(BO[:, 0:1], tri[:], row(deg_all, t), start=True, stop=True).then_inc(s_off, 1)
                        if tl.has(-1):
                            q = tl.at(-1)
                            pe.wait_ge(s_sel, q.t + 1)
                            wait(pe, s_gcopy, q.t)
                            for c in range(ET):
                                mm = nc.tensor.matmul(BG[:, c * GC:(c + 1) * GC], sel[q.b][:, c * P:(c + 1) * P], G_in[q.b][:],
                                                      start=True, stop=True)
                            mm.then_inc(s_g, 1)

                    sweep(pe, NT, 1, body)

                @block.scalar
                def _(act):
                    def body(tl):
                        u, b, t = tl.u, tl.b, tl.t
                        if tl.has(0):
                            wait(act, s_kvout[b], u * 16)
                            act.wait_ge(s_proj, t * 3 + 2)
                            nc.scalar.activation(kvrow[b][:, 0:HK], Bqkv[1][:, 0:HK], ACT.Copy).then_inc(s_pcopy, 1)
                            nc.scalar.activation(flat(Q[:, bass.ds(t, 1), :]), Bqkv[0][:, 0:HK], ACT.Copy,
                                                 scale=KD ** -0.5).then_inc(s_pcopy, 1)
                        if tl.has(-1):
                            q = tl.at(-1)
                            wait(act, s_edge, q.t * EDGESTEPS)
                            act.wait_ge(s_g, q.t + 1)
                            nc.scalar.activation(flat(G[:]), BG[:, 0:ET * GC], ACT.Copy).then_inc(s_gcopy, 1)
                            nc.scalar.activation(row(sel_all, q.t, EW), sel[q.b][:], ACT.Copy).then_inc(s_keep, 1)
                        if tl.has(0):
                            act.wait_ge(s_proj, t * 3 + 3)
                            nc.scalar.activation(kvrow[b][:, HK:2 * HK], Bqkv[2][:, 0:HK], ACT.Copy).then_inc(s_pcopy, 1)

                    sweep(act, NT, 1, body)

                @block.vector
                def _(dve):
                    nc.vector.memset(ones8[:], 1.0).then_inc(s_ones, 1)
                    for b in range(2):
                        nc.vector.memset(adjb[b][:, :, SW:SB], 1.0).then_inc(s_ones, 1)
                    dve.wait_ge(s_ones, 3)
                    dve.wait_ge(s_const, 13)

                    def rows(tl):
                        u, b, t = tl.u, tl.b, tl.t
                        wait(dve, s_g, t - 1)
                        wait(dve, s_end, t * 3)
                        dve.wait_ge(s_adj[b], u * 16 + 16)
                        nc.vector.memset(beat[:], 0.0).then_inc(s_beat, 1)
                        for s in range(SEGS):
                            f = nc.vector.max_index(found[:, s * 8:(s + 1) * 8], ones8[:], adjb[b][:, s, :])
                        f.then_inc(s_find, 1)

                    def ranks(tl):
                        b, t = tl.b, tl.t
                        step = Chain(dve, s_row, tl, ROWSTEPS)
                        dve.wait_ge(s_find, t + 1)
                        dve.wait_ge(s_beat, t + 1)
                        step(nc.vector.tensor_scalar(valid[:], found[:], float(SW), None, ALU.is_lt), then=False)
                        step(nc.vector.tensor_tensor(G_in[b][:, 0:NS], found[:], seg0[:], ALU.add), then=False)
                        dve.wait_ge(s_row, t * ROWSTEPS + 1)
                        step(nc.vector.tensor_tensor_scan(count[:], ones[:, 0:NS], valid[:], 0.0, ALU.mult, ALU.add), then=False)
                        step(nc.vector.tensor_scalar(row(full_all, t, SEGS), valid[:, 7:NS:8], 1.0, None, ALU.mult), then=False)
                        dve.wait_ge(s_row, t * ROWSTEPS + 3)
                        step(nc.vector.tensor_scalar(row(deg_all, t), count[:, NS - 1:NS], 1.0, None, ALU.mult), then=False)
                        step(nc.vector.tensor_tensor(G_in[b][:, NS:2 * NS], count[:], valid[:], ALU.mult))

                    def offsets(tl):
                        b, t = tl.b, tl.t
                        dve.wait_ge(s_off, t + 1)
                        wait(dve, s_sel, t - 1)
                        nc.vector.tensor_tensor(end2[b][:], BO[:, 0:1], count[:, NS - 1:NS], ALU.add).then_inc(s_end, 1)
                        nc.vector.tensor_copy(G_in[b][:, GC - 2:GC - 1], BO[:, 0:1]).then_inc(s_end, 1)
                        nc.vector.tensor_tensor(row(end_all, t), BO[:, 0:1], count[:, NS - 1:NS], ALU.add).then_inc(s_end, 1)

                    def edges(tl):
                        b, t = tl.b, tl.t
                        step = Chain(dve, s_edge, tl, EDGESTEPS)
                        dve.wait_ge(s_gcopy, t + 1)
                        r1 = row(rank1_all, t, ET)
                        step(nc.vector.tensor_tensor(r1, edge1[:], G[:, :, GC - 2], ALU.subtract), then=False)
                        step(nc.vector.tensor_scalar(row(row1_all, t, ET), G[:, :, GC - 1], 1.0, None, ALU.mult), then=False)
                        dve.wait_ge(s_edge, t * EDGESTEPS + 1)
                        step(nc.vector.tensor_tensor(pick[:], G[:, :, NS:2 * NS], r1.unsqueeze(2).to_broadcast([P, ET, NS]),
                                                     ALU.is_equal))
                        step(nc.vector.tensor_tensor(pick[:], pick[:], G[:, :, 0:NS], ALU.mult))
                        step(nc.vector.tensor_reduce(node[:], pick[:], AX_X, ALU.add))
                        step(nc.vector.tensor_scalar(row(idx_all, t, ET), node[:], OFF, None, ALU.add), then=False)
                        step(nc.vector.scalar_tensor_tensor(out=same[:], in0=row(row1_all, t, ET), scalar=row(tile0, t), in1=node[:],
                                                            op0=ALU.add, op1=ALU.is_equal))
                        step(nc.vector.tensor_scalar(row(skip_all, t, ET), same[:], NONE, None, ALU.mult), then=False)

                    def body(tl):
                        if tl.has(0):
                            rows(tl)
                            ranks(tl)
                            offsets(tl)
                        if tl.has(-1):
                            edges(tl.at(-1))

                    sweep(dve, NT, 1, body)
                    dve.wait_ge(s_edge, NT * EDGESTEPS)
                    dve.wait_ge(s_end, NT * 3)

        with ExitStack() as ph:
            def pb(name, shape):
                return ph.enter_context(nc.psum_tensor(name, shape, F32))

            def sb2(name, shape, dt=F32):
                return ph.enter_context(nc.sbuf_tensor(name, shape, dt))

            kv = [[ring[:, (b * ET + c) * 2 * HK:(b * ET + c + 1) * 2 * HK] for c in range(ET)] for b in range(2)]
            wo = sb2("f_wo", [P, HC, D])
            own = [sb2(f"f_own{b}", [P, 2 * HK]) for b in range(2)]
            prod = [sb2(f"f_prod{b}", [P, HK]) for b in range(2)]
            oprod = sb2("f_oprod", [P, HK])
            score = [sb2(f"f_score{b}", [P, ET, H]) for b in range(2)]
            oscore = [sb2(f"f_oscore{b}", [P, H]) for b in range(2)]
            hot = sb2("f_hot", [P, ET, RANKS])
            spread = sb2("f_spread", [P, ET, H, RANKS])
            absent = sb2("f_absent", [P, RANKS])
            byrank = sb2("f_byrank", [P, H, RANKS])
            top = sb2("f_top", [P, H])
            top1 = sb2("f_top1", [P, H])
            top2 = sb2("f_top2", [P, H])
            expo = sb2("f_expo", [P, (ET + 1) * H])
            prob = [sb2(f"f_prob{b}", [P, (ET + 1) * H]) for b in range(2)]
            pv = [sb2(f"f_pv{c}", [P, HK]) for c in range(ET)]
            opv = sb2("f_opv", [P, HK])
            den = sb2("f_den", [P, H])
            att = sb2("f_att", [P, HK])
            attn = sb2("f_attn", [P, HK])
            attT = att
            Bq = [pb(f"f_Bq{b}", [P, 512]) for b in range(2)]
            BM, BE, BO, BD, BT, BR = (pb(n, [P, 512]) for n in ("f_BM", "f_BE", "f_BOut", "f_BD", "f_BT", "f_BR"))

            s_clear = sem("f_clear")
            s_wo = sem("f_wo")
            s_stage = sem("f_stage")
            s_kv = [[sem(f"f_kv{b}{c}") for c in range(ET)] for b in range(2)]
            s_own = [sem(f"f_own{b}") for b in range(2)]
            s_qe = sem("f_qe")
            s_mul = sem("f_mul")
            s_dot = sem("f_dot")
            s_selT = sem("f_selT")
            s_oprod = sem("f_oprod")
            s_oscore = sem("f_oscore")
            s_hot = sem("f_hot")
            s_byrank = sem("f_byrank")
            s_top = sem("f_top")
            s_tope = sem("f_tope")
            s_absent = sem("f_absent")
            s_expo = sem("f_expo")
            s_prob = sem("f_prob")
            s_pvp = sem("f_pvp")
            s_pva = sem("f_pva")
            s_opv = sem("f_opv")
            s_out = sem("f_outp")
            s_den = sem("f_den")
            s_att = sem("f_att")
            s_attn = sem("f_attn")
            s_stats = sem("f_stats")
            s_attT = sem("f_attT")
            s_attTc = sem("f_attTc")
            s_res = sem("f_res")
            s_sum = sem("f_sum")
            ON_POOL = 3
            ORDER = (0, 3, 1, 4, 2)

            with nc.Block() as block:
                @block.sync
                def _(sp):
                    sp.dma_start(wo[:], dram["Wo"].rearrange("(c p) d -> p c d", p=P)).then_inc(s_wo, 16)

                    def body(tl):
                        wait(sp, s_opv, tl.t - 1)
                        sp.dma_start(own[tl.b][:], kv_table[bass.ds(tl.t * P, P), :]).then_inc(s_own[tl.b], 16)

                    sweep(sp, NT, 0, body)

                @block.gpsimd
                def _(pool):
                    pool.memset(ring[:, ET * 2 * HK:], 0.0).then_inc(s_clear, 1)

                    def gathers(tl):
                        pool.wait_ge(s_stage, tl.t + 1)
                        for c in range(ET):
                            if c < ON_POOL:
                                wait(pool, s_pvp, (tl.t - 2) * ON_POOL + c + 1)
                            else:
                                wait(pool, s_pva, (tl.t - 2) * (ET - ON_POOL) + c - ON_POOL + 1)
                            passed(pool)
                            pool.indirect_dma_start(
                                out=kv[tl.b][c], out_offset=None, in_=kv_table,
                                in_offset=bass.IndirectOffsetOnAxis(ap=idx[tl.b][:, c:c + 1], axis=0),
                                bounds_check=NP - 1, oob_is_err=False).then_inc(s_kv[tl.b][c], 16)

                    def products(tl):
                        b, t = tl.b, tl.t
                        pool.wait_ge(s_prob, t + 1)
                        for c in range(ON_POOL):
                            wait(pool, s_out, (t - 1) * ET + ORDER.index(c) + 1)
                            pool.tensor_tensor(pv[c][:].rearrange("p (h k) -> p h k", h=H),
                                               kv[b][c][:, HK:2 * HK].rearrange("p (h k) -> p h k", h=H),
                                               prob[b][:, c * H:(c + 1) * H].unsqueeze(2).to_broadcast([P, H, KD]),
                                               ALU.mult).then_inc(s_pvp, 1)

                    def own_values(tl):
                        b, t = tl.b, tl.t
                        wait(pool, s_att, t * 3)
                        pool.tensor_tensor(opv[:].rearrange("p (h k) -> p h k", h=H),
                                           own[b][:, HK:2 * HK].rearrange("p (h k) -> p h k", h=H),
                                           prob[b][:, ET * H:(ET + 1) * H].unsqueeze(2).to_broadcast([P, H, KD]),
                                           ALU.mult).then_inc(s_opv, 1)

                    def own_keys(tl):
                        pool.wait_ge(s_own[tl.b], tl.u * 16 + 16)
                        wait(pool, s_oscore, tl.t * 2)
                        passed(pool)
                        pool.tensor_tensor(oprod[:], flat(Q[:, bass.ds(tl.t, 1), :]), own[tl.b][:, 0:HK], ALU.mult).then_inc(s_oprod, 1)

                    pool.wait_ge(s_clear, 2)
                    gathers(Tile(0, 0, NT))
                    own_keys(Tile(0, 0, NT))

                    def body(tl):
                        if tl.has(-1):
                            products(tl.at(-1))
                            own_values(tl.at(-1))
                        if tl.has(1):
                            gathers(tl.at(1))
                            own_keys(tl.at(1))

                    sweep(pool, NT, 1, body)

                @block.scalar
                def _(act):
                    def stage(tl):
                        nc.scalar.activation(idx[tl.b][:], row(idx_all, tl.t, ET), ACT.Copy)
                        nc.scalar.activation(sel[tl.b][:], row(sel_all, tl.t, EW), ACT.Copy).then_inc(s_stage, 1)

                    stage(Tile(0, 0, NT))

                    def body(tl):
                        if tl.has(-2):
                            r = tl.at(-2)
                            wait(act, s_attT, r.t)
                            act.wait_ge(s_att, r.t * 3 + 3)
                            for h in range(H):
                                a = nc.scalar.activation(attn[:, h * KD:(h + 1) * KD], att[:, h * KD:(h + 1) * KD], ACT.Copy,
                                                         scale=den[:, h:h + 1])
                            a.then_inc(s_attn, 1)
                        if tl.has(-1):
                            q = tl.at(-1)
                            act.wait_ge(s_expo, q.t * 2 + 2)
                            nc.scalar.activation(prob[q.b][:], expo[:], ACT.Exp).then_inc(s_prob, 1)
                        if tl.has(1):
                            stage(tl.at(1))
                        if tl.has(-2):
                            wait(act, s_res, r.t)
                            act.wait_ge(s_attT, r.t + 1)
                            nc.scalar.activation(attT[:], BT[:, 0:HK], ACT.Copy).then_inc(s_attTc, 1)
                        if tl.has(-1):
                            act.wait_ge(s_prob, q.t + 1)
                            for c in range(ON_POOL, ET):
                                wait(act, s_out, (q.t - 1) * ET + ORDER.index(c) + 1)
                                for h in range(H):
                                    a = nc.scalar.activation(pv[c][:, h * KD:(h + 1) * KD],
                                                             kv[q.b][c][:, HK + h * KD:HK + (h + 1) * KD], ACT.Copy,
                                                             scale=prob[q.b][:, c * H + h:c * H + h + 1])
                                a.then_inc(s_pva, 1)

                    sweep(act, NT, 2, body)

                @block.tensor
                def _(pe):
                    pe.wait_ge(s_wo, 16)

                    def queries(tl, cs):
                        for c in cs:
                            wait(pe, s_mul, tl.t * ET + c - 1)
                            if c == 0:
                                pe.wait_ge(s_stage, tl.t + 1)
                            nc.tensor.matmul(Bq[(tl.b * ET + c) % 2][:, 0:HK], sel[tl.b][:, c * P:(c + 1) * P],
                                             flat(Q[:, bass.ds(tl.t, 1), :]), start=True, stop=True).then_inc(s_qe, 1)

                    def sums(tl, ks):
                        for k in ks:
                            c = ORDER[k]
                            if c < ON_POOL:
                                pe.wait_ge(s_pvp, tl.t * ON_POOL + c + 1)
                            else:
                                pe.wait_ge(s_pva, tl.t * (ET - ON_POOL) + c - ON_POOL + 1)
                            nc.tensor.matmul(BO[:, 0:HK], selT[tl.b][:, c, :], pv[c][:], start=k == 0, stop=k == ET - 1).then_inc(s_out, 1)

                    def body(tl):
                        if tl.has(0):
                            queries(tl, range(0, 2))
                        if tl.has(-1):
                            q = tl.at(-1)
                            wait(pe, s_top, q.t * 4 - 3)
                            pe.wait_ge(s_hot, q.t * 2 + 2)
                            for c in range(ET):
                                mm = nc.tensor.matmul(BM[:, 0:H * RANKS], selT[q.b][:, c, :], flat(spread[:, c, :, :]),
                                                      start=c == 0, stop=c == ET - 1)
                            mm.then_inc(s_byrank, 1)
                        if tl.has(0):
                            queries(tl, range(2, 3))
                        if tl.has(-1):
                            wait(pe, s_expo, q.t * 2)
                            pe.wait_ge(s_top, q.t * 4 + 4)
                            for c in range(ET):
                                mm = nc.tensor.matmul(BE[:, c * H:(c + 1) * H], sel[q.b][:, c * P:(c + 1) * P], top[:],
                                                      start=True, stop=True)
                            mm.then_inc(s_tope, 1)
                        if tl.has(0):
                            queries(tl, range(3, ET))
                        if tl.has(-2):
                            r = tl.at(-2)
                            wait(pe, s_attTc, r.t)
                            pe.wait_ge(s_attn, r.t + 1)
                            for c in range(HC):
                                mm = nc.tensor.transpose(BT[:, c * P:(c + 1) * P], attn[:, c * P:(c + 1) * P], ident[:])
                            mm.then_inc(s_attT, 1)
                        if tl.has(-1):
                            wait(pe, s_att, q.t * 3)
                            sums(q, range(0, 1))
                        if tl.has(-2):
                            wait(pe, s_sum, r.t)
                            pe.wait_ge(s_attTc, r.t + 1)
                            for c in range(HC):
                                mm = nc.tensor.matmul(BR[:, 0:D], attT[:, c * P:(c + 1) * P], wo[:, c, :],
                                                      start=c == 0, stop=c == HC - 1)
                            mm.then_inc(s_res, 1)
                        if tl.has(-1):
                            sums(q, range(1, ET))
                            for c in range(ET):
                                mm = nc.tensor.matmul(BD[:, 0:H], selT[q.b][:, c, :], prob[q.b][:, c * H:(c + 1) * H],
                                                      start=c == 0, stop=c == ET - 1)
                            mm.then_inc(s_den, 1)

                    sweep(pe, NT, 2, body)

                @block.vector
                def _(dve):
                    nc.vector.memset(ring[:, 0:ET * 2 * HK], 0.0).then_inc(s_clear, 1)

                    def times_keys(tl, c):
                        b, t = tl.b, tl.t
                        n, k = t * ET + c, (b * ET + c) % 2
                        dve.wait_ge(s_kv[b][c], tl.u * 16 + 16)
                        wait(dve, s_dot, n - 1)
                        dve.wait_ge(s_qe, n + 1)
                        nc.vector.tensor_tensor(prod[k][:], Bq[k][:, 0:HK], kv[b][c][:, 0:HK], ALU.mult).then_inc(s_mul, 1)

                    def by_head(tl, c):
                        b, t = tl.b, tl.t
                        n, k = t * ET + c, (b * ET + c) % 2
                        dve.wait_ge(s_mul, n + 1)
                        nc.vector.tensor_reduce(score[b][:, c, :], prod[k][:].rearrange("p (h k) -> p h k", h=H), AX_X,
                                                ALU.add).then_inc(s_dot, 1)

                    def own_scores(tl):
                        step = Chain(dve, s_oscore, tl, 2)
                        dve.wait_ge(s_oprod, tl.t + 1)
                        step(nc.vector.tensor_reduce(top1[:], oprod[:].rearrange("p (h k) -> p h k", h=H), AX_X, ALU.add))
                        step(nc.vector.tensor_scalar(oscore[tl.b][:], top1[:], 0.01, None, ALU.add), then=False)

                    def build_selT(tl):
                        nc.vector.tensor_tensor(selT[tl.b][:], row(row1_all, tl.t, ET).unsqueeze(2).to_broadcast([P, ET, P]),
                                                iota_i[:].unsqueeze(1).to_broadcast([P, ET, P]), ALU.is_equal).then_inc(s_selT, 1)

                    def by_rank(tl):
                        step = Chain(dve, s_hot, tl, 2)
                        dve.wait_ge(s_dot, tl.t * ET + ET)
                        wait(dve, s_byrank, tl.t)
                        step(nc.vector.tensor_tensor(hot[:], row(rank1_all, tl.t, ET).unsqueeze(2).to_broadcast([P, ET, RANKS]),
                                                     iota_r[:].unsqueeze(1).to_broadcast([P, ET, RANKS]), ALU.is_equal))
                        dve.wait_ge(s_selT, tl.t + 1)
                        step(nc.vector.tensor_tensor(spread[:], hot[:].unsqueeze(2).to_broadcast([P, ET, H, RANKS]),
                                                     score[tl.b][:].unsqueeze(3).to_broadcast([P, ET, H, RANKS]), ALU.mult), then=False)

                    def maximum(tl):
                        step = Chain(dve, s_top, tl, 4)
                        wait(dve, s_tope, tl.t)
                        dve.wait_ge(s_oscore, tl.t * 2 + 2)
                        wait(dve, s_prob, tl.t)
                        nc.vector.tensor_scalar(absent[:], iota_r[:], row(deg_all, tl.t), -1e30, ALU.is_gt, ALU.mult).then_inc(s_absent, 1)
                        dve.wait_ge(s_absent, tl.t + 1)
                        dve.wait_ge(s_byrank, tl.t + 1)
                        step(nc.vector.tensor_tensor(byrank[:], BM[:, 0:H * RANKS].rearrange("p (h r) -> p h r", h=H),
                                                     absent[:].unsqueeze(1).to_broadcast([P, H, RANKS]), ALU.add))
                        step(nc.vector.tensor_reduce(top2[:], byrank[:], AX_X, ALU.max))
                        step(nc.vector.tensor_tensor(top[:], top2[:], oscore[tl.b][:], ALU.max))
                        step(nc.vector.tensor_tensor(expo[:, ET * H:(ET + 1) * H], oscore[tl.b][:], top[:], ALU.subtract), then=False)

                    def exponents(tl):
                        step = Chain(dve, s_expo, tl, 2)
                        dve.wait_ge(s_tope, tl.t + 1)
                        wait(dve, s_prob, tl.t)
                        edges = expo[:, 0:ET * H].rearrange("p (c h) -> p c h", c=ET)
                        step(nc.vector.tensor_tensor(edges, score[tl.b][:], BE[:, 0:ET * H].rearrange("p (c h) -> p c h", c=ET),
                                                     ALU.subtract))
                        step(nc.vector.tensor_tensor(edges, edges, row(skip_all, tl.t, ET).unsqueeze(2).to_broadcast([P, ET, H]),
                                                     ALU.add), then=False)

                    def normalise(tl):
                        step = Chain(dve, s_att, tl, 3)
                        dve.wait_ge(s_den, tl.t + 1)
                        wait(dve, s_res, tl.t)
                        step(nc.vector.tensor_tensor(den[:], BD[:, 0:H], prob[tl.b][:, ET * H:(ET + 1) * H], ALU.add))
                        step(nc.vector.reciprocal(den[:], den[:]), then=False)
                        dve.wait_ge(s_opv, tl.t + 1)
                        step(nc.vector.tensor_tensor(att[:], BO[:, 0:HK], opv[:], ALU.add), then=False)

                    def residual(tl):
                        wait(dve, s_sum, tl.t)
                        dve.wait_ge(s_res, tl.t + 1)
                        r = flat(xs[:, bass.ds(tl.t, 1), :])
                        nc.vector.tensor_tensor(r, r, BR[:, 0:D], ALU.add).then_inc(s_sum, 1)

                    def statistics(tl):
                        if isinstance(tl.u, int):
                            dve.wait_ge(s_sum, tl.t + 1)
                        nc.vector.bn_stats(flat(stats[:, bass.ds(tl.t, 1), :]), flat(xs[:, bass.ds(tl.t, 1), :])).then_inc(s_stats, 1)

                    def body(tl):
                        if tl.has(-1):
                            by_rank(tl.at(-1))
                        if tl.has(-2):
                            normalise(tl.at(-2))
                        if tl.has(0):
                            times_keys(tl, 0)
                            times_keys(tl, 1)
                            by_head(tl, 0)
                        if tl.has(-1):
                            maximum(tl.at(-1))
                        if tl.has(0):
                            by_head(tl, 1)
                            times_keys(tl, 2)
                            times_keys(tl, 3)
                            by_head(tl, 2)
                        if tl.has(-1):
                            exponents(tl.at(-1))
                        if tl.has(0):
                            times_keys(tl, 4)
                            by_head(tl, 3)
                            by_head(tl, 4)
                            own_scores(tl)
                            build_selT(tl)
                        if tl.has(-3):
                            residual(tl.at(-3))
                        if tl.has(-4):
                            statistics(tl.at(-4))

                    sweep(dve, NT, 4, body)
                    dve.wait_ge(s_sum, NT)
                    dve.wait_ge(s_selT, NT)
                    dve.wait_ge(s_stats, NT)

        x2 = Q[:].rearrange("p t m -> p (t m)")[:, 0:NT * XW].rearrange("p (t w) -> p t w", w=XW)
        PARTS = ((0, NT // 2), (NT // 2, NT - 4), (NT - 4, NT))
        node_all = sb("f_nodes", [P, NT, 4])
        wsa = sb("f_wsa", [P, DC, D])
        wgcn = sb("f_wgcn", [P, DC, D])
        wab = sb("f_wab", [P, 2 * DC, 2])
        bg_b = sb("f_bg", [P, D])
        s_var = sem("f_var")
        s_std = sem("f_std")
        s_norm = sem("f_norm")

        def moments(dve, k):
            n0 = k * (NT + 1)
            for t in range(NT):
                nc.vector.bn_aggr(mv[:, t, :], stats[:, t, :]).then_inc(s_norm, 1)
            dve.wait_ge(s_norm, n0 + NT)
            nc.vector.tensor_scalar(std[:], mv[:, :, 1], EPS, None, ALU.add).then_inc(s_var, 1)
            dve.wait_ge(s_std, k + 1)
            nc.vector.reciprocal(rstd[:], std[:]).then_inc(s_norm, 1)
            dve.wait_ge(s_norm, n0 + NT + 1)

        with ExitStack() as ph:
            def pb(name, shape):
                return ph.enter_context(nc.psum_tensor(name, shape, F32))

            def sb3(name, shape, dt=F32):
                return ph.enter_context(nc.sbuf_tensor(name, shape, dt))

            wsaT = sb3("f_wsaT", [P, DC, D])
            asa = sb3("f_asa", [P, DC, 2])
            bias4 = sb3("f_bias4", [P, 4])
            coef = sb3("f_coef", [P, DC, 4])
            staged = [sb3(f"f_staged{b}", [P, D]) for b in range(2)]
            stagedT = [sb3(f"f_stagedT{b}", [P, DC, P]) for b in range(2)]
            over = sb3("f_over", [P, 3])
            over1 = sb3("f_over1", [P, 1])
            BT = [pb(f"f_B3T{b}", [P, 512]) for b in range(2)]
            BN = [pb(f"f_B3N{b}", [P, 512]) for b in range(2)]
            BC = pb("f_B3C", [P, 512])
            BF = pb("f_B3F", [P, 512])
            s_w3 = sem("f_w3")
            s_init = sem("f_init")
            s_over = sem("f_over")
            s_oversum = sem("f_oversum")
            s_coef = sem("f_coef")
            s_row3 = sem("f_row3")
            s_t3 = sem("f_t3")
            s_tc3 = sem("f_tc3")
            s_xs3 = sem("f_xs3")
            s_n3 = sem("f_n3")
            s_node3 = sem("f_node3")
            s_xout = sem("f_xout")

            with nc.Block() as block:
                @block.sync
                def _(sp):
                    loads = ((wsaT[:], dram["W_saT"].rearrange("(c p) n -> p c n", p=P)), (asa[:], dram["a_sa"].rearrange("(c p) n -> p c n", p=P)),
                             (wab[:], dram["Wab"].rearrange("(c p) n -> p c n", p=P)), (bias4[:, 2:4], dram["bab"].partition_broadcast(P)),
                             (wsa[:], dram["W_sa"].rearrange("(c p) n -> p c n", p=P)), (wgcn[:], dram["W_gcn"].rearrange("(c p) n -> p c n", p=P)),
                             (bg_b[:], dram["b_gcn"].partition_broadcast(P)))
                    for dst, src in loads:
                        sp.dma_start(dst, src).then_inc(s_w3, 16)

                    table = x_table.rearrange("(t p) w -> p t w", p=P)
                    for first, last in PARTS:
                        sp.wait_ge(s_node3, last * 2)
                        sp.wait_ge(s_xs3, last)
                        sp.dma_start(table[:, first:last, :], x2[:, first:last, :]).then_inc(s_xout, 16)
                    sp.wait_ge(s_xout, 16 * len(PARTS))

                @block.gpsimd
                def _(pool):
                    pool.memset(bias4[:, 0:2], 0.0).then_inc(s_init, 1)
                    pool.memset(x2[:, :, D + 1:XW], 0.0).then_inc(s_init, 1)

                @block.tensor
                def _(pe):
                    pe.wait_ge(s_w3, 16 * 7)
                    for dc in range(DC):
                        for oc in range(DC):
                            mm = nc.tensor.matmul(BC[:, dc * 2:dc * 2 + 2], wsaT[:, oc, dc * P:(dc + 1) * P], asa[:, oc, :],
                                                  start=oc == 0, stop=oc == DC - 1)
                    mm.then_inc(s_coef, 1)
                    pe.wait_ge(s_over, 7)
                    nc.tensor.matmul(BF[:, 0:1], ones[:], over1[:], start=True, stop=True).then_inc(s_oversum, 1)
                    pe.wait_ge(s_coef, 3)

                    def body(tl):
                        if tl.has(0):
                            t, b = tl.t, tl.b
                            wait(pe, s_tc3, t - 1)
                            pe.wait_ge(s_row3, t + 1)
                            for dc in range(DC):
                                mm = nc.tensor.transpose(BT[b][:, dc * P:(dc + 1) * P], staged[b][:, dc * P:(dc + 1) * P], ident[:])
                            mm.then_inc(s_t3, 1)
                        if tl.has(-1):
                            q = tl.at(-1)
                            wait(pe, s_node3, q.t * 2 - 2)
                            pe.wait_ge(s_tc3, q.t + 1)
                            for dc in range(DC):
                                mm = nc.tensor.matmul(BN[q.b][:, 0:4], stagedT[q.b][:, dc, :], coef[:, dc, :],
                                                      start=dc == 0, stop=dc == DC - 1)
                            mm.then_inc(s_n3, 1)

                    sweep(pe, NT, 1, body)

                @block.scalar
                def _(act):
                    act.wait_ge(s_var, 1)
                    nc.scalar.activation(std[:], std[:], ACT.Sqrt).then_inc(s_std, 1)

                    def body(tl):
                        t, b = tl.t, tl.b
                        wait(act, s_n3, t - 1)
                        act.wait_ge(s_t3, t + 1)
                        nc.scalar.activation(flat(stagedT[b][:]), BT[b][:, 0:D], ACT.Copy).then_inc(s_tc3, 1)
                        nc.scalar.activation(flat(x2[:, bass.ds(t, 1), 0:D]), staged[b][:], ACT.Copy).then_inc(s_xs3, 1)

                    sweep(act, NT, 0, body)

                @block.vector
                def _(dve):
                    nc.vector.tensor_reduce(over[:, 0:1], full_all[:], AX_X, ALU.max).then_inc(s_over, 1)
                    nc.vector.tensor_reduce(over[:, 1:2], deg_all[:], AX_X, ALU.max).then_inc(s_over, 1)
                    nc.vector.tensor_reduce(over[:, 2:3], end_all[:], AX_X, ALU.max).then_inc(s_over, 1)
                    dve.wait_ge(s_over, 3)
                    for k, most in ((0, 0), (1, RANKS), (2, EW)):
                        nc.vector.tensor_scalar(over[:, k:k + 1], over[:, k:k + 1], float(most), None, ALU.is_gt).then_inc(s_over, 1)
                    dve.wait_ge(s_over, 6)
                    nc.vector.tensor_reduce(over1[:], over[:], AX_X, ALU.add).then_inc(s_over, 1)
                    dve.wait_ge(s_oversum, 1)
                    nc.vector.tensor_scalar(flag[:], BF[:, 0:1], 0.0, None, ALU.is_gt).then_inc(s_over, 1)
                    dve.wait_ge(s_init, 2)
                    dve.wait_ge(s_coef, 1)
                    nc.vector.tensor_copy(coef[:, :, 0:2], BC[:, 0:2 * DC].rearrange("p (c k) -> p c k", k=2)).then_inc(s_coef, 1)
                    nc.vector.tensor_copy(coef[:, :, 2:4], wab[:, DC:2 * DC, :]).then_inc(s_coef, 1)
                    moments(dve, 0)

                    def body(tl):
                        if tl.has(0):
                            t, b = tl.t, tl.b
                            wait(dve, s_xs3, t - 1)
                            nc.vector.tensor_scalar(staged[b][:, 0:D], flat(xs[:, bass.ds(t, 1), :]), mv[:, bass.ds(t, 1), 0],
                                                    rstd[:, bass.ds(t, 1)], ALU.subtract, ALU.mult).then_inc(s_row3, 1)
                        if tl.has(-1):
                            q = tl.at(-1)
                            dve.wait_ge(s_n3, q.t + 1)
                            nc.vector.tensor_tensor(flat(node_all[:, bass.ds(q.t, 1), :]), BN[q.b][:, 0:4], bias4[:], ALU.add).then_inc(s_node3, 1)
                            nc.vector.tensor_scalar(x2[:, bass.ds(q.t, 1), D], BN[q.b][:, 1:2], 1.0, None, ALU.mult).then_inc(s_node3, 1)

                    sweep(dve, NT, 1, body)
                    dve.wait_ge(s_over, 8)

        with ExitStack() as ph:
            def pb(name, shape):
                return ph.enter_context(nc.psum_tensor(name, shape, F32))

            def sb4(name, shape, dt=F32):
                return ph.enter_context(nc.sbuf_tensor(name, shape, dt))

            xg = [ring[:, b * ET * XW:(b + 1) * ET * XW].rearrange("p (c w) -> p c w", c=ET) for b in range(2)]
            yg = ring[:, 2 * ET * XW:3 * ET * XW].rearrange("p (c w) -> p c w", c=ET)
            ys = xs
            arg = sb4("f_arg", [P, ET])
            live = sb4("f_live", [P, ET])
            esum = sb4("f_esum", [P, 1])
            zs = sb4("f_zs", [P, 2 * D])
            zT = sb4("f_zT", [P, 4, P])
            gate = sb4("f_gate", [P, 2])
            yt = sb4("f_yt", [P, D])
            BE, B1, B2, BZT, BR, BA = (pb(n, [P, 512]) for n in ("f_4E", "f_41", "f_42", "f_4T", "f_4R", "f_4A"))

            s_clear = sem("f_clear4")
            s_idx = sem("f_idx4")
            s_stage = sem("f_stage4")
            s_xg = [[sem(f"f_xg{b}{c}") for c in range(ET)] for b in range(2)]
            s_selT = sem("f_selT4")
            s_left = sem("f_left")
            s_arg = sem("f_arg")
            s_w = sem("f_w")
            s_yg = sem("f_yg")
            s_z1 = sem("f_z14")
            s_z = sem("f_z4")
            s_zs = sem("f_zs")
            s_zT = sem("f_zT")
            s_zTc = sem("f_zTc")
            s_f = sem("f_f")
            s_gz = sem("f_gz")
            s_ge = sem("f_ge")
            s_fin = sem("f_fin")
            s_y = sem("f_y")
            s_ye = sem("f_ye")
            s_ylast = sem("f_ylast")
            s_out = sem("f_out")
            s_fin2 = sem("f_fin2")
            s_stats = sem("f_stats4")
            FIN = 3

            with nc.Block() as block:
                @block.sync
                def _(sp):
                    out_t = out.rearrange("(t p) d -> p t d", p=P)
                    half = NT // 2
                    for k in range(2):
                        sp.wait_ge(s_ylast, (k + 1) * half)
                        sp.dma_start(out_t[:, k * half:(k + 1) * half, :], ys[:, k * half:(k + 1) * half, :]).then_inc(s_out, 16)
                    sp.wait_ge(s_out, 32)

                @block.gpsimd
                def _(pool):
                    pool.wait_ge(s_clear, 1)

                    def gathers(tl):
                        wait(pool, s_z1, tl.t - 1)
                        wait(pool, s_yg, (tl.t - 1) * ET)
                        pool.wait_ge(s_idx, tl.t + 1)
                        passed(pool)
                        for c in range(ET):
                            pool.indirect_dma_start(
                                out=xg[tl.b][:, c, :], out_offset=None, in_=x_table,
                                in_offset=bass.IndirectOffsetOnAxis(ap=idx[tl.b][:, c:c + 1], axis=0),
                                bounds_check=NP - 1, oob_is_err=False).then_inc(s_xg[tl.b][c], 16)

                    gathers(Tile(0, 0, NT))
                    gathers(Tile(0, 1, NT))

                    def body(tl):
                        if tl.has(2):
                            gathers(tl.at(2))

                    sweep(pool, NT, 0, body)

                @block.scalar
                def _(act):
                    def stage_idx(tl):
                        nc.scalar.activation(idx[tl.b][:], row(idx_all, tl.t, ET), ACT.Copy).then_inc(s_idx, 1)

                    def stage_sel(tl):
                        nc.scalar.activation(sel[tl.b][:], row(sel_all, tl.t, EW), ACT.Copy).then_inc(s_stage, 1)

                    stage_idx(Tile(0, 0, NT))
                    stage_idx(Tile(0, 1, NT))
                    stage_sel(Tile(0, 0, NT))

                    def body(tl):
                        if tl.has(0):
                            wait(act, s_z, tl.t)
                            act.wait_ge(s_arg, tl.t * 4 + 4)
                            nc.scalar.activation(yg[:, :, D], arg[:], ACT.Exp, scale=-1.0).then_inc(s_w, 1)
                        if tl.has(2):
                            stage_idx(tl.at(2))
                        if tl.has(1):
                            stage_sel(tl.at(1))
                        if tl.has(-1):
                            q = tl.at(-1)
                            wait(act, s_f, q.t)
                            act.wait_ge(s_zT, q.t + 1)
                            nc.scalar.activation(flat(zT[:]), BZT[:], ACT.Copy).then_inc(s_zTc, 1)
                            act.wait_ge(s_gz, q.t + 1)
                            nc.scalar.activation(gate[:], gate[:], ACT.Tanh, scale=0.5).then_inc(s_ge, 1)
                            act.wait_ge(s_y, q.t + 1)
                            nc.scalar.activation(yt[:], yt[:], ACT.Tanh, scale=0.5).then_inc(s_ye, 1)

                    sweep(act, NT, 1, body)
                    act.wait_ge(s_var, 2)
                    nc.scalar.activation(std[:], std[:], ACT.Sqrt).then_inc(s_std, 1)

                @block.tensor
                def _(pe):
                    def body(tl):
                        u, b, t = tl.u, tl.b, tl.t
                        if tl.has(0):
                            pe.wait_ge(s_stage, t + 1)
                            wait(pe, s_arg, t * 4 - 3)
                            for c in range(ET):
                                mm = nc.tensor.matmul(BE[:, c:c + 1], sel[b][:, c * P:(c + 1) * P], node_all[:, bass.ds(t, 1), 0],
                                                      start=True, stop=True)
                            mm.then_inc(s_left, 1)
                        if tl.has(-1):
                            q = tl.at(-1)
                            pe.wait_ge(s_zs, q.t * 4 + 4)
                            wait(pe, s_zTc, q.t)
                            for k in range(2 * DC):
                                mm = nc.tensor.transpose(BZT[:, k * P:(k + 1) * P], zs[:, k * P:(k + 1) * P], ident[:])
                            mm.then_inc(s_zT, 1)
                        if tl.has(0):
                            pe.wait_ge(s_selT, t + 1)
                            for c in range(ET):
                                pe.wait_ge(s_xg[b][c], u * 16 + 16)
                                mm = nc.tensor.matmul(B1[:, 0:D], selT[b][:, c, :], xg[b][:, c, 0:D], start=c == 0, stop=c == ET - 1)
                            mm.then_inc(s_z1, 1)
                        if tl.has(-1):
                            pe.wait_ge(s_zTc, q.t + 1)
                            wait(pe, s_y, q.t)
                            for dc in range(DC):
                                nc.tensor.matmul(BR[:, 0:D], zT[:, DC + dc, :], wsa[:, dc, :], start=dc == 0, stop=dc == DC - 1)
                            for dc in range(DC):
                                nc.tensor.matmul(BR[:, D:2 * D], zT[:, dc, :], wgcn[:, dc, :], start=dc == 0, stop=dc == DC - 1)
                            for dc in range(DC):
                                mm = nc.tensor.matmul(BA[:, 0:2], zT[:, dc, :], wab[:, dc, :], start=dc == 0, stop=dc == DC - 1)
                            mm.then_inc(s_f, 1)
                        if tl.has(0):
                            for c in range(ET):
                                pe.wait_ge(s_yg, t * ET + c + 1)
                                mm = nc.tensor.matmul(B2[:, 0:D + 1], selT[b][:, c, :], yg[:, c, 0:D + 1], start=c == 0, stop=c == ET - 1)
                            mm.then_inc(s_z, 1)

                    sweep(pe, NT, 1, body)

                @block.vector
                def _(dve):
                    nc.vector.memset(ring[:, 0:3 * ET * XW], 0.0).then_inc(s_clear, 1)

                    def weights(tl):
                        b, t = tl.b, tl.t
                        wait(dve, s_z, t - 1)
                        nc.vector.tensor_tensor(selT[b][:], row(row1_all, t, ET).unsqueeze(2).to_broadcast([P, ET, P]),
                                                iota_i[:].unsqueeze(1).to_broadcast([P, ET, P]), ALU.is_equal).then_inc(s_selT, 1)
                        step = Chain(dve, s_arg, tl, 4)
                        dve.wait_ge(s_left, t + 1)
                        wait(dve, s_w, t)
                        for c in range(ET):
                            dve.wait_ge(s_xg[b][c], tl.u * 16 + 16)
                        step(nc.vector.tensor_tensor(arg[:], BE[:, 0:ET], xg[b][:, :, D], ALU.add), then=False)
                        step(nc.vector.tensor_scalar(live[:], row(row1_all, t, ET), 1.0, None, ALU.is_ge))
                        step(nc.vector.tensor_tensor(arg[:], arg[:], live[:], ALU.mult))
                        step(nc.vector.scalar_tensor_tensor(out=arg[:], in0=arg[:], scalar=0.01, in1=arg[:], op0=ALU.mult, op1=ALU.max),
                             then=False)

                    def weighted(tl):
                        b, t = tl.b, tl.t
                        dve.wait_ge(s_w, t + 1)
                        for c in range(ET):
                            nc.vector.tensor_scalar(yg[:, c, 0:D], xg[b][:, c, 0:D], yg[:, c, D:D + 1], None, ALU.mult).then_inc(s_yg, 1)

                    def take_sums(tl):
                        t = tl.t
                        step = Chain(dve, s_zs, tl, 4)
                        dve.wait_ge(s_z, t + 1)
                        wait(dve, s_zT, t)
                        step(nc.vector.tensor_scalar(esum[:], B2[:, D:D + 1], 1e-5, None, ALU.add))
                        step(nc.vector.reciprocal(esum[:], esum[:]), then=False)
                        step(nc.vector.tensor_copy(zs[:, 0:D], B1[:, 0:D]))
                        step(nc.vector.tensor_scalar(zs[:, D:2 * D], B2[:, 0:D], esum[:, 0:1], None, ALU.mult), then=False)

                    def finish(tl):
                        t = tl.t
                        step = Chain(dve, s_fin, tl, FIN)
                        wait(dve, s_fin, t * FIN)
                        wait(dve, s_fin2, t * 2)
                        dve.wait_ge(s_f, t + 1)
                        nc.vector.tensor_tensor(gate[:], BA[:, 0:2], flat(node_all[:, bass.ds(t, 1), 2:4]), ALU.add).then_inc(s_gz, 1)
                        step(nc.vector.tensor_tensor(yt[:], BR[:, D:2 * D], bg_b[:], ALU.add), then=False)
                        dve.wait_ge(s_ge, t + 1)
                        step(nc.vector.tensor_scalar(gate[:], gate[:], 0.5, 0.5, ALU.mult, ALU.add))
                        step(nc.vector.tensor_scalar(yt[:], yt[:], gate[:, 1:2], None, ALU.mult))
                        nc.vector.scalar_tensor_tensor(out=yt[:], in0=BR[:, 0:D], scalar=gate[:, 0:1], in1=yt[:],
                                                       op0=ALU.mult, op1=ALU.add).then_inc(s_y, 1)
                        if tl.has(-1):
                            statistics(tl.at(-1))

                    def finish2(tl):
                        t = tl.t
                        step = Chain(dve, s_fin2, tl, 2)
                        dve.wait_ge(s_ye, t + 1)
                        step(nc.vector.tensor_scalar(yt[:], yt[:], 0.5, 0.5, ALU.mult, ALU.add))
                        step(nc.vector.tensor_tensor(flat(ys[:, bass.ds(t, 1), :]), yt[:], flat(x2[:, bass.ds(t, 1), 0:D]), ALU.add),
                             then=False)

                    def statistics(tl):
                        nc.vector.bn_stats(flat(stats[:, bass.ds(tl.t, 1), :]), flat(ys[:, bass.ds(tl.t, 1), :])).then_inc(s_stats, 1)

                    def body(tl):
                        if tl.has(-1):
                            take_sums(tl.at(-1))
                        if tl.has(0):
                            weights(tl)
                        if tl.has(-2):
                            finish2(tl.at(-2))
                        if tl.has(0):
                            weighted(tl)
                        if tl.has(-1):
                            finish(tl.at(-1))

                    sweep(dve, NT, 2, body)
                    dve.wait_ge(s_fin2, NT * 2)
                    statistics(Tile(NT // 2 - 1, 1, NT))
                    dve.wait_ge(s_stats, NT)
                    moments(dve, 1)
                    with dve.Fori(0, NT) as t:
                        r = flat(ys[:, bass.ds(t, 1), :])
                        nc.vector.tensor_scalar(r, r, mv[:, bass.ds(t, 1), 0], rstd[:, bass.ds(t, 1)], ALU.subtract,
                                                ALU.mult).then_inc(s_ylast, 1)


def dense_path(nc, x, xT, adj, Wq, Wk, Wv, Wo, W_sa, W_saT, a_sa, W_gcn, b_gcn, Wab, bab, out):
    NP, D = x.shape
    NT = NP // P
    HK = Wq.shape[1]
    KD = 64
    NHP = HK // P
    DC = D // P
    NCH = 8
    CW = NP // NCH
    GROUPS = [4, 3, 3, 3, 4, 3, 3, 3]
    START = [sum(GROUPS[:g]) for g in range(8)]
    assert sum(GROUPS) == NT and NT % 2 == 0 and CW <= 512
    PROJ = 3 * NCH
    PER_HP = PROJ + NT * 2 * NCH
    EPS = 1e-5
    NORM0 = 3 * NT + 1
    HEAD1 = NORM0 + 5
    STEPS = 12
    LAST = HEAD1 + NT * STEPS + NORM0

    with ExitStack() as ctx:
        def sb(name, shape):
            return ctx.enter_context(nc.sbuf_tensor(name, shape, F32))

        def pb(name, shape):
            return ctx.enter_context(nc.psum_tensor(name, shape, F32))

        def sem(name):
            return ctx.enter_context(nc.semaphore(name))

        ident = sb("ident", [P, P])
        eye_bias = sb("eye_bias", [P, P])
        xs = sb("xs", [P, NT, D])
        big = sb("big", [P, 2 * NP])
        xTs = big[:, :].rearrange("p (c n) -> p c n", c=DC)
        wpair = sb("wpair", [P, 3, DC, P])
        wo_s = sb("wo_s", [P, D])
        QK = sb("QK", [P, 2 * NP])
        QT, KT = QK[:, 0:NP], QK[:, NP:2 * NP]
        V = sb("V", [P, NT, P])
        SR = V[:].rearrange("p t m -> p (t m)")
        qtile = sb("qtile", [P, P])
        bias = [sb(f"bias{u}", [P, NP]) for u in range(2)]
        prob = [sb(f"prob{h}", [P, NP]) for h in range(2)]
        PT = [sb(f"PT{h}", [P, NP]) for h in range(2)]
        negmax = sb("negmax", [P, 2])
        rowmax = sb("rowmax", [P, 2])
        rowsum = sb("rowsum", [P, 2])
        rinv = sb("rinv", [P, 2])
        oT = sb("oT", [P, P])
        stats = sb("stats", [P, NT, 6])
        mv = sb("mv", [P, NT, 2])
        std = sb("std", [P, NT])
        rstd = sb("rstd", [P, NT])
        wsa = sb("wsa", [P, DC, D])
        wsaT = sb("wsaT", [P, DC, D])
        asa = sb("asa", [P, DC, 2])
        wgcn = sb("wgcn", [P, DC, D])
        wab = sb("wab", [P, 2 * DC, 2])
        bab_b = sb("bab_b", [P, 2])
        bg_b = sb("bg_b", [P, D])
        coef = sb("coef", [P, DC, 4])
        ones = sb("ones", [P, P])
        wr_b = sb("wr_b", [P, DC, P])
        node = sb("node", [P, NT, 4])
        zs = sb("zs", [P, 2, D])
        zT = sb("zT", [P, 4, P])
        gate = sb("gate", [P, 2])
        esum = sb("esum", [P, 1])
        yt = sb("yt", [P, D])
        ys = QK[:, :].rearrange("p (t d) -> p t d", d=D)

        S = [pb(f"S{b}", [P, 512]) for b in range(4)]
        T = [pb(f"T{b}", [P, 512]) for b in range(2)]
        O = pb("O", [P, 512])
        R = pb("R", [P, 512])

        s_id = sem("s_id")
        s_x = sem("s_x")
        s_w = sem("s_w")
        s_adj = [sem(f"s_adj{u}") for u in range(2)]
        s_bias = [sem(f"s_bias{u}") for u in range(2)]
        s_bias_used = [sem(f"s_bias_used{u}") for u in range(2)]
        s_chunk = sem("s_chunk")
        s_taken = sem("s_taken")
        s_q = sem("s_q")
        s_max = sem("s_max")
        s_dve = sem("s_dve")
        s_exp = sem("s_exp")
        s_tr = [sem(f"s_tr{b}") for b in range(2)]
        s_cp = [sem(f"s_cp{b}") for b in range(2)]
        s_pv = sem("s_pv")
        s_oT = sem("s_oT")
        s_res = sem("s_res")
        s_acc = sem("s_acc")
        s_att = sem("s_att")
        s_v = sem("s_v")
        s_w1 = sem("s_w1")
        s_var = sem("s_var")
        s_std = sem("s_std")
        s_coef = sem("s_coef")
        s_xT = sem("s_xT")
        s_xTc = sem("s_xTc")
        s_sr = sem("s_sr")
        s_node = sem("s_node")
        s_adj1 = [sem(f"s_adj1{u}") for u in range(2)]
        s_leak = sem("s_leak")
        s_ee = sem("s_ee")
        s_z = sem("s_z")
        s_zs = sem("s_zs")
        s_zT = sem("s_zT")
        s_zTc = sem("s_zTc")
        s_f = sem("s_f")
        s_gz = sem("s_gz")
        s_ge = sem("s_ge")
        s_y = sem("s_y")
        s_ye = sem("s_ye")
        s_out = sem("s_out")

        with nc.Block() as block:
            @block.sync
            def _(sp):
                sp.dma_start(xs[:], x.rearrange("(t p) d -> p t d", p=P)).then_inc(s_x, 16)
                sp.dma_start(xTs, xT.rearrange("(c p) n -> p c n", p=P)).then_inc(s_x, 16)
                with sp.Fori(0, NHP) as hp:
                    sp.wait_ge(s_acc, hp * (2 * NT))
                    for w, W in enumerate((Wq, Wk, Wv)):
                        sp.dma_start(wpair[:, w], W.rearrange("(c p) (h m) -> h p c m", p=P, m=P)[bass.ds(hp, 1)].rearrange("h p c m -> (h p) c m")).then_inc(s_w, 16)
                    sp.dma_start(wo_s[:], Wo.rearrange("(h p) d -> h p d", p=P)[bass.ds(hp, 1)].rearrange("h p d -> (h p) d")).then_inc(s_w, 16)
                    with sp.Fori(0, NT // 2) as t2:
                        for u in range(2):
                            sp.wait_ge(s_bias_used[u], hp * (NT // 2) + t2)
                            sp.dma_start(bias[u][:], adj[bass.ds((t2 * 2 + u) * P, P), :]).then_inc(s_adj[u], 16)

                for dst, src in ((wsa[:], W_sa.rearrange("(c p) n -> p c n", p=P)), (wsaT[:], W_saT.rearrange("(c p) n -> p c n", p=P)),
                                 (asa[:], a_sa.rearrange("(c p) n -> p c n", p=P)), (wgcn[:], W_gcn.rearrange("(c p) n -> p c n", p=P)),
                                 (wab[:], Wab.rearrange("(c p) n -> p c n", p=P)), (bab_b[:], bab.partition_broadcast(P)),
                                 (bg_b[:], b_gcn.partition_broadcast(P))):
                    sp.dma_start(dst, src).then_inc(s_w1, 16)
                sp.wait_ge(s_acc, NHP * NT * 2)
                with sp.Fori(0, NT // 2) as t2:
                    for u in range(2):
                        sp.wait_ge(s_z, t2 * 4)
                        sp.dma_start(bias[u][:], adj[bass.ds((t2 * 2 + u) * P, P), :]).then_inc(s_adj1[u], 16)
                sp.wait_ge(s_var, 2)
                sp.wait_ge(s_v, LAST)
                sp.dma_start(out.rearrange("(t p) d -> p t d", p=P), ys[:]).then_inc(s_out, 16)
                sp.wait_ge(s_out, 16)

            @block.gpsimd
            def _(pool):
                pool.memset(ident[:], 0.0).then_inc(s_id, 1)
                pool.memset(eye_bias[:], -BIG).then_inc(s_id, 1)
                pool.wait_ge(s_id, 2)
                for m, one in ((ident, 1.0), (eye_bias, 0.01)):
                    pool.affine_select(out=m[:], in_=m[:], compare_op=ALU.not_equal, fill=one, base=0,
                                       pattern=[[-1, P]], channel_multiplier=1).then_inc(s_id, 1)

            @block.tensor
            def _(pe):
                pe.wait_ge(s_id, 4)
                pe.wait_ge(s_x, 32)
                with pe.Fori(0, NHP) as hp:
                    pe.wait_ge(s_w, hp * 64 + 64)
                    n = 0
                    for w in range(2):
                        for c in range(NCH):
                            pe.wait_ge(s_taken, hp * PER_HP + n + 1)
                            for dc in range(DC):
                                mm = nc.tensor.matmul(S[n % 4][:, 0:CW], wpair[:, w, dc, :], xTs[:, dc, c * CW:(c + 1) * CW],
                                                      start=dc == 0, stop=dc == DC - 1)
                            mm.then_inc(s_chunk, 1)
                            n += 1
                    for g in range(8):
                        pe.wait_ge(s_taken, hp * PER_HP + n + 1)
                        for b in range(GROUPS[g]):
                            k = START[g] + b
                            for dc in range(DC):
                                mm = nc.tensor.matmul(S[n % 4][:, b * P:(b + 1) * P], xTs[:, dc, k * P:(k + 1) * P],
                                                      wpair[:, 2, dc, :], start=dc == 0, stop=dc == DC - 1)
                        mm.then_inc(s_chunk, 1)
                        n += 1
                    with pe.Fori(0, NT) as i:
                        it = hp * NT + i
                        pe.wait_ge(s_q, it + 1)
                        for h in range(2):
                            for c in range(NCH):
                                m = h * NCH + c
                                pe.wait_ge(s_taken, hp * PER_HP + i * (2 * NCH) + PROJ + m + 1)
                                nc.tensor.matmul(S[m % 4][:, 0:CW], qtile[h * KD:(h + 1) * KD, :],
                                                 KT[h * KD:(h + 1) * KD, c * CW:(c + 1) * CW],
                                                 start=True, stop=True).then_inc(s_chunk, 1)
                        for h in range(2):
                            pe.wait_ge(s_exp, it * 2 + h + 1)

                            def pv(g):
                                pe.wait_ge(s_cp[g % 2], it * 8 + h * 4 + g // 2 + 1)
                                for b in range(GROUPS[g]):
                                    k = START[g] + b
                                    mm = nc.tensor.matmul(O[h * KD:(h + 1) * KD, 0:P], V[:, k, h * KD:(h + 1) * KD],
                                                          PT[h][:, k * P:(k + 1) * P], start=k == 0, stop=k == NT - 1)
                                return mm

                            for g in range(8):
                                pe.wait_ge(s_cp[g % 2], it * 8 + h * 4 + g // 2)
                                for b in range(GROUPS[g]):
                                    k = START[g] + b
                                    mm = nc.tensor.transpose(T[g % 2][:, b * P:(b + 1) * P], prob[h][:, k * P:(k + 1) * P], ident[:])
                                mm.then_inc(s_tr[g % 2], 1)
                                if g:
                                    pv(g - 1)
                            pv(7).then_inc(s_pv, 1)
                            pe.wait_ge(s_oT, it * 2 + h + 1)
                            pe.wait_ge(s_acc, it * 2 + h)
                            nc.tensor.matmul(R[:, 0:D], oT[h * KD:(h + 1) * KD, :], wo_s[h * KD:(h + 1) * KD, :],
                                             start=True, stop=True).then_inc(s_res, 1)

                pe.wait_ge(s_w1, 16 * 7)
                pe.wait_ge(s_acc, NHP * NT * 2)
                for dc in range(DC):
                    for oc in range(DC):
                        mm = nc.tensor.matmul(R[:, dc * 2:dc * 2 + 2], wsaT[:, oc, dc * P:(dc + 1) * P], asa[:, oc, :],
                                              start=oc == 0, stop=oc == DC - 1)
                mm.then_inc(s_coef, 1)
                pe.wait_ge(s_v, NORM0)
                for t in range(NT):
                    if t:
                        pe.wait_ge(s_xTc, t)
                    for dc in range(DC):
                        mm = nc.tensor.transpose(S[0][:, dc * P:(dc + 1) * P], xs[:, t, dc * P:(dc + 1) * P], ident[:])
                    mm.then_inc(s_xT, 1)
                pe.wait_ge(s_xTc, NT)
                pe.wait_ge(s_coef, 3)
                for c in range(NCH):
                    if c:
                        pe.wait_ge(s_xTc, NT + c)
                    for dc in range(DC):
                        mm = nc.tensor.matmul(S[1][:, 0:CW], wr_b[:, dc, :], xTs[:, dc, c * CW:(c + 1) * CW],
                                              start=dc == 0, stop=dc == DC - 1)
                    mm.then_inc(s_sr, 1)
                for t in range(NT):
                    for dc in range(DC):
                        mm = nc.tensor.matmul(S[2][:, t * 4:t * 4 + 4], xTs[:, dc, t * P:(t + 1) * P], coef[:, dc, :],
                                              start=dc == 0, stop=dc == DC - 1)
                mm.then_inc(s_node, 1)
                pe.wait_ge(s_node, 2)
                with pe.Fori(0, NT // 2) as t2:
                    for u in range(2):
                        i = t2 * 2 + u
                        it = NHP * NT + t2 * 2 + u
                        for h in range(2):
                            if h == 0:
                                pe.wait_ge(s_adj1[u], t2 * 16 + 16)
                                src = bias[u]
                            else:
                                pe.wait_ge(s_ee, i * 2 + 2)
                                src = prob[0]

                            def agg(g):
                                pe.wait_ge(s_cp[g % 2], it * 8 + h * 4 + g // 2 + 1)
                                for b in range(GROUPS[g]):
                                    k = START[g] + b
                                    mm = nc.tensor.matmul(S[h][:, 0:D], PT[h][:, k * P:(k + 1) * P], xs[:, k, :],
                                                          start=k == 0, stop=k == NT - 1)
                                return mm

                            for g in range(8):
                                pe.wait_ge(s_cp[g % 2], it * 8 + h * 4 + g // 2)
                                for b in range(GROUPS[g]):
                                    k = START[g] + b
                                    mm = nc.tensor.transpose(T[g % 2][:, b * P:(b + 1) * P], src[:, k * P:(k + 1) * P], ident[:])
                                mm.then_inc(s_tr[g % 2], 1)
                                if g:
                                    agg(g - 1)
                            agg(7).then_inc(s_z, 1)
                        pe.wait_ge(s_zs, i + 1)
                        for q in range(4):
                            mm = nc.tensor.transpose(S[2][:, q * P:(q + 1) * P], zs[:, q // 2, (q % 2) * P:(q % 2 + 1) * P], ident[:])
                        mm.then_inc(s_zT, 1)
                        pe.wait_ge(s_zTc, i + 1)
                        pe.wait_ge(s_y, i)
                        for dc in range(DC):
                            nc.tensor.matmul(R[:, 0:D], zT[:, 2 + dc, :], wsa[:, dc, :], start=dc == 0, stop=dc == DC - 1)
                        for dc in range(DC):
                            nc.tensor.matmul(R[:, D:2 * D], zT[:, dc, :], wgcn[:, dc, :], start=dc == 0, stop=dc == DC - 1)
                        for dc in range(DC):
                            mm = nc.tensor.matmul(O[:, 0:2], zT[:, dc, :], wab[:, dc, :], start=dc == 0, stop=dc == DC - 1)
                        mm.then_inc(s_f, 1)

            @block.scalar
            def _(act):
                with act.Fori(0, NHP) as hp:
                    act.wait_ge(s_taken, hp * PER_HP + PROJ + 4)
                    with act.Fori(0, NT) as i:
                        it = hp * NT + i
                        act.wait_ge(s_chunk, hp * PER_HP + i * (2 * NCH) + PROJ)
                        nc.scalar.activation(qtile[:], QT[:, bass.ds(i * P, P)], ACT.Copy, scale=KD ** -0.5).then_inc(s_q, 1)
                        for h in range(2):
                            act.wait_ge(s_max, it * 2 + h + 1)
                            nc.scalar.activation(prob[h][:], prob[h][:], ACT.Exp, bias=negmax[:, h:h + 1],
                                                 accum_out=rowsum[:, h:h + 1]).then_inc(s_exp, 1)
                        for h in range(2):
                            for g in range(0, 8, 2):
                                act.wait_ge(s_tr[0], it * 8 + h * 4 + g // 2 + 1)
                                w = GROUPS[g] * P
                                nc.scalar.activation(PT[h][:, START[g] * P:START[g] * P + w], T[0][:, 0:w], ACT.Copy).then_inc(s_cp[0], 1)
                            act.wait_ge(s_pv, it * 2 + h + 1)
                            nc.scalar.activation(oT[h * KD:(h + 1) * KD, :], O[h * KD:(h + 1) * KD, 0:P], ACT.Copy).then_inc(s_oT, 1)

                act.wait_ge(s_var, 1)
                nc.scalar.activation(std[:], std[:], ACT.Sqrt).then_inc(s_std, 1)
                with act.Fori(0, NT // 2) as t2:
                    for u in range(2):
                        i = t2 * 2 + u
                        it = NHP * NT + t2 * 2 + u
                        for h in range(2):
                            if h == 1:
                                act.wait_ge(s_leak, i + 1)
                                nc.scalar.activation(prob[1][:], prob[1][:], ACT.Exp, scale=-1.0).then_inc(s_ee, 1)
                            for g in range(0, 8, 2):
                                act.wait_ge(s_tr[0], it * 8 + h * 4 + g // 2 + 1)
                                w = GROUPS[g] * P
                                nc.scalar.activation(PT[h][:, START[g] * P:START[g] * P + w], T[0][:, 0:w], ACT.Copy).then_inc(s_cp[0], 1)
                        act.wait_ge(s_zT, i + 1)
                        nc.scalar.activation(zT[:].rearrange("p a b -> p (a b)"), S[2][:], ACT.Copy).then_inc(s_zTc, 1)
                        act.wait_ge(s_gz, i + 1)
                        nc.scalar.activation(gate[:], gate[:], ACT.Exp, scale=-1.0).then_inc(s_ge, 1)
                        act.wait_ge(s_y, i + 1)
                        nc.scalar.activation(yt[:], yt[:], ACT.Exp, scale=-1.0).then_inc(s_ye, 1)
                act.wait_ge(s_var, 2)
                nc.scalar.activation(std[:], std[:], ACT.Sqrt).then_inc(s_std, 1)

            @block.vector
            def _(dve):
                for b in range(4):
                    nc.vector.memset(S[b][:], 0.0).then_inc(s_taken, 1)
                dve.wait_ge(s_x, 32)
                dve.wait_ge(s_id, 4)
                with dve.Fori(0, NHP) as hp:
                    n = 0
                    for buf in (QT, KT):
                        for c in range(NCH):
                            dve.wait_ge(s_chunk, hp * PER_HP + n + 1)
                            nc.vector.tensor_copy(buf[:, c * CW:(c + 1) * CW], S[n % 4][:, 0:CW]).then_inc(s_taken, 1)
                            n += 1
                    for g in range(8):
                        dve.wait_ge(s_chunk, hp * PER_HP + n + 1)
                        w = GROUPS[g] * P
                        nc.vector.tensor_copy(V[:, START[g]:START[g] + GROUPS[g], :].rearrange("p a b -> p (a b)"),
                                              S[n % 4][:, 0:w]).then_inc(s_taken, 1)
                        n += 1
                    with dve.Fori(0, NT // 2) as t2:
                        for u in range(2):
                            it = hp * NT + t2 * 2 + u
                            base = hp * PER_HP + t2 * (4 * NCH) + u * 2 * NCH + PROJ
                            it2 = hp * (NT // 2) + t2
                            dve.wait_ge(s_adj[u], it2 * 16 + 16)
                            nc.vector.tensor_scalar(bias[u][:], bias[u][:], BIG, -BIG, ALU.mult, ALU.add).then_inc(s_bias[u], 1)
                            dve.wait_ge(s_bias[u], it2 * 2 + 1)
                            diag = bias[u][:, bass.ds((t2 * 2 + u) * P, P)]
                            nc.vector.tensor_tensor(diag, diag, eye_bias[:], ALU.max).then_inc(s_bias[u], 1)
                            dve.wait_ge(s_bias[u], it2 * 2 + 2)
                            for h in range(2):
                                for c in range(NCH):
                                    m = h * NCH + c
                                    dve.wait_ge(s_chunk, base + m + 1)
                                    nc.vector.tensor_tensor(prob[h][:, c * CW:(c + 1) * CW], S[m % 4][:, 0:CW],
                                                            bias[u][:, c * CW:(c + 1) * CW], ALU.add).then_inc(s_taken, 1)
                                dve.wait_ge(s_taken, base + h * NCH + NCH + 4)
                                top = nc.vector.reduce_max(rowmax[:, h:h + 1], prob[h][:], AX_X)
                                if h == 0:
                                    top.then_inc(s_dve, 1)
                                    dve.wait_ge(s_dve, it + 1)
                                else:
                                    top.then_inc(s_bias_used[u], 1)
                                    dve.wait_ge(s_bias_used[u], hp * (NT // 2) + t2 + 1)
                                nc.vector.tensor_scalar(negmax[:, h:h + 1], rowmax[:, h:h + 1], -1.0, None,
                                                        ALU.mult).then_inc(s_max, 1)
                            for h in range(2):
                                for g in range(1, 8, 2):
                                    dve.wait_ge(s_tr[1], it * 8 + h * 4 + g // 2 + 1)
                                    w = GROUPS[g] * P
                                    nc.vector.tensor_copy(PT[h][:, START[g] * P:START[g] * P + w], T[1][:, 0:w]).then_inc(s_cp[1], 1)
                                dve.wait_ge(s_exp, it * 2 + h + 1)
                                nc.vector.reciprocal(rinv[:, h:h + 1], rowsum[:, h:h + 1]).then_inc(s_att, 1)
                                dve.wait_ge(s_att, it * 2 + h + 1)
                                dve.wait_ge(s_res, it * 2 + h + 1)
                                row = xs[:, bass.ds(t2 * 2 + u, 1), :].rearrange("p a d -> p (a d)")
                                nc.vector.scalar_tensor_tensor(out=row, in0=R[:, 0:D], scalar=rinv[:, h:h + 1], in1=row,
                                                               op0=ALU.mult, op1=ALU.add).then_inc(s_acc, 1)
                                dve.wait_ge(s_acc, it * 2 + h + 1)

                def layernorm(buf, n0, k):
                    with dve.Fori(0, NT) as t:
                        nc.vector.bn_stats(stats[:, bass.ds(t, 1), :].rearrange("p a d -> p (a d)"),
                                           buf[:, bass.ds(t, 1), :].rearrange("p a d -> p (a d)")).then_inc(s_v, 1)
                    dve.wait_ge(s_v, n0 + NT)
                    for t in range(NT):
                        nc.vector.bn_aggr(mv[:, t, :], stats[:, t, :]).then_inc(s_v, 1)
                    dve.wait_ge(s_v, n0 + 2 * NT)
                    nc.vector.tensor_scalar(std[:], mv[:, :, 1], EPS, None, ALU.add).then_inc(s_var, 1)
                    dve.wait_ge(s_std, k + 1)
                    nc.vector.reciprocal(rstd[:], std[:]).then_inc(s_v, 1)
                    dve.wait_ge(s_v, n0 + 2 * NT + 1)
                    with dve.Fori(0, NT) as t:
                        row = buf[:, bass.ds(t, 1), :].rearrange("p a d -> p (a d)")
                        nc.vector.tensor_scalar(row, row, mv[:, bass.ds(t, 1), 0], rstd[:, bass.ds(t, 1)], ALU.subtract,
                                                ALU.mult).then_inc(s_v, 1)

                layernorm(xs, 0, 0)
                dve.wait_ge(s_coef, 1)
                nc.vector.tensor_copy(coef[:, :, 0:2], R[:, 0:2 * DC].rearrange("p (c k) -> p c k", k=2)).then_inc(s_v, 1)
                nc.vector.tensor_copy(coef[:, :, 2:4], wab[:, DC:2 * DC, :]).then_inc(s_v, 1)
                nc.vector.memset(ones[:], 1.0).then_inc(s_v, 1)
                dve.wait_ge(s_v, NORM0 + 3)
                for dc in range(DC):
                    nc.vector.tensor_scalar(wr_b[:, dc, :], ones[:], coef[:, dc, 1:2], None, ALU.mult).then_inc(s_coef, 1)
                for t in range(NT):
                    dve.wait_ge(s_xT, t + 1)
                    nc.vector.tensor_copy(xTs[:, :, t * P:(t + 1) * P],
                                          S[0][:, 0:D].rearrange("p (c n) -> p c n", c=DC)).then_inc(s_xTc, 1)
                for c in range(NCH):
                    dve.wait_ge(s_sr, c + 1)
                    nc.vector.tensor_copy(SR[:, c * CW:(c + 1) * CW], S[1][:, 0:CW]).then_inc(s_xTc, 1)
                dve.wait_ge(s_node, 1)
                nc.vector.tensor_copy(node[:].rearrange("p t k -> p (t k)"), S[2][:, 0:NT * 4]).then_inc(s_node, 1)
                dve.wait_ge(s_node, 2)
                for k in range(2):
                    nc.vector.tensor_scalar(node[:, :, 2 + k], node[:, :, 2 + k], bab_b[:, k:k + 1], None, ALU.add).then_inc(s_v, 1)
                dve.wait_ge(s_v, HEAD1)
                dve.wait_ge(s_xTc, NT + NCH)
                with dve.Fori(0, NT // 2) as t2:
                    for u in range(2):
                        i = t2 * 2 + u
                        it = NHP * NT + t2 * 2 + u
                        n = 0

                        def step(ins):
                            nonlocal n
                            n += 1
                            ins.then_inc(s_v, 1)
                            dve.wait_ge(s_v, i * STEPS + (HEAD1 + n))

                        def copies(h):
                            for g in range(1, 8, 2):
                                dve.wait_ge(s_tr[1], it * 8 + h * 4 + g // 2 + 1)
                                w = GROUPS[g] * P
                                nc.vector.tensor_copy(PT[h][:, START[g] * P:START[g] * P + w], T[1][:, 0:w]).then_inc(s_cp[1], 1)

                        step(nc.vector.tensor_scalar(prob[1][:], SR[:], node[:, bass.ds(i, 1), 0], None, ALU.add))
                        step(nc.vector.scalar_tensor_tensor(out=prob[1][:], in0=prob[1][:], scalar=0.01, in1=prob[1][:],
                                                            op0=ALU.mult, op1=ALU.max))
                        dve.wait_ge(s_adj1[u], t2 * 16 + 16)
                        nc.vector.tensor_tensor(prob[1][:], prob[1][:], bias[u][:], ALU.mult).then_inc(s_leak, 1)
                        copies(0)
                        dve.wait_ge(s_ee, i * 2 + 1)
                        nc.vector.tensor_tensor_reduce(out=prob[0][:], in0=prob[1][:], in1=bias[u][:], scale=1.0, scalar=0.0,
                                                       op0=ALU.mult, op1=ALU.add, accum_out=esum[:]).then_inc(s_ee, 1)
                        copies(1)
                        dve.wait_ge(s_ee, i * 2 + 2)
                        step(nc.vector.tensor_scalar(esum[:], esum[:], 1e-5, None, ALU.add))
                        step(nc.vector.reciprocal(esum[:], esum[:]))
                        dve.wait_ge(s_z, i * 2 + 2)
                        step(nc.vector.tensor_copy(zs[:, 0, :], S[0][:, 0:D]))
                        nc.vector.tensor_scalar(zs[:, 1, :], S[1][:, 0:D], esum[:, 0:1], None, ALU.mult).then_inc(s_zs, 1)
                        dve.wait_ge(s_f, i + 1)
                        nc.vector.tensor_tensor(gate[:], O[:, 0:2], node[:, bass.ds(i, 1), 2:4].rearrange("p a k -> p (a k)"),
                                                ALU.add).then_inc(s_gz, 1)
                        step(nc.vector.tensor_tensor(yt[:], R[:, D:2 * D], bg_b[:], ALU.add))
                        dve.wait_ge(s_ge, i + 1)
                        step(nc.vector.tensor_scalar(gate[:], gate[:], 1.0, None, ALU.add))
                        step(nc.vector.reciprocal(gate[:], gate[:]))
                        step(nc.vector.tensor_scalar(yt[:], yt[:], gate[:, 1:2], None, ALU.mult))
                        nc.vector.scalar_tensor_tensor(out=yt[:], in0=R[:, 0:D], scalar=gate[:, 0:1], in1=yt[:],
                                                       op0=ALU.mult, op1=ALU.add).then_inc(s_y, 1)
                        dve.wait_ge(s_ye, i + 1)
                        step(nc.vector.tensor_scalar(yt[:], yt[:], 1.0, None, ALU.add))
                        step(nc.vector.reciprocal(yt[:], yt[:]))
                        step(nc.vector.tensor_tensor(ys[:, bass.ds(i, 1), :].rearrange("p a d -> p (a d)"), yt[:],
                                                     xs[:, bass.ds(i, 1), :].rearrange("p a d -> p (a d)"), ALU.add))
                        assert n == STEPS
                layernorm(ys, HEAD1 + NT * STEPS, 1)




def adj_resnorm(nc, x, xT, adj, Wq, Wk, Wv, Wo, W_sa, W_saT, a_sa, W_gcn, b_gcn, Wab, bab, out):
    NP, D = x.shape
    HK = Wq.shape[1]
    kv_table = nc.dram_tensor("kv_table", (NP, 2 * HK), F32, kind="Internal").ap()
    x_table = nc.dram_tensor("x_table", (NP, D + 4), F32, kind="Internal").ap()
    dram = {"x": x, "xT": xT, "adj": adj, "Wq": Wq, "Wk": Wk, "Wv": Wv, "Wo": Wo, "W_sa": W_sa, "W_saT": W_saT, "a_sa": a_sa,
            "W_gcn": W_gcn, "b_gcn": b_gcn, "Wab": Wab, "bab": bab}
    with nc.sbuf_tensor("flag", [P, 1], I32) as flag:
        sparse_path(nc, dram, (kv_table, x_table), flag, out)
        overflow = nc.values_load(flag[0:1, 0:1], min_val=0, max_val=1, skip_runtime_bounds_check_because="it is a comparison's result")
        with nc.If(overflow > 0):
            dense_path(nc, x, xT, adj, Wq, Wk, Wv, Wo, W_sa, W_saT, a_sa, W_gcn, b_gcn, Wab, bab, out)


def kernel(**inputs):
    import numpy as _np
    import concourse.bacc as _bacc
    from concourse import mybir as _mybir
    from concourse.bass_utils import run_bass_kernel_spmd as _run

    a = {k: _np.asarray(v) for k, v in inputs.items()}
    N, D = a["x"].shape
    NP = -(-N // 128) * 128
    x = _np.zeros((NP, D), a["x"].dtype)
    x[:N] = a["x"]
    adj = _np.zeros((NP, NP), a["adj"].dtype)
    adj[:N, :N] = a["adj"]

    def heads_last(w):
        return w.transpose(1, 0, 2).reshape(D, -1)

    laid = {
        "x": x, "xT": x.T, "adj": adj,
        "Wq": heads_last(a["L0_gnn_Wqs"]), "Wk": heads_last(a["L0_gnn_Wks"]), "Wv": heads_last(a["L0_gnn_Wvs"]),
        "Wo": a["L0_gnn_Wo"].reshape(-1, D),
        "W_sa": a["L1_gnn_W_sa"], "W_saT": a["L1_gnn_W_sa"].T, "a_sa": a["L1_gnn_a_sa"].reshape(2, D).T,
        "W_gcn": a["L1_gnn_W_gcnb"], "b_gcn": a["L1_gnn_b_gcnb"],
        "Wab": _np.concatenate([a["L1_gnn_Wa"], a["L1_gnn_Wb"]], 0).T,
        "bab": _np.concatenate([a["L1_gnn_ba"], a["L1_gnn_bb"]]),
    }
    nc = _bacc.Bacc("TRN2", target_bir_lowering=False, num_devices=1)
    arrays, args = {}, []
    for name, v in laid.items():
        v = _np.ascontiguousarray(v)
        arrays[f"in_{name}"] = v
        args.append(nc.dram_tensor(f"in_{name}", v.shape, _mybir.dt.from_np(v.dtype), kind="ExternalInput").ap())
    args.append(nc.dram_tensor("out_0", (NP, D), _mybir.dt.float32, kind="ExternalOutput").ap())
    adj_resnorm(nc, *args)
    r = _run(nc, [arrays], core_ids=[0])
    return r.results[0]["out_0"][:N]
```

```python
from contextlib import ExitStack
from itertools import zip_longest

import concourse.bass as bass
from concourse import mybir

F32 = mybir.dt.float32
BF16 = mybir.dt.bfloat16
U32 = mybir.dt.uint32
I32 = mybir.dt.int32
ALU = mybir.AluOpType
ACT = mybir.ActivationFunctionType
AX_X = mybir.AxisListType.X
P = 128
KD = 64
BIG = 1e16
EPS = 1e-5
SEGS = 4
RANKS = 16
ET = 5
OFF = 8192.0
NONE = -3e4


class Tile:

    def __init__(self, u, b, count):
        self.u, self.b, self.count = u, b, count
        self.t = u * 2 + b

    def at(self, k):
        s = self.b + k
        return Tile(self.u + s // 2, s % 2, self.count)

    def has(self, k):
        return not isinstance(self.u, int) or 0 <= self.t + k < self.count


def sweep(eng, count, lag, body, pairs=1):
    first = max(1, (lag + 1) // 2)
    first += (count // 2 - 1 - first) % pairs
    for t in range(2 * first):
        body(Tile(t // 2, t % 2, count))
    with eng.Fori(first, count // 2 - 1, pairs) as u:
        for k in range(2 * pairs):
            body(Tile(u + k // 2 if k > 1 else u, k % 2, count))
    for t in range(count - 2, count + lag):
        body(Tile(t // 2, t % 2, count))


def wait(eng, sem, value):
    if not isinstance(value, int) or value > 0:
        eng.wait_ge(sem, value)


class Chain:

    def __init__(self, eng, sem, tile, per):
        self.eng, self.sem, self.per, self.base, self.n = eng, sem, per, tile.t * per, 0

    def __call__(self, ins, then=True):
        self.n += 1
        assert self.n <= self.per
        ins.then_inc(self.sem, 1)
        if then:
            self.eng.wait_ge(self.sem, self.base + self.n)

    def join(self):
        self.eng.wait_ge(self.sem, self.base + self.n)


def flat(ap):
    return ap.rearrange("p a b -> p (a b)")


def row(buf, t, n=1):
    return buf[:, bass.ds(t * n, n)]


def sparse_path(nc, dram, scratch, flag, out):
    x, xT, adj = dram["x"], dram["xT"], dram["adj"]
    NP, D = x.shape
    NT = NP // P
    HK = dram["Wq"].shape[1]
    H = HK // KD
    DC = D // P
    HC = HK // P
    SW = NP // SEGS
    SB = SW + 8
    NS = SEGS * 8
    EW = ET * P
    GC = 2 * NS + 2
    XW = D + 4
    kv_table, x_table = scratch
    assert SW * SEGS == NP and NT % 2 == 0 and NT >= 6

    with ExitStack() as ctx:
        def sb(name, shape, dt=F32):
            return ctx.enter_context(nc.sbuf_tensor(name, shape, dt))

        def sem(name):
            return ctx.enter_context(nc.semaphore(name))

        s_passed = sem("f_passed")

        def passed(eng):
            eng.sem_inc(s_passed, 1)

        ident = sb("f_ident", [P, P])
        ones = sb("f_ones", [P, P])
        tri = sb("f_tri", [P, P])
        iota_e = sb("f_iota_e", [P, EW])
        iota_i = sb("f_iota_i", [P, P])
        iota_r = sb("f_iota_r", [P, RANKS])
        edge1 = sb("f_edge1", [P, ET])
        tile0 = sb("f_tile0", [P, NT])
        seg0 = sb("f_seg0", [P, NS])
        xs = sb("f_xs", [P, NT, D])
        Q = sb("f_Q", [P, NT, HK])
        deg_all = sb("f_deg", [P, NT])
        end_all = sb("f_end", [P, NT])
        full_all = sb("f_full", [P, NT * SEGS])
        idx_all = sb("f_idx", [P, NT * ET], U32)
        row1_all = sb("f_row1", [P, NT * ET])
        rank1_all = sb("f_rank1", [P, NT * ET])
        skip_all = sb("f_skip", [P, NT * ET])
        sel_all = sb("f_sel", [P, NT * EW], BF16)
        sel = [sb(f"f_sel{b}", [P, EW]) for b in range(2)]
        selT = [sb(f"f_selT{b}", [P, ET, P]) for b in range(2)]
        idx = [sb(f"f_idx{b}", [P, ET], U32) for b in range(2)]
        ring = sb("f_ring", [P, 2 * ET * 2 * HK])
        stats = sb("f_stats", [P, NT, 6])
        mv = sb("f_mv", [P, NT, 2])
        std = sb("f_std", [P, NT])
        rstd = sb("f_rstd", [P, NT])
        s_const = sem("f_const")
        s_load = sem("f_load")

        with ExitStack() as ph:
            def pb(name, shape):
                return ph.enter_context(nc.psum_tensor(name, shape, F32))

            def sb1(name, shape, dt=F32):
                return ph.enter_context(nc.sbuf_tensor(name, shape, dt))

            adjb = [ring[:, b * SEGS * SB:(b + 1) * SEGS * SB].rearrange("p (s w) -> p s w", s=SEGS) for b in range(2)]
            w0 = 2 * SEGS * SB
            wqkv = ring[:, w0:w0 + 3 * DC * HK].rearrange("p (w c m) -> p w c m", w=3, c=DC)
            ones8 = sb1("f_ones8", [P, 8])
            xt = [sb1(f"f_xt{b}", [P, DC, P]) for b in range(2)]
            kvrow = [sb1(f"f_kvrow{b}", [P, 2 * HK]) for b in range(2)]
            found = sb1("f_found", [P, NS], U32)
            valid = sb1("f_valid", [P, NS])
            count = sb1("f_count", [P, NS])
            end2 = [sb1(f"f_end2{b}", [P, 1]) for b in range(2)]
            G_in = [sb1(f"f_Gin{b}", [P, GC]) for b in range(2)]
            G = sb1("f_G", [P, ET, GC])
            after = sb1("f_after", [P, EW])
            before = sb1("f_before", [P, EW])
            pick = sb1("f_pick", [P, ET, NS])
            node = sb1("f_node", [P, ET])
            same = sb1("f_same", [P, ET])
            beat = sb1("f_beat", [P, 1])
            Bqkv = [pb(f"f_B{w}", [P, 512]) for w in range(3)]
            BG = pb("f_BG", [P, 512])
            BO = pb("f_BO", [P, 512])

            s_ones = sem("f_ones")
            s_adj = [sem(f"f_adj{b}") for b in range(2)]
            s_xt = [sem(f"f_xt{b}") for b in range(2)]
            s_beat = sem("f_beat")
            s_find = sem("f_find")
            s_proj = sem("f_proj")
            s_pcopy = sem("f_pcopy")
            s_kvout = [sem(f"f_kvout{b}") for b in range(2)]
            s_row = sem("f_row")
            s_off = sem("f_off")
            s_end = sem("f_end")
            s_sel = sem("f_sel")
            s_selp = sem("f_selp")
            s_keep = sem("f_keep")
            s_g = sem("f_g")
            s_gcopy = sem("f_gcopy")
            s_edge = sem("f_edge")
            ROWSTEPS, EDGESTEPS = 6, 8

            with nc.Block() as block:
                @block.sync
                def _(sp):
                    def body(tl):
                        u, b, t = tl.u, tl.b, tl.t
                        if tl.has(0):
                            wait(sp, s_find, t - 1)
                            sp.dma_start(adjb[b][:, :, 0:SW], adj[bass.ds(t * P, P), :].rearrange("p (s w) -> p s w", s=SEGS)).then_inc(s_adj[b], 16)
                            wait(sp, s_proj, (t - 1) * 3)
                            passed(sp)
                            sp.dma_start(xt[b][:], xT[:, bass.ds(t * P, P)].rearrange("(c p) n -> p c n", p=P)).then_inc(s_xt[b], 16)
                            if isinstance(t, int) and t == 0:
                                for w, W in enumerate(("Wq", "Wk", "Wv")):
                                    sp.dma_start(wqkv[:, w], dram[W].rearrange("(c p) m -> p c m", p=P)).then_inc(s_load, 16)

                    sweep(sp, NT, 0, body)
                    for b in range(2):
                        sp.wait_ge(s_kvout[b], 16 * (NT // 2))

                @block.gpsimd
                def _(pool):
                    for m, v in ((ident, 0.0), (ones, 1.0), (tri, 1.0)):
                        pool.memset(m[:], v).then_inc(s_const, 1)
                    pool.wait_ge(s_const, 3)
                    pool.affine_select(out=ident[:], in_=ident[:], compare_op=ALU.not_equal, fill=1.0, base=0,
                                       pattern=[[-1, P]], channel_multiplier=1).then_inc(s_const, 1)
                    pool.affine_select(out=tri[:], in_=tri[:], compare_op=ALU.is_gt, fill=0.0, base=0,
                                       pattern=[[1, P]], channel_multiplier=-1).then_inc(s_const, 1)
                    for out_, pattern, base, cm in (
                            (iota_e[:], [[1, EW]], 0, 0), (iota_i[:], [[1, P]], 1, 0), (iota_r[:], [[1, RANKS]], 1, 0),
                            (edge1[:], [[P, ET]], 1, 1), (tile0[:], [[P, NT]], -int(OFF) - 1, 0),
                            (seg0[:].rearrange("p (s k) -> p s k", k=8), [[SW, SEGS], [0, 8]], -int(OFF), 0),
                            (G_in[0][:, GC - 1:GC], [[1, 1]], 1, 1), (G_in[1][:, GC - 1:GC], [[1, 1]], 1, 1)):
                        pool.iota(out_, pattern, base=base, channel_multiplier=cm,
                                  allow_small_or_imprecise_dtypes=True).then_inc(s_const, 1)

                    def body(tl):
                        t, b = tl.t, tl.b
                        wait(pool, s_keep, t - 1)
                        pool.wait_ge(s_end, t * 3 + 3)
                        passed(pool)
                        off = G_in[b][:, GC - 2:GC - 1]
                        pool.tensor_scalar(after[:], iota_e[:], off, None, ALU.is_ge).then_inc(s_selp, 1)
                        pool.tensor_scalar(before[:], iota_e[:], end2[b][:], None, ALU.is_lt).then_inc(s_selp, 1)
                        pool.wait_ge(s_selp, t * 2 + 2)
                        pool.tensor_tensor(sel[b][:], after[:], before[:], ALU.mult).then_inc(s_sel, 1)
                        pool.wait_ge(s_sel, t + 1)
                        passed(pool)

                    sweep(pool, NT, 0, body)

                @block.tensor
                def _(pe):
                    pe.wait_ge(s_load, 48)
                    pe.wait_ge(s_const, 13)

                    def proj(tl, w):
                        for dc in range(DC):
                            mm = nc.tensor.matmul(Bqkv[w][:, 0:HK], xt[tl.b][:, dc, :], wqkv[:, w, dc, :],
                                                  start=dc == 0, stop=dc == DC - 1)
                        mm.then_inc(s_proj, 1)

                    def body(tl):
                        u, b, t = tl.u, tl.b, tl.t
                        if tl.has(-2):
                            q = tl.at(-2)
                            pe.wait_ge(s_sel, q.t + 1)
                            wait(pe, s_gcopy, q.t)
                            for c in range(ET):
                                mm = nc.tensor.matmul(BG[:, c * GC:(c + 1) * GC], sel[q.b][:, c * P:(c + 1) * P], G_in[q.b][:],
                                                      start=True, stop=True)
                            mm.then_inc(s_g, 1)
                        if tl.has(0):
                            pe.wait_ge(s_xt[b], u * 16 + 16)
                            wait(pe, s_pcopy, t * 3 - 1)
                            proj(tl, 0)
                            proj(tl, 1)
                            wait(pe, s_pcopy, t * 3)
                            proj(tl, 2)
                            pe.wait_ge(s_row, t * ROWSTEPS + ROWSTEPS)
                            wait(pe, s_end, t * 3)
                            nc.tensor.matmul(BO[:, 0:1], tri[:], row(deg_all, t), start=True, stop=True).then_inc(s_off, 1)

                    sweep(pe, NT, 2, body)

                @block.scalar
                def _(act):
                    def body(tl):
                        u, b, t = tl.u, tl.b, tl.t
                        if tl.has(-2):
                            q = tl.at(-2)
                            wait(act, s_edge, q.t * EDGESTEPS)
                            act.wait_ge(s_g, q.t + 1)
                            nc.scalar.activation(flat(G[:]), BG[:, 0:ET * GC], ACT.Copy).then_inc(s_gcopy, 1)
                            nc.scalar.activation(row(sel_all, q.t, EW), sel[q.b][:], ACT.Copy).then_inc(s_keep, 1)
                        if tl.has(0):
                            wait(act, s_kvout[b], u * 16)
                            act.wait_ge(s_proj, t * 3 + 2)
                            nc.scalar.activation(kvrow[b][:, 0:HK], Bqkv[1][:, 0:HK], ACT.Copy).then_inc(s_pcopy, 1)
                            nc.scalar.activation(flat(Q[:, bass.ds(t, 1), :]), Bqkv[0][:, 0:HK], ACT.Copy,
                                                 scale=KD ** -0.5).then_inc(s_pcopy, 1)
                            act.wait_ge(s_proj, t * 3 + 3)
                            nc.scalar.activation(kvrow[b][:, HK:2 * HK], Bqkv[2][:, 0:HK], ACT.Copy).then_inc(s_pcopy, 1)
                            act.wait_ge(s_pcopy, t * 3 + 3)
                            passed(act)
                            act.dma_start(kv_table[bass.ds(t * P, P), :], kvrow[b][:]).then_inc(s_kvout[b], 16)

                    sweep(act, NT, 2, body)

                @block.vector
                def _(dve):
                    nc.vector.memset(ones8[:], 1.0).then_inc(s_ones, 1)
                    for b in range(2):
                        nc.vector.memset(adjb[b][:, :, SW:SB], 1.0).then_inc(s_ones, 1)
                    dve.wait_ge(s_ones, 3)
                    dve.wait_ge(s_const, 13)

                    def rows(tl):
                        u, b, t = tl.u, tl.b, tl.t
                        wait(dve, s_g, t - 1)
                        wait(dve, s_end, t * 3)
                        dve.wait_ge(s_adj[b], u * 16 + 16)
                        nc.vector.memset(beat[:], 0.0).then_inc(s_beat, 1)
                        for s in range(SEGS):
                            f = nc.vector.max_index(found[:, s * 8:(s + 1) * 8], ones8[:], adjb[b][:, s, :])
                        f.then_inc(s_find, 1)

                    def rows_steps(tl):
                        b, t = tl.b, tl.t
                        step = Chain(dve, s_row, tl, ROWSTEPS)
                        dve.wait_ge(s_find, t + 1)
                        dve.wait_ge(s_beat, t + 1)
                        step(nc.vector.tensor_scalar(valid[:], found[:], float(SW), None, ALU.is_lt), then=False)
                        step(nc.vector.tensor_tensor(G_in[b][:, 0:NS], found[:], seg0[:], ALU.add), then=False)
                        yield
                        dve.wait_ge(s_row, t * ROWSTEPS + 1)
                        step(nc.vector.tensor_tensor_scan(count[:], ones[:, 0:NS], valid[:], 0.0, ALU.mult, ALU.add), then=False)
                        step(nc.vector.tensor_scalar(row(full_all, t, SEGS), valid[:, 7:NS:8], 1.0, None, ALU.mult), then=False)
                        yield
                        dve.wait_ge(s_row, t * ROWSTEPS + 3)
                        step(nc.vector.tensor_scalar(row(deg_all, t), count[:, NS - 1:NS], 1.0, None, ALU.mult), then=False)
                        step(nc.vector.tensor_tensor(G_in[b][:, NS:2 * NS], count[:], valid[:], ALU.mult), then=False)
                        yield
                        dve.wait_ge(s_off, t + 1)
                        wait(dve, s_sel, t - 1)
                        nc.vector.tensor_tensor(end2[b][:], BO[:, 0:1], count[:, NS - 1:NS], ALU.add).then_inc(s_end, 1)
                        nc.vector.tensor_copy(G_in[b][:, GC - 2:GC - 1], BO[:, 0:1]).then_inc(s_end, 1)
                        nc.vector.tensor_tensor(row(end_all, t), BO[:, 0:1], count[:, NS - 1:NS], ALU.add).then_inc(s_end, 1)

                    def edges_steps(tl):
                        b, t = tl.b, tl.t
                        step = Chain(dve, s_edge, tl, EDGESTEPS)
                        dve.wait_ge(s_gcopy, t + 1)
                        r1 = row(rank1_all, t, ET)
                        step(nc.vector.tensor_tensor(r1, edge1[:], G[:, :, GC - 2], ALU.subtract), then=False)
                        step(nc.vector.tensor_scalar(row(row1_all, t, ET), G[:, :, GC - 1], 1.0, None, ALU.mult), then=False)
                        yield
                        dve.wait_ge(s_edge, t * EDGESTEPS + 1)
                        step(nc.vector.tensor_tensor(pick[:], G[:, :, NS:2 * NS], r1.unsqueeze(2).to_broadcast([P, ET, NS]),
                                                     ALU.is_equal), then=False)
                        yield
                        dve.wait_ge(s_edge, t * EDGESTEPS + 3)
                        step(nc.vector.tensor_tensor(pick[:], pick[:], G[:, :, 0:NS], ALU.mult))
                        step(nc.vector.tensor_reduce(node[:], pick[:], AX_X, ALU.add), then=False)
                        yield
                        dve.wait_ge(s_edge, t * EDGESTEPS + 5)
                        step(nc.vector.scalar_tensor_tensor(out=same[:], in0=row(row1_all, t, ET), scalar=row(tile0, t), in1=node[:],
                                                            op0=ALU.add, op1=ALU.is_equal), then=False)
                        step(nc.vector.tensor_scalar(row(idx_all, t, ET), node[:], OFF, None, ALU.add), then=False)
                        yield
                        dve.wait_ge(s_edge, t * EDGESTEPS + 6)
                        step(nc.vector.tensor_scalar(row(skip_all, t, ET), same[:], NONE, None, ALU.mult), then=False)

                    def body(tl):
                        if tl.has(0):
                            rows(tl)
                        for _ in zip_longest(rows_steps(tl) if tl.has(0) else (), edges_steps(tl.at(-2)) if tl.has(-2) else ()):
                            pass

                    sweep(dve, NT, 2, body)
                    dve.wait_ge(s_edge, NT * EDGESTEPS)
                    dve.wait_ge(s_end, NT * 3)

        with ExitStack() as ph:
            def pb(name, shape):
                return ph.enter_context(nc.psum_tensor(name, shape, F32))

            def sb2(name, shape, dt=F32):
                return ph.enter_context(nc.sbuf_tensor(name, shape, dt))

            kv = [[ring[:, (b * ET + c) * 2 * HK:(b * ET + c + 1) * 2 * HK] for c in range(ET)] for b in range(2)]
            wo = sb2("f_wo", [P, HC, D])
            own = [sb2(f"f_own{b}", [P, 2 * HK]) for b in range(2)]
            prod = [sb2(f"f_prod{b}", [P, HK]) for b in range(2)]
            score = [sb2(f"f_score{b}", [P, ET, H]) for b in range(2)]
            oscore = [sb2(f"f_oscore{b}", [P, H]) for b in range(2)]
            hot = sb2("f_hot", [P, ET, RANKS])
            spread = sb2("f_spread", [P, ET, H, RANKS])
            absent = sb2("f_absent", [P, RANKS])
            byrank = sb2("f_byrank", [P, H, RANKS])
            top = sb2("f_top", [P, H])
            top1 = sb2("f_top1", [P, H])
            top2 = sb2("f_top2", [P, H])
            expo = sb2("f_expo", [P, (ET + 1) * H])
            prob = [sb2(f"f_prob{b}", [P, (ET + 1) * H]) for b in range(2)]
            pv = [sb2(f"f_pv{c}", [P, HK]) for c in range(ET)]
            opv = [sb2(f"f_opv{b}", [P, HK]) for b in range(2)]
            den = sb2("f_den", [P, H])
            top3 = sb2("f_top3", [P, H, 3], BF16)
            rest = sb2("f_rest2", [P, H])
            ranksum = [sb2(f"f_ranksum{b}", [P, H]) for b in range(2)]
            att = sb2("f_att", [P, HK])
            attn = iota_e[:, 0:HK]
            attT = att
            Bq = [pb(f"f_Bq{b}", [P, 512]) for b in range(2)]
            BM, BE, BO, BT, BR, BS = (pb(n, [P, 512]) for n in ("f_BM", "f_BE", "f_BOut", "f_BT", "f_BR", "f_BS"))
            ident_b = sb2("f_ident_b", [P, P], BF16)

            s_clear = sem("f_clear")
            s_clear_dve = sem("f_clear_dve")
            s_wo = sem("f_wo")
            s_xs = sem("f_xs")
            s_stage = sem("f_stage")
            s_kv = [[sem(f"f_kv{b}{c}") for c in range(ET)] for b in range(2)]
            s_own = [sem(f"f_own{b}") for b in range(2)]
            s_qe = sem("f_qe")
            s_mul = sem("f_mul")
            s_dot = sem("f_dot")
            s_ident_b = sem("f_ident_b")
            s_turned = sem("f_turned")
            s_selT = sem("f_selT")
            s_oprod = sem("f_oprod")
            s_oscore = sem("f_oscore")
            s_hot = sem("f_hot")
            s_byrank = sem("f_byrank")
            s_top = sem("f_top")
            s_rowp = sem("f_rowp")
            s_ranksum = sem("f_ranksum")
            TOP = 10
            s_tope = sem("f_tope")
            s_absent = sem("f_absent")
            s_expo = sem("f_expo")
            s_prob = sem("f_prob")
            s_pvp = sem("f_pvp")
            s_pva = sem("f_pva")
            s_opv = sem("f_opv")
            s_out = sem("f_outp")
            s_att = sem("f_att")
            s_attn = sem("f_attn")
            s_stats = sem("f_stats")
            s_attT = sem("f_attT")
            s_attTc = sem("f_attTc")
            s_res = sem("f_res")
            s_sum = sem("f_sum")
            CLEAR = ET * HK
            ON_POOL = 3
            ORDER = (0, 3, 1, 4, 2)

            with nc.Block() as block:
                @block.sync
                def _(sp):
                    sp.dma_start(wo[:], dram["Wo"].rearrange("(c p) d -> p c d", p=P)).then_inc(s_wo, 16)

                    def body(tl):
                        wait(sp, s_opv, tl.t - 1)
                        sp.dma_start(own[tl.b][:], kv_table[bass.ds(tl.t * P, P), :]).then_inc(s_own[tl.b], 16)
                        if isinstance(tl.t, int) and tl.t == 1:
                            sp.wait_ge(s_kv[1][ET - 1], 16)
                            sp.dma_start(xs[:], x.rearrange("(t p) d -> p t d", p=P)).then_inc(s_xs, 16)

                    sweep(sp, NT, 0, body)

                @block.gpsimd
                def _(pool):
                    pool.memset(ring[:, CLEAR:ET * 2 * HK], 0.0).then_inc(s_clear, 1)

                    def gather(tl, c):
                        if c == 0:
                            pool.wait_ge(s_stage, tl.t + 1)
                        if c < ON_POOL:
                            wait(pool, s_pvp, (tl.t - 2) * ON_POOL + c + 1)
                        else:
                            wait(pool, s_pva, (tl.t - 2) * (ET - ON_POOL) + c - ON_POOL + 1)
                        passed(pool)
                        pool.indirect_dma_start(
                            out=kv[tl.b][c], out_offset=None, in_=kv_table,
                            in_offset=bass.IndirectOffsetOnAxis(ap=idx[tl.b][:, c:c + 1], axis=0),
                            bounds_check=NP - 1, oob_is_err=False).then_inc(s_kv[tl.b][c], 16)

                    def product(tl, c):
                        b, t = tl.b, tl.t
                        if c == 0:
                            pool.wait_ge(s_prob, t + 1)
                        wait(pool, s_out, (t - 1) * ET + ORDER.index(c) + 1)
                        pool.tensor_tensor(pv[c][:].rearrange("p (h k) -> p h k", h=H),
                                           kv[b][c][:, HK:2 * HK].rearrange("p (h k) -> p h k", h=H),
                                           prob[b][:, c * H:(c + 1) * H].unsqueeze(2).to_broadcast([P, H, KD]),
                                           ALU.mult).then_inc(s_pvp, 1)

                    def own_values(tl):
                        b, t = tl.b, tl.t
                        wait(pool, s_att, (t - 1) * 3)
                        pool.tensor_tensor(opv[b][:].rearrange("p (h k) -> p h k", h=H),
                                           own[b][:, HK:2 * HK].rearrange("p (h k) -> p h k", h=H),
                                           prob[b][:, ET * H:(ET + 1) * H].unsqueeze(2).to_broadcast([P, H, KD]),
                                           ALU.mult).then_inc(s_opv, 1)

                    def own_keys(tl):
                        pool.wait_ge(s_own[tl.b], tl.u * 16 + 16)
                        wait(pool, s_oscore, tl.t * 2)
                        passed(pool)
                        pool.tensor_tensor(own[tl.b][:, 0:HK], flat(Q[:, bass.ds(tl.t, 1), :]), own[tl.b][:, 0:HK], ALU.mult).then_inc(s_oprod, 1)

                    pool.wait_ge(s_clear, 1)
                    pool.wait_ge(s_clear_dve, 1)
                    for c in range(ET):
                        gather(Tile(0, 0, NT), c)
                    pool.wait_ge(s_clear_dve, 2)

                    def body(tl):
                        if tl.has(0):
                            own_keys(tl)
                        for c in range(ET):
                            if tl.has(-1) and c < ON_POOL:
                                product(tl.at(-1), c)
                            if tl.has(-1) and c == ON_POOL:
                                own_values(tl.at(-1))
                            if tl.has(1):
                                gather(tl.at(1), c)

                    sweep(pool, NT, 1, body)

                @block.scalar
                def _(act):
                    def stage(tl):
                        nc.scalar.activation(idx[tl.b][:], row(idx_all, tl.t, ET), ACT.Copy)
                        nc.scalar.activation(sel[tl.b][:], row(sel_all, tl.t, EW), ACT.Copy).then_inc(s_stage, 1)

                    def values(q, c):
                        wait(act, s_out, (q.t - 1) * ET + ORDER.index(c) + 1)
                        for h in range(H):
                            a = nc.scalar.activation(pv[c][:, h * KD:(h + 1) * KD],
                                                     kv[q.b][c][:, HK + h * KD:HK + (h + 1) * KD], ACT.Copy,
                                                     scale=prob[q.b][:, c * H + h:c * H + h + 1])
                        a.then_inc(s_pva, 1)

                    nc.scalar.activation(ident_b[:], ident[:], ACT.Copy).then_inc(s_ident_b, 1)
                    stage(Tile(0, 0, NT))

                    def body(tl):
                        if tl.has(-1):
                            q = tl.at(-1)
                            act.wait_ge(s_turned, q.t * 2 + 2)
                            nc.scalar.activation(selT[q.b][:, 4, :], BS[:, 0:P], ACT.Copy).then_inc(s_selT, 1)
                        if tl.has(-2):
                            for c in range(ON_POOL + 1, ET):
                                values(tl.at(-2), c)
                        if tl.has(-3):
                            r = tl.at(-3)
                            wait(act, s_attT, r.t)
                            act.wait_ge(s_att, r.t * 3 + 3)
                            for h in range(H):
                                a = nc.scalar.activation(attn[:, h * KD:(h + 1) * KD], att[:, h * KD:(h + 1) * KD], ACT.Copy,
                                                         scale=den[:, h:h + 1])
                            a.then_inc(s_attn, 1)
                        if tl.has(-1):
                            act.wait_ge(s_top, q.t * TOP + TOP)
                            nc.scalar.activation(flat(byrank[:]), flat(byrank[:]), ACT.Exp).then_inc(s_rowp, 1)
                            act.wait_ge(s_expo, q.t * 2 + 2)
                            nc.scalar.activation(prob[q.b][:], expo[:], ACT.Exp).then_inc(s_prob, 1)
                        if tl.has(1):
                            stage(tl.at(1))
                        if tl.has(-3):
                            wait(act, s_res, r.t)
                            act.wait_ge(s_attT, r.t + 1)
                            nc.scalar.activation(attT[:], BT[:, 0:HK], ACT.Copy).then_inc(s_attTc, 1)
                        if tl.has(-1):
                            act.wait_ge(s_prob, q.t + 1)
                            values(q, ON_POOL)
                        if tl.has(0):
                            act.wait_ge(s_turned, tl.t * 2 + 1)
                            wait(act, s_out, (tl.t - 1) * ET)
                            nc.scalar.activation(flat(selT[tl.b][:, 0:4, :]), BS[:], ACT.Copy).then_inc(s_selT, 1)

                    sweep(act, NT, 3, body)

                @block.tensor
                def _(pe):
                    pe.wait_ge(s_wo, 16)

                    def queries(tl, cs):
                        for c in cs:
                            wait(pe, s_mul, tl.t * ET + c - 1)
                            if c == 0:
                                pe.wait_ge(s_stage, tl.t + 1)
                            nc.tensor.matmul(Bq[(tl.b * ET + c) % 2][:, 0:HK], sel[tl.b][:, c * P:(c + 1) * P],
                                             flat(Q[:, bass.ds(tl.t, 1), :]), start=True, stop=True).then_inc(s_qe, 1)

                    def sums(tl, ks):
                        for k in ks:
                            c = ORDER[k]
                            if c < ON_POOL:
                                pe.wait_ge(s_pvp, tl.t * ON_POOL + c + 1)
                            else:
                                pe.wait_ge(s_pva, tl.t * (ET - ON_POOL) + c - ON_POOL + 1)
                            nc.tensor.matmul(BO[:, 0:HK], selT[tl.b][:, c, :], pv[c][:], start=k == 0, stop=k == ET - 1).then_inc(s_out, 1)

                    def turn(tl, cs):
                        for c in cs:
                            k = c % 4
                            mm = nc.tensor.matmul(BS[:, k * P:(k + 1) * P], sel_all[:, bass.ds(tl.t * EW + c * P, P)], ident_b[:],
                                                  start=True, stop=True)
                        mm.then_inc(s_turned, 1)

                    pe.wait_ge(s_ident_b, 1)

                    def body(tl):
                        if tl.has(0):
                            queries(tl, range(0, 1))
                        if tl.has(-1):
                            q = tl.at(-1)
                            pe.wait_ge(s_selT, q.t * 2 + 1)
                            turn(q, range(4, ET))
                        if tl.has(0):
                            queries(tl, range(1, 2))
                        if tl.has(-1):
                            wait(pe, s_top, q.t * TOP - TOP + 1)
                            pe.wait_ge(s_selT, q.t * 2 + 2)
                            pe.wait_ge(s_hot, q.t * 3 + 3)
                            for c in range(ET):
                                mm = nc.tensor.matmul(BM[:, 0:H * RANKS], selT[q.b][:, c, :], flat(spread[:, c, :, :]),
                                                      start=c == 0, stop=c == ET - 1)
                            mm.then_inc(s_byrank, 1)
                        if tl.has(0):
                            queries(tl, range(2, 3))
                        if tl.has(-2):
                            r = tl.at(-2)
                            wait(pe, s_att, r.t * 3)
                            sums(r, range(0, 2))
                        if tl.has(-1):
                            wait(pe, s_expo, q.t * 2)
                            pe.wait_ge(s_top, q.t * TOP + TOP)
                            for c in range(ET):
                                mm = nc.tensor.matmul(BE[:, c * H * 3:(c + 1) * H * 3], sel_all[:, bass.ds(q.t * EW + c * P, P)],
                                                      flat(top3[:]), start=True, stop=True)
                            mm.then_inc(s_tope, 1)
                        if tl.has(0):
                            queries(tl, range(3, 4))
                        if tl.has(-3):
                            z = tl.at(-3)
                            wait(pe, s_attTc, z.t)
                            pe.wait_ge(s_attn, z.t + 1)
                            for c in range(HC):
                                mm = nc.tensor.transpose(BT[:, c * P:(c + 1) * P], attn[:, c * P:(c + 1) * P], ident[:])
                            mm.then_inc(s_attT, 1)
                        if tl.has(0):
                            queries(tl, range(4, ET))
                            wait(pe, s_selT, tl.t * 2)
                            turn(tl, range(0, 4))
                        if tl.has(-2):
                            sums(r, range(2, ET))
                        if tl.has(-3):
                            wait(pe, s_sum, z.t)
                            pe.wait_ge(s_attTc, z.t + 1)
                            for c in range(HC):
                                mm = nc.tensor.matmul(BR[:, 0:D], attT[:, c * P:(c + 1) * P], wo[:, c, :],
                                                      start=c == 0, stop=c == HC - 1)
                            mm.then_inc(s_res, 1)

                    sweep(pe, NT, 3, body)

                @block.vector
                def _(dve):
                    nc.vector.memset(ring[:, 0:CLEAR], 0.0).then_inc(s_clear_dve, 1)
                    nc.vector.memset(ring[:, ET * 2 * HK:], 0.0).then_inc(s_clear_dve, 1)

                    def times_keys(tl, c):
                        b, t = tl.b, tl.t
                        n, k = t * ET + c, (b * ET + c) % 2
                        dve.wait_ge(s_kv[b][c], tl.u * 16 + 16)
                        wait(dve, s_dot, n - 1)
                        dve.wait_ge(s_qe, n + 1)
                        nc.vector.tensor_tensor(prod[k][:], Bq[k][:, 0:HK], kv[b][c][:, 0:HK], ALU.mult).then_inc(s_mul, 1)

                    def by_head(tl, c):
                        b, t = tl.b, tl.t
                        n, k = t * ET + c, (b * ET + c) % 2
                        dve.wait_ge(s_mul, n + 1)
                        nc.vector.tensor_reduce(score[b][:, c, :], prod[k][:].rearrange("p (h k) -> p h k", h=H), AX_X,
                                                ALU.add).then_inc(s_dot, 1)

                    def own_scores(tl):
                        step = Chain(dve, s_oscore, tl, 2)
                        dve.wait_ge(s_oprod, tl.t + 1)
                        step(nc.vector.tensor_reduce(top1[:], own[tl.b][:, 0:HK].rearrange("p (h k) -> p h k", h=H), AX_X, ALU.add))
                        step(nc.vector.tensor_scalar(oscore[tl.b][:], top1[:], 0.01, None, ALU.add), then=False)

                    def by_rank(tl):
                        step = Chain(dve, s_hot, tl, 3)
                        dve.wait_ge(s_dot, tl.t * ET + ET)
                        wait(dve, s_byrank, tl.t)
                        step(nc.vector.tensor_tensor(score[tl.b][:], score[tl.b][:], row(skip_all, tl.t, ET).unsqueeze(2).to_broadcast([P, ET, H]),
                                                     ALU.add), then=False)
                        step(nc.vector.tensor_tensor(hot[:], row(rank1_all, tl.t, ET).unsqueeze(2).to_broadcast([P, ET, RANKS]),
                                                     iota_r[:].unsqueeze(1).to_broadcast([P, ET, RANKS]), ALU.is_equal))
                        step(nc.vector.tensor_tensor(spread[:], hot[:].unsqueeze(2).to_broadcast([P, ET, H, RANKS]),
                                                     score[tl.b][:].unsqueeze(3).to_broadcast([P, ET, H, RANKS]), ALU.mult), then=False)

                    def maximum(tl):
                        step = Chain(dve, s_top, tl, TOP)
                        wait(dve, s_tope, tl.t)
                        dve.wait_ge(s_oscore, tl.t * 2 + 2)
                        wait(dve, s_prob, tl.t)
                        wait(dve, s_ranksum, tl.t)
                        nc.vector.tensor_scalar(absent[:], iota_r[:], row(deg_all, tl.t), -1e30, ALU.is_gt, ALU.mult).then_inc(s_absent, 1)
                        dve.wait_ge(s_absent, tl.t + 1)
                        dve.wait_ge(s_byrank, tl.t + 1)
                        step(nc.vector.tensor_tensor(byrank[:], BM[:, 0:H * RANKS].rearrange("p (h r) -> p h r", h=H),
                                                     absent[:].unsqueeze(1).to_broadcast([P, H, RANKS]), ALU.add))
                        step(nc.vector.tensor_reduce(top2[:], byrank[:], AX_X, ALU.max))
                        step(nc.vector.tensor_tensor(top[:], top2[:], oscore[tl.b][:], ALU.max))
                        step(nc.vector.tensor_copy(top3[:, :, 0], top[:]), then=False)
                        step(nc.vector.tensor_tensor(expo[:, ET * H:(ET + 1) * H], oscore[tl.b][:], top[:], ALU.subtract), then=False)
                        dve.wait_ge(s_top, tl.t * TOP + 4)
                        step(nc.vector.tensor_tensor(rest[:], top[:], top3[:, :, 0], ALU.subtract), then=False)

                    def maximum_rest(tl):
                        step = Chain(dve, s_top, tl, TOP)
                        step.n = 6
                        step.join()
                        step(nc.vector.tensor_copy(top3[:, :, 1], rest[:]), then=False)
                        step(nc.vector.tensor_tensor(byrank[:], byrank[:], top[:].unsqueeze(2).to_broadcast([P, H, RANKS]), ALU.subtract),
                             then=False)
                        dve.wait_ge(s_top, tl.t * TOP + 7)
                        step(nc.vector.tensor_tensor(rest[:], rest[:], top3[:, :, 1], ALU.subtract))
                        step(nc.vector.tensor_copy(top3[:, :, 2], rest[:]), then=False)

                    def exponents(tl):
                        step = Chain(dve, s_expo, tl, 2)
                        dve.wait_ge(s_tope, tl.t + 1)
                        wait(dve, s_prob, tl.t)
                        edges = expo[:, 0:ET * H].rearrange("p (c h) -> p c h", c=ET)
                        step(nc.vector.tensor_reduce(expo[:, 0:ET * H], BE[:, 0:ET * H * 3].rearrange("p (e k) -> p e k", k=3), AX_X, ALU.add))
                        step(nc.vector.tensor_tensor(edges, score[tl.b][:], edges, ALU.subtract), then=False)

                    def rank_sums(tl):
                        dve.wait_ge(s_rowp, tl.t + 1)
                        wait(dve, s_att, (tl.t - 1) * 3)
                        nc.vector.tensor_reduce(ranksum[tl.b][:], byrank[:], AX_X, ALU.add).then_inc(s_ranksum, 1)

                    def normalise(tl):
                        step = Chain(dve, s_att, tl, 3)
                        dve.wait_ge(s_ranksum, tl.t + 1)
                        wait(dve, s_res, tl.t)
                        step(nc.vector.tensor_tensor(den[:], ranksum[tl.b][:], prob[tl.b][:, ET * H:(ET + 1) * H], ALU.add))
                        step(nc.vector.reciprocal(den[:], den[:]), then=False)
                        dve.wait_ge(s_opv, tl.t + 1)
                        dve.wait_ge(s_out, tl.t * ET + ET)
                        step(nc.vector.tensor_tensor(att[:], BO[:, 0:HK], opv[tl.b][:], ALU.add), then=False)

                    def residual(tl):
                        if isinstance(tl.t, int) and tl.t == 0:
                            dve.wait_ge(s_xs, 16)
                        wait(dve, s_sum, tl.t)
                        dve.wait_ge(s_res, tl.t + 1)
                        r = flat(xs[:, bass.ds(tl.t, 1), :])
                        nc.vector.tensor_tensor(r, r, BR[:, 0:D], ALU.add).then_inc(s_sum, 1)

                    def statistics(tl):
                        if isinstance(tl.u, int):
                            dve.wait_ge(s_sum, tl.t + 1)
                        nc.vector.bn_stats(flat(stats[:, bass.ds(tl.t, 1), :]), flat(xs[:, bass.ds(tl.t, 1), :])).then_inc(s_stats, 1)

                    def body(tl):
                        if tl.has(0):
                            times_keys(tl, 0)
                            by_head(tl, 0)
                        if tl.has(-1):
                            maximum(tl.at(-1))
                        if tl.has(0):
                            times_keys(tl, 1)
                        if tl.has(-1):
                            maximum_rest(tl.at(-1))
                        if tl.has(0):
                            by_head(tl, 1)
                            times_keys(tl, 2)
                        if tl.has(-1):
                            exponents(tl.at(-1))
                        if tl.has(0):
                            by_head(tl, 2)
                            times_keys(tl, 3)
                            times_keys(tl, 4)
                            by_head(tl, 3)
                            by_head(tl, 4)
                        if tl.has(-1):
                            rank_sums(tl.at(-1))
                        if tl.has(0):
                            by_rank(tl)
                            own_scores(tl)
                        if tl.has(-2):
                            normalise(tl.at(-2))
                        if tl.has(-3):
                            residual(tl.at(-3))
                        if tl.has(-4):
                            statistics(tl.at(-4))

                    sweep(dve, NT, 4, body)
                    dve.wait_ge(s_sum, NT)
                    dve.wait_ge(s_stats, NT)

        x2 = Q[:].rearrange("p t m -> p (t m)")[:, 0:NT * XW].rearrange("p (t w) -> p t w", w=XW)
        PARTS = ((0, NT // 2), (NT // 2, NT - 4), (NT - 4, NT))
        node_all = sb("f_nodes", [P, NT, 4])
        left3 = sb("f_left3", [P, NT, 3], BF16)
        wsa = sb("f_wsa", [P, DC, D])
        wgcn = sb("f_wgcn", [P, DC, D + 2])
        wab = sb("f_wab", [P, 2 * DC, 2])
        bg_b = sb("f_bg", [P, D])
        s_var = sem("f_var")
        s_std = sem("f_std")
        s_norm = sem("f_norm")

        def moments(dve, k):
            n0 = k * (NT + 1)
            for t in range(NT):
                nc.vector.bn_aggr(mv[:, t, :], stats[:, t, :]).then_inc(s_norm, 1)
            dve.wait_ge(s_norm, n0 + NT)
            nc.vector.tensor_scalar(std[:], mv[:, :, 1], EPS, None, ALU.add).then_inc(s_var, 1)
            dve.wait_ge(s_std, k + 1)
            nc.vector.reciprocal(rstd[:], std[:]).then_inc(s_norm, 1)
            dve.wait_ge(s_norm, n0 + NT + 1)

        with ExitStack() as ph:
            def pb(name, shape):
                return ph.enter_context(nc.psum_tensor(name, shape, F32))

            def sb3(name, shape, dt=F32):
                return ph.enter_context(nc.sbuf_tensor(name, shape, dt))

            wsaT = sb3("f_wsaT", [P, DC, D])
            asa = sb3("f_asa", [P, DC, 2])
            bias4 = sb3("f_bias4", [P, 4])
            coef = sb3("f_coef", [P, DC, 4])
            staged = [sb3(f"f_staged{b}", [P, D]) for b in range(2)]
            stagedT = [sb3(f"f_stagedT{b}", [P, DC, P]) for b in range(2)]
            over = sb3("f_over", [P, 3])
            over1 = sb3("f_over1", [P, 1])
            BT = [pb(f"f_B3T{b}", [P, 512]) for b in range(2)]
            BN = [pb(f"f_B3N{b}", [P, 512]) for b in range(2)]
            BC = pb("f_B3C", [P, 512])
            BF = pb("f_B3F", [P, 512])
            s_w3 = sem("f_w3")
            s_w4 = sem("f_w4")
            s_init = sem("f_init")
            s_over = sem("f_over")
            s_oversum = sem("f_oversum")
            s_coef = sem("f_coef")
            s_row3 = sem("f_row3")
            s_t3 = sem("f_t3")
            s_tc3 = sem("f_tc3")
            s_xs3 = sem("f_xs3")
            s_n3 = sem("f_n3")
            s_node3 = sem("f_node3")
            s_xout = sem("f_xout")
            s_parts = sem("f_parts")
            rest = sb3("f_rest", [P, NT])

            with nc.Block() as block:
                @block.sync
                def _(sp):
                    loads = ((wsaT[:], dram["W_saT"].rearrange("(c p) n -> p c n", p=P)), (asa[:], dram["a_sa"].rearrange("(c p) n -> p c n", p=P)),
                             (wab[:], dram["Wab"].rearrange("(c p) n -> p c n", p=P)), (bias4[:, 2:4], dram["bab"].partition_broadcast(P)),
                             (wsa[:], dram["W_sa"].rearrange("(c p) n -> p c n", p=P)), (wgcn[:, :, 0:D], dram["W_gcn"].rearrange("(c p) n -> p c n", p=P)),
                             (wgcn[:, :, D:D + 2], dram["Wab"][0:D, :].rearrange("(c p) n -> p c n", p=P)),
                             (bg_b[:], dram["b_gcn"].partition_broadcast(P)))
                    for k, (dst, src) in enumerate(loads):
                        sp.dma_start(dst, src).then_inc(s_w3 if k < 4 else s_w4, 16)

                    table = x_table.rearrange("(t p) w -> p t w", p=P)
                    for first, last in PARTS:
                        sp.wait_ge(s_node3, last * 2)
                        sp.wait_ge(s_xs3, last)
                        sp.dma_start(table[:, first:last, :], x2[:, first:last, :]).then_inc(s_xout, 16)
                    sp.wait_ge(s_w4, 16 * 4)
                    sp.wait_ge(s_xout, 16 * len(PARTS))

                @block.gpsimd
                def _(pool):
                    pool.memset(bias4[:, 0:2], 0.0).then_inc(s_init, 1)
                    pool.memset(x2[:, :, D + 1:XW], 0.0).then_inc(s_init, 1)
                    pool.memset(ring[:, 0:3 * ET * XW], 0.0).then_inc(s_init, 1)

                @block.tensor
                def _(pe):
                    pe.wait_ge(s_w3, 16 * 4)
                    for dc in range(DC):
                        for oc in range(DC):
                            mm = nc.tensor.matmul(BC[:, dc * 2:dc * 2 + 2], wsaT[:, oc, dc * P:(dc + 1) * P], asa[:, oc, :],
                                                  start=oc == 0, stop=oc == DC - 1)
                    mm.then_inc(s_coef, 1)
                    pe.wait_ge(s_over, 7)
                    nc.tensor.matmul(BF[:, 0:1], ones[:], over1[:], start=True, stop=True).then_inc(s_oversum, 1)
                    pe.wait_ge(s_coef, 3)

                    def body(tl):
                        if tl.has(0):
                            t, b = tl.t, tl.b
                            wait(pe, s_tc3, t - 1)
                            pe.wait_ge(s_row3, t + 1)
                            for dc in range(DC):
                                mm = nc.tensor.transpose(BT[b][:, dc * P:(dc + 1) * P], staged[b][:, dc * P:(dc + 1) * P], ident[:])
                            mm.then_inc(s_t3, 1)
                        if tl.has(-1):
                            q = tl.at(-1)
                            wait(pe, s_node3, q.t * 2 - 2)
                            pe.wait_ge(s_tc3, q.t + 1)
                            for dc in range(DC):
                                mm = nc.tensor.matmul(BN[q.b][:, 0:4], stagedT[q.b][:, dc, :], coef[:, dc, :],
                                                      start=dc == 0, stop=dc == DC - 1)
                            mm.then_inc(s_n3, 1)

                    sweep(pe, NT, 1, body, 2)

                @block.scalar
                def _(act):
                    act.wait_ge(s_var, 1)
                    nc.scalar.activation(std[:], std[:], ACT.Sqrt).then_inc(s_std, 1)

                    def body(tl):
                        t, b = tl.t, tl.b
                        wait(act, s_n3, t - 1)
                        act.wait_ge(s_t3, t + 1)
                        nc.scalar.activation(flat(stagedT[b][:]), BT[b][:, 0:D], ACT.Copy).then_inc(s_tc3, 1)
                        nc.scalar.activation(flat(x2[:, bass.ds(t, 1), 0:D]), staged[b][:], ACT.Copy).then_inc(s_xs3, 1)

                    sweep(act, NT, 0, body, 2)

                @block.vector
                def _(dve):
                    moments(dve, 0)
                    nc.vector.tensor_reduce(over[:, 0:1], full_all[:], AX_X, ALU.max).then_inc(s_over, 1)
                    nc.vector.tensor_reduce(over[:, 1:2], deg_all[:], AX_X, ALU.max).then_inc(s_over, 1)
                    nc.vector.tensor_reduce(over[:, 2:3], end_all[:], AX_X, ALU.max).then_inc(s_over, 1)
                    dve.wait_ge(s_over, 3)
                    for k, most in ((0, 0), (1, RANKS), (2, EW)):
                        nc.vector.tensor_scalar(over[:, k:k + 1], over[:, k:k + 1], float(most), None, ALU.is_gt).then_inc(s_over, 1)
                    dve.wait_ge(s_over, 6)
                    nc.vector.tensor_reduce(over1[:], over[:], AX_X, ALU.add).then_inc(s_over, 1)
                    dve.wait_ge(s_oversum, 1)
                    nc.vector.tensor_scalar(flag[:], BF[:, 0:1], 0.0, None, ALU.is_gt).then_inc(s_over, 1)
                    dve.wait_ge(s_init, 2)
                    dve.wait_ge(s_coef, 1)
                    nc.vector.tensor_copy(coef[:, :, 0:2], BC[:, 0:2 * DC].rearrange("p (c k) -> p c k", k=2)).then_inc(s_coef, 1)
                    nc.vector.tensor_copy(coef[:, :, 2:4], wab[:, DC:2 * DC, :]).then_inc(s_coef, 1)
                    def body(tl):
                        if tl.has(0):
                            t, b = tl.t, tl.b
                            wait(dve, s_xs3, t - 1)
                            nc.vector.tensor_scalar(staged[b][:, 0:D], flat(xs[:, bass.ds(t, 1), :]), mv[:, bass.ds(t, 1), 0],
                                                    rstd[:, bass.ds(t, 1)], ALU.subtract, ALU.mult).then_inc(s_row3, 1)
                        if tl.has(-2):
                            q = tl.at(-2)
                            dve.wait_ge(s_n3, q.t + 1)
                            nc.vector.tensor_tensor(flat(node_all[:, bass.ds(q.t, 1), :]), BN[q.b][:, 0:4], bias4[:], ALU.add).then_inc(s_node3, 1)
                            nc.vector.tensor_scalar(x2[:, bass.ds(q.t, 1), D], BN[q.b][:, 1:2], 1.0, None, ALU.mult).then_inc(s_node3, 1)

                    sweep(dve, NT, 2, body, 2)
                    dve.wait_ge(s_over, 8)
                    dve.wait_ge(s_node3, NT * 2)
                    nc.vector.tensor_copy(left3[:, :, 0], node_all[:, :, 0]).then_inc(s_parts, 1)
                    for k in (1, 2):
                        dve.wait_ge(s_parts, 2 * k - 1)
                        nc.vector.tensor_tensor(rest[:], (node_all[:, :, 0], rest[:])[k - 1], left3[:, :, k - 1], ALU.subtract).then_inc(s_parts, 1)
                        dve.wait_ge(s_parts, 2 * k)
                        nc.vector.tensor_copy(left3[:, :, k], rest[:]).then_inc(s_parts, 1)

        with ExitStack() as ph:
            def pb(name, shape):
                return ph.enter_context(nc.psum_tensor(name, shape, F32))

            def sb4(name, shape, dt=F32):
                return ph.enter_context(nc.sbuf_tensor(name, shape, dt))

            xg = [ring[:, b * ET * XW:(b + 1) * ET * XW].rearrange("p (c w) -> p c w", c=ET) for b in range(2)]
            yg = ring[:, 2 * ET * XW:3 * ET * XW].rearrange("p (c w) -> p c w", c=ET)
            ys = xs
            arg = sb4("f_arg", [P, ET])
            live = sb4("f_live", [P, ET])
            left = sb4("f_left", [P, ET])
            esum = sb4("f_esum", [P, 1])
            zs = sb4("f_zs", [P, 2 * D])
            zT = sb4("f_zT", [P, 4, P])
            gate = sb4("f_gate", [P, 2])
            shift = sb4("f_shift", [P, NT])
            yt = sb4("f_yt", [P, D])
            BE, B1, B2, BZT, BR, BA = (pb(n, [P, 512]) for n in ("f_4E", "f_41", "f_42", "f_4T", "f_4R", "f_4A"))

            s_idx = sem("f_idx4")
            s_xg, HAD = s_kv, NT // 2 * 16
            s_selT = sem("f_selT4")
            s_left = sem("f_left")
            s_arg = sem("f_arg")
            s_w = sem("f_w")
            s_yg = sem("f_yg")
            s_z1 = sem("f_z14")
            s_z = sem("f_z4")
            s_zs = sem("f_zs")
            s_zT = sem("f_zT")
            s_zTc = sem("f_zTc")
            s_f = sem("f_f")
            s_gz = sem("f_gz")
            s_ge = sem("f_ge")
            s_fin = sem("f_fin")
            s_y = sem("f_y")
            s_ye = sem("f_ye")
            s_ylast = sem("f_ylast")
            s_ylast2 = sem("f_ylast2")
            s_shift = sem("f_shift")
            BY_DVE = NT // 2
            CUTS = (0, NT // 8, NT // 3, NT // 2)
            s_out = sem("f_out")
            s_fin2 = sem("f_fin2")
            s_stats = sem("f_stats4")
            FIN = 3

            with nc.Block() as block:
                @block.sync
                def _(sp):
                    out_t = out.rearrange("(t p) d -> p t d", p=P)
                    for first, last in zip(CUTS, CUTS[1:]):
                        sp.wait_ge(s_ylast, last)
                        sp.dma_start(out_t[:, first:last, :], ys[:, first:last, :]).then_inc(s_out, 16)
                        sp.wait_ge(s_ylast2, last)
                        sp.dma_start(out_t[:, BY_DVE + first:BY_DVE + last, :],
                                     ys[:, BY_DVE + first:BY_DVE + last, :]).then_inc(s_out, 16)
                    sp.wait_ge(s_out, 16 * 2 * (len(CUTS) - 1))

                @block.gpsimd
                def _(pool):
                    def gathers(tl):
                        wait(pool, s_z1, tl.t - 1)
                        wait(pool, s_yg, (tl.t - 1) * ET)
                        pool.wait_ge(s_idx, tl.t + 1)
                        passed(pool)
                        for c in range(ET):
                            pool.indirect_dma_start(
                                out=xg[tl.b][:, c, :], out_offset=None, in_=x_table,
                                in_offset=bass.IndirectOffsetOnAxis(ap=idx[tl.b][:, c:c + 1], axis=0),
                                bounds_check=NP - 1, oob_is_err=False).then_inc(s_xg[tl.b][c], 16)

                    gathers(Tile(0, 0, NT))
                    gathers(Tile(0, 1, NT))

                    def body(tl):
                        if tl.has(2):
                            gathers(tl.at(2))

                    sweep(pool, NT, 0, body)

                @block.scalar
                def _(act):
                    def stage_idx(tl):
                        nc.scalar.activation(idx[tl.b][:], row(idx_all, tl.t, ET), ACT.Copy).then_inc(s_idx, 1)

                    stage_idx(Tile(0, 0, NT))
                    stage_idx(Tile(0, 1, NT))

                    def body(tl):
                        if tl.has(0):
                            wait(act, s_z, tl.t)
                            act.wait_ge(s_arg, tl.t * 5 + 5)
                            nc.scalar.activation(yg[:, :, D], arg[:], ACT.Exp, scale=-1.0).then_inc(s_w, 1)
                        if tl.has(-2):
                            r = tl.at(-2)
                            act.wait_ge(s_gz, r.t + 1)
                            nc.scalar.activation(gate[:], gate[:], ACT.Tanh, scale=0.5).then_inc(s_ge, 1)
                        if tl.has(-1):
                            q = tl.at(-1)
                            wait(act, s_f, q.t)
                            act.wait_ge(s_zT, q.t + 1)
                            nc.scalar.activation(flat(zT[:]), BZT[:], ACT.Copy).then_inc(s_zTc, 1)
                        if tl.has(-2):
                            act.wait_ge(s_y, r.t + 1)
                            nc.scalar.activation(yt[:], yt[:], ACT.Tanh, scale=0.5).then_inc(s_ye, 1)
                        if tl.has(2):
                            stage_idx(tl.at(2))

                    sweep(act, NT, 2, body)
                    act.wait_ge(s_var, 2)
                    nc.scalar.activation(std[:], std[:], ACT.Sqrt).then_inc(s_std, 1)
                    act.wait_ge(s_shift, 1)
                    for t in range(BY_DVE, NT):
                        nc.scalar.activation(ys[:, t, :], ys[:, t, :], ACT.Identity, bias=shift[:, t:t + 1],
                                             scale=rstd[:, t:t + 1]).then_inc(s_ylast2, 1)

                @block.tensor
                def _(pe):
                    def body(tl):
                        u, b, t = tl.u, tl.b, tl.t
                        if tl.has(0):
                            wait(pe, s_arg, t * 5 - 4)
                            for c in range(ET):
                                mm = nc.tensor.matmul(BE[:, c * 3:(c + 1) * 3], sel_all[:, bass.ds(t * EW + c * P, P)],
                                                      flat(left3[:, bass.ds(t, 1), :]), start=True, stop=True)
                            mm.then_inc(s_left, 1)
                            wait(pe, s_zs, t * 4)
                            pe.wait_ge(s_selT, t + 1)
                            for c in range(ET):
                                pe.wait_ge(s_xg[b][c], HAD + u * 16 + 16)
                                mm = nc.tensor.matmul(B1[:, 0:D], selT[b][:, c, :], xg[b][:, c, 0:D], start=c == 0, stop=c == ET - 1)
                            mm.then_inc(s_z1, 1)
                        if tl.has(-1):
                            q = tl.at(-1)
                            pe.wait_ge(s_zs, q.t * 4 + 4)
                            wait(pe, s_zTc, q.t)
                            for k in range(2 * DC):
                                mm = nc.tensor.transpose(BZT[:, k * P:(k + 1) * P], zs[:, k * P:(k + 1) * P], ident[:])
                            mm.then_inc(s_zT, 1)
                        if tl.has(0):
                            for c in range(ET):
                                pe.wait_ge(s_yg, t * ET + c + 1)
                                mm = nc.tensor.matmul(B2[:, 0:D + 1], selT[b][:, c, :], yg[:, c, 0:D + 1], start=c == 0, stop=c == ET - 1)
                            mm.then_inc(s_z, 1)
                        if tl.has(-1):
                            pe.wait_ge(s_zTc, q.t + 1)
                            wait(pe, s_y, q.t)
                            for dc in range(DC):
                                nc.tensor.matmul(BR[:, 0:D], zT[:, DC + dc, :], wsa[:, dc, :], start=dc == 0, stop=dc == DC - 1)
                            for dc in range(DC):
                                mm = nc.tensor.matmul(BA[:, 0:D + 2], zT[:, dc, :], wgcn[:, dc, :], start=dc == 0, stop=dc == DC - 1)
                            mm.then_inc(s_f, 1)

                    sweep(pe, NT, 1, body)

                @block.vector
                def _(dve):

                    def build_selT(tl):
                        wait(dve, s_z, tl.t - 1)
                        nc.vector.tensor_tensor(selT[tl.b][:], row(row1_all, tl.t, ET).unsqueeze(2).to_broadcast([P, ET, P]),
                                                iota_i[:].unsqueeze(1).to_broadcast([P, ET, P]), ALU.is_equal).then_inc(s_selT, 1)

                    def weights(tl):
                        b, t = tl.b, tl.t
                        step = Chain(dve, s_arg, tl, 5)
                        dve.wait_ge(s_left, t + 1)
                        wait(dve, s_w, t)
                        step(nc.vector.tensor_reduce(left[:], BE[:, 0:ET * 3].rearrange("p (c k) -> p c k", k=3), AX_X, ALU.add), then=False)
                        step(nc.vector.tensor_scalar(live[:], row(row1_all, t, ET), 1.0, None, ALU.is_ge), then=False)
                        for c in range(ET):
                            dve.wait_ge(s_xg[b][c], HAD + tl.u * 16 + 16)
                        dve.wait_ge(s_arg, t * 5 + 1)
                        step(nc.vector.tensor_tensor(arg[:], left[:], xg[b][:, :, D], ALU.add))
                        step(nc.vector.tensor_tensor(arg[:], arg[:], live[:], ALU.mult))
                        step(nc.vector.scalar_tensor_tensor(out=arg[:], in0=arg[:], scalar=0.01, in1=arg[:], op0=ALU.mult, op1=ALU.max),
                             then=False)

                    def weighted(tl):
                        b, t = tl.b, tl.t
                        dve.wait_ge(s_w, t + 1)
                        for c in range(ET):
                            nc.vector.tensor_scalar(yg[:, c, 0:D], xg[b][:, c, 0:D], yg[:, c, D:D + 1], None, ALU.mult).then_inc(s_yg, 1)

                    def take_sums(tl):
                        t = tl.t
                        step = Chain(dve, s_zs, tl, 4)
                        dve.wait_ge(s_z, t + 1)
                        wait(dve, s_zT, t)
                        step(nc.vector.tensor_scalar(esum[:], B2[:, D:D + 1], 1e-5, None, ALU.add), then=False)
                        step(nc.vector.tensor_copy(zs[:, 0:D], B1[:, 0:D]), then=False)
                        dve.wait_ge(s_zs, t * 4 + 1)
                        step(nc.vector.reciprocal(esum[:], esum[:]))
                        step(nc.vector.tensor_scalar(zs[:, D:2 * D], B2[:, 0:D], esum[:, 0:1], None, ALU.mult), then=False)

                    def gates(tl):
                        t = tl.t
                        step = Chain(dve, s_fin, tl, FIN)
                        wait(dve, s_fin, t * FIN)
                        wait(dve, s_fin2, t * 2)
                        dve.wait_ge(s_f, t + 1)
                        nc.vector.tensor_tensor(gate[:], BA[:, D:D + 2], flat(node_all[:, bass.ds(t, 1), 2:4]), ALU.add).then_inc(s_gz, 1)
                        step(nc.vector.tensor_tensor(yt[:], BA[:, 0:D], bg_b[:], ALU.add), then=False)

                    def mix(tl):
                        t = tl.t
                        dve.wait_ge(s_ge, t + 1)
                        nc.vector.tensor_scalar(gate[:], gate[:], 0.5, 0.5, ALU.mult, ALU.add).then_inc(s_fin, 1)
                        dve.wait_ge(s_fin, t * FIN + 2)
                        nc.vector.tensor_scalar(yt[:], yt[:], gate[:, 1:2], None, ALU.mult).then_inc(s_fin, 1)
                        dve.wait_ge(s_fin, t * FIN + 3)
                        nc.vector.scalar_tensor_tensor(out=yt[:], in0=BR[:, 0:D], scalar=gate[:, 0:1], in1=yt[:],
                                                       op0=ALU.mult, op1=ALU.add).then_inc(s_y, 1)

                    def residual(tl):
                        t = tl.t
                        step = Chain(dve, s_fin2, tl, 2)
                        dve.wait_ge(s_ye, t + 1)
                        step(nc.vector.tensor_scalar(yt[:], yt[:], 0.5, 0.5, ALU.mult, ALU.add))
                        step(nc.vector.tensor_tensor(flat(ys[:, bass.ds(t, 1), :]), yt[:], flat(x2[:, bass.ds(t, 1), 0:D]), ALU.add),
                             then=False)

                    def statistics(tl):
                        if isinstance(tl.u, int):
                            dve.wait_ge(s_fin2, tl.t * 2 + 2)
                        nc.vector.bn_stats(flat(stats[:, bass.ds(tl.t, 1), :]), flat(ys[:, bass.ds(tl.t, 1), :])).then_inc(s_stats, 1)

                    build_selT(Tile(0, 0, NT))

                    def body(tl):
                        if tl.has(0):
                            weights(tl)
                        if tl.has(-2):
                            gates(tl.at(-2))
                        if tl.has(-3):
                            statistics(tl.at(-3))
                        if tl.has(0):
                            weighted(tl)
                        if tl.has(-2):
                            mix(tl.at(-2))
                        if tl.has(1):
                            build_selT(tl.at(1))
                        if tl.has(-2):
                            residual(tl.at(-2))
                        if tl.has(0):
                            take_sums(tl)

                    sweep(dve, NT, 3, body)
                    dve.wait_ge(s_stats, NT)
                    moments(dve, 1)
                    nc.vector.scalar_tensor_tensor(out=shift[:], in0=mv[:, :, 0], scalar=-1.0, in1=rstd[:], op0=ALU.mult,
                                                   op1=ALU.mult).then_inc(s_shift, 1)
                    for t in range(BY_DVE):
                        nc.vector.tensor_scalar(ys[:, t, :], ys[:, t, :], mv[:, t, 0:1], rstd[:, t:t + 1], ALU.subtract,
                                                ALU.mult).then_inc(s_ylast, 1)


def dense_path(nc, x, xT, adj, Wq, Wk, Wv, Wo, W_sa, W_saT, a_sa, W_gcn, b_gcn, Wab, bab, out):
    NP, D = x.shape
    NT = NP // P
    HK = Wq.shape[1]
    KD = 64
    NHP = HK // P
    DC = D // P
    NCH = 8
    CW = NP // NCH
    GROUPS = [4, 3, 3, 3, 4, 3, 3, 3]
    START = [sum(GROUPS[:g]) for g in range(8)]
    assert sum(GROUPS) == NT and NT % 2 == 0 and CW <= 512
    PROJ = 3 * NCH
    PER_HP = PROJ + NT * 2 * NCH
    EPS = 1e-5
    NORM0 = 3 * NT + 1
    HEAD1 = NORM0 + 5
    STEPS = 12
    LAST = HEAD1 + NT * STEPS + NORM0

    with ExitStack() as ctx:
        def sb(name, shape):
            return ctx.enter_context(nc.sbuf_tensor(name, shape, F32))

        def pb(name, shape):
            return ctx.enter_context(nc.psum_tensor(name, shape, F32))

        def sem(name):
            return ctx.enter_context(nc.semaphore(name))

        ident = sb("ident", [P, P])
        eye_bias = sb("eye_bias", [P, P])
        xs = sb("xs", [P, NT, D])
        big = sb("big", [P, 2 * NP])
        xTs = big[:, :].rearrange("p (c n) -> p c n", c=DC)
        wpair = sb("wpair", [P, 3, DC, P])
        wo_s = sb("wo_s", [P, D])
        QK = sb("QK", [P, 2 * NP])
        QT, KT = QK[:, 0:NP], QK[:, NP:2 * NP]
        V = sb("V", [P, NT, P])
        SR = V[:].rearrange("p t m -> p (t m)")
        qtile = sb("qtile", [P, P])
        bias = [sb(f"bias{u}", [P, NP]) for u in range(2)]
        prob = [sb(f"prob{h}", [P, NP]) for h in range(2)]
        PT = [sb(f"PT{h}", [P, NP]) for h in range(2)]
        negmax = sb("negmax", [P, 2])
        rowmax = sb("rowmax", [P, 2])
        rowsum = sb("rowsum", [P, 2])
        rinv = sb("rinv", [P, 2])
        oT = sb("oT", [P, P])
        stats = sb("stats", [P, NT, 6])
        mv = sb("mv", [P, NT, 2])
        std = sb("std", [P, NT])
        rstd = sb("rstd", [P, NT])
        wsa = sb("wsa", [P, DC, D])
        wsaT = sb("wsaT", [P, DC, D])
        asa = sb("asa", [P, DC, 2])
        wgcn = sb("wgcn", [P, DC, D])
        wab = sb("wab", [P, 2 * DC, 2])
        bab_b = sb("bab_b", [P, 2])
        bg_b = sb("bg_b", [P, D])
        coef = sb("coef", [P, DC, 4])
        ones = sb("ones", [P, P])
        wr_b = sb("wr_b", [P, DC, P])
        node = sb("node", [P, NT, 4])
        zs = sb("zs", [P, 2, D])
        zT = sb("zT", [P, 4, P])
        gate = sb("gate", [P, 2])
        esum = sb("esum", [P, 1])
        yt = sb("yt", [P, D])
        ys = QK[:, :].rearrange("p (t d) -> p t d", d=D)

        S = [pb(f"S{b}", [P, 512]) for b in range(4)]
        T = [pb(f"T{b}", [P, 512]) for b in range(2)]
        O = pb("O", [P, 512])
        R = pb("R", [P, 512])

        s_id = sem("s_id")
        s_x = sem("s_x")
        s_w = sem("s_w")
        s_adj = [sem(f"s_adj{u}") for u in range(2)]
        s_bias = [sem(f"s_bias{u}") for u in range(2)]
        s_bias_used = [sem(f"s_bias_used{u}") for u in range(2)]
        s_chunk = sem("s_chunk")
        s_taken = sem("s_taken")
        s_q = sem("s_q")
        s_max = sem("s_max")
        s_dve = sem("s_dve")
        s_exp = sem("s_exp")
        s_tr = [sem(f"s_tr{b}") for b in range(2)]
        s_cp = [sem(f"s_cp{b}") for b in range(2)]
        s_pv = sem("s_pv")
        s_oT = sem("s_oT")
        s_res = sem("s_res")
        s_acc = sem("s_acc")
        s_att = sem("s_att")
        s_v = sem("s_v")
        s_w1 = sem("s_w1")
        s_var = sem("s_var")
        s_std = sem("s_std")
        s_coef = sem("s_coef")
        s_xT = sem("s_xT")
        s_xTc = sem("s_xTc")
        s_sr = sem("s_sr")
        s_node = sem("s_node")
        s_adj1 = [sem(f"s_adj1{u}") for u in range(2)]
        s_leak = sem("s_leak")
        s_ee = sem("s_ee")
        s_z = sem("s_z")
        s_zs = sem("s_zs")
        s_zT = sem("s_zT")
        s_zTc = sem("s_zTc")
        s_f = sem("s_f")
        s_gz = sem("s_gz")
        s_ge = sem("s_ge")
        s_y = sem("s_y")
        s_ye = sem("s_ye")
        s_out = sem("s_out")

        with nc.Block() as block:
            @block.sync
            def _(sp):
                sp.dma_start(xs[:], x.rearrange("(t p) d -> p t d", p=P)).then_inc(s_x, 16)
                sp.dma_start(xTs, xT.rearrange("(c p) n -> p c n", p=P)).then_inc(s_x, 16)
                with sp.Fori(0, NHP) as hp:
                    sp.wait_ge(s_acc, hp * (2 * NT))
                    for w, W in enumerate((Wq, Wk, Wv)):
                        sp.dma_start(wpair[:, w], W.rearrange("(c p) (h m) -> h p c m", p=P, m=P)[bass.ds(hp, 1)].rearrange("h p c m -> (h p) c m")).then_inc(s_w, 16)
                    sp.dma_start(wo_s[:], Wo.rearrange("(h p) d -> h p d", p=P)[bass.ds(hp, 1)].rearrange("h p d -> (h p) d")).then_inc(s_w, 16)
                    with sp.Fori(0, NT // 2) as t2:
                        for u in range(2):
                            sp.wait_ge(s_bias_used[u], hp * (NT // 2) + t2)
                            sp.dma_start(bias[u][:], adj[bass.ds((t2 * 2 + u) * P, P), :]).then_inc(s_adj[u], 16)

                for dst, src in ((wsa[:], W_sa.rearrange("(c p) n -> p c n", p=P)), (wsaT[:], W_saT.rearrange("(c p) n -> p c n", p=P)),
                                 (asa[:], a_sa.rearrange("(c p) n -> p c n", p=P)), (wgcn[:], W_gcn.rearrange("(c p) n -> p c n", p=P)),
                                 (wab[:], Wab.rearrange("(c p) n -> p c n", p=P)), (bab_b[:], bab.partition_broadcast(P)),
                                 (bg_b[:], b_gcn.partition_broadcast(P))):
                    sp.dma_start(dst, src).then_inc(s_w1, 16)
                sp.wait_ge(s_acc, NHP * NT * 2)
                with sp.Fori(0, NT // 2) as t2:
                    for u in range(2):
                        sp.wait_ge(s_z, t2 * 4)
                        sp.dma_start(bias[u][:], adj[bass.ds((t2 * 2 + u) * P, P), :]).then_inc(s_adj1[u], 16)
                sp.wait_ge(s_var, 2)
                sp.wait_ge(s_v, LAST)
                sp.dma_start(out.rearrange("(t p) d -> p t d", p=P), ys[:]).then_inc(s_out, 16)
                sp.wait_ge(s_out, 16)

            @block.gpsimd
            def _(pool):
                pool.memset(ident[:], 0.0).then_inc(s_id, 1)
                pool.memset(eye_bias[:], -BIG).then_inc(s_id, 1)
                pool.wait_ge(s_id, 2)
                for m, one in ((ident, 1.0), (eye_bias, 0.01)):
                    pool.affine_select(out=m[:], in_=m[:], compare_op=ALU.not_equal, fill=one, base=0,
                                       pattern=[[-1, P]], channel_multiplier=1).then_inc(s_id, 1)

            @block.tensor
            def _(pe):
                pe.wait_ge(s_id, 4)
                pe.wait_ge(s_x, 32)
                with pe.Fori(0, NHP) as hp:
                    pe.wait_ge(s_w, hp * 64 + 64)
                    n = 0
                    for w in range(2):
                        for c in range(NCH):
                            pe.wait_ge(s_taken, hp * PER_HP + n + 1)
                            for dc in range(DC):
                                mm = nc.tensor.matmul(S[n % 4][:, 0:CW], wpair[:, w, dc, :], xTs[:, dc, c * CW:(c + 1) * CW],
                                                      start=dc == 0, stop=dc == DC - 1)
                            mm.then_inc(s_chunk, 1)
                            n += 1
                    for g in range(8):
                        pe.wait_ge(s_taken, hp * PER_HP + n + 1)
                        for b in range(GROUPS[g]):
                            k = START[g] + b
                            for dc in range(DC):
                                mm = nc.tensor.matmul(S[n % 4][:, b * P:(b + 1) * P], xTs[:, dc, k * P:(k + 1) * P],
                                                      wpair[:, 2, dc, :], start=dc == 0, stop=dc == DC - 1)
                        mm.then_inc(s_chunk, 1)
                        n += 1
                    with pe.Fori(0, NT) as i:
                        it = hp * NT + i
                        pe.wait_ge(s_q, it + 1)
                        for h in range(2):
                            for c in range(NCH):
                                m = h * NCH + c
                                pe.wait_ge(s_taken, hp * PER_HP + i * (2 * NCH) + PROJ + m + 1)
                                nc.tensor.matmul(S[m % 4][:, 0:CW], qtile[h * KD:(h + 1) * KD, :],
                                                 KT[h * KD:(h + 1) * KD, c * CW:(c + 1) * CW],
                                                 start=True, stop=True).then_inc(s_chunk, 1)
                        for h in range(2):
                            pe.wait_ge(s_exp, it * 2 + h + 1)

                            def pv(g):
                                pe.wait_ge(s_cp[g % 2], it * 8 + h * 4 + g // 2 + 1)
                                for b in range(GROUPS[g]):
                                    k = START[g] + b
                                    mm = nc.tensor.matmul(O[h * KD:(h + 1) * KD, 0:P], V[:, k, h * KD:(h + 1) * KD],
                                                          PT[h][:, k * P:(k + 1) * P], start=k == 0, stop=k == NT - 1)
                                return mm

                            for g in range(8):
                                pe.wait_ge(s_cp[g % 2], it * 8 + h * 4 + g // 2)
                                for b in range(GROUPS[g]):
                                    k = START[g] + b
                                    mm = nc.tensor.transpose(T[g % 2][:, b * P:(b + 1) * P], prob[h][:, k * P:(k + 1) * P], ident[:])
                                mm.then_inc(s_tr[g % 2], 1)
                                if g:
                                    pv(g - 1)
                            pv(7).then_inc(s_pv, 1)
                            pe.wait_ge(s_oT, it * 2 + h + 1)
                            pe.wait_ge(s_acc, it * 2 + h)
                            nc.tensor.matmul(R[:, 0:D], oT[h * KD:(h + 1) * KD, :], wo_s[h * KD:(h + 1) * KD, :],
                                             start=True, stop=True).then_inc(s_res, 1)

                pe.wait_ge(s_w1, 16 * 7)
                pe.wait_ge(s_acc, NHP * NT * 2)
                for dc in range(DC):
                    for oc in range(DC):
                        mm = nc.tensor.matmul(R[:, dc * 2:dc * 2 + 2], wsaT[:, oc, dc * P:(dc + 1) * P], asa[:, oc, :],
                                              start=oc == 0, stop=oc == DC - 1)
                mm.then_inc(s_coef, 1)
                pe.wait_ge(s_v, NORM0)
                for t in range(NT):
                    if t:
                        pe.wait_ge(s_xTc, t)
                    for dc in range(DC):
                        mm = nc.tensor.transpose(S[0][:, dc * P:(dc + 1) * P], xs[:, t, dc * P:(dc + 1) * P], ident[:])
                    mm.then_inc(s_xT, 1)
                pe.wait_ge(s_xTc, NT)
                pe.wait_ge(s_coef, 3)
                for c in range(NCH):
                    if c:
                        pe.wait_ge(s_xTc, NT + c)
                    for dc in range(DC):
                        mm = nc.tensor.matmul(S[1][:, 0:CW], wr_b[:, dc, :], xTs[:, dc, c * CW:(c + 1) * CW],
                                              start=dc == 0, stop=dc == DC - 1)
                    mm.then_inc(s_sr, 1)
                for t in range(NT):
                    for dc in range(DC):
                        mm = nc.tensor.matmul(S[2][:, t * 4:t * 4 + 4], xTs[:, dc, t * P:(t + 1) * P], coef[:, dc, :],
                                              start=dc == 0, stop=dc == DC - 1)
                mm.then_inc(s_node, 1)
                pe.wait_ge(s_node, 2)
                with pe.Fori(0, NT // 2) as t2:
                    for u in range(2):
                        i = t2 * 2 + u
                        it = NHP * NT + t2 * 2 + u
                        for h in range(2):
                            if h == 0:
                                pe.wait_ge(s_adj1[u], t2 * 16 + 16)
                                src = bias[u]
                            else:
                                pe.wait_ge(s_ee, i * 2 + 2)
                                src = prob[0]

                            def agg(g):
                                pe.wait_ge(s_cp[g % 2], it * 8 + h * 4 + g // 2 + 1)
                                for b in range(GROUPS[g]):
                                    k = START[g] + b
                                    mm = nc.tensor.matmul(S[h][:, 0:D], PT[h][:, k * P:(k + 1) * P], xs[:, k, :],
                                                          start=k == 0, stop=k == NT - 1)
                                return mm

                            for g in range(8):
                                pe.wait_ge(s_cp[g % 2], it * 8 + h * 4 + g // 2)
                                for b in range(GROUPS[g]):
                                    k = START[g] + b
                                    mm = nc.tensor.transpose(T[g % 2][:, b * P:(b + 1) * P], src[:, k * P:(k + 1) * P], ident[:])
                                mm.then_inc(s_tr[g % 2], 1)
                                if g:
                                    agg(g - 1)
                            agg(7).then_inc(s_z, 1)
                        pe.wait_ge(s_zs, i + 1)
                        for q in range(4):
                            mm = nc.tensor.transpose(S[2][:, q * P:(q + 1) * P], zs[:, q // 2, (q % 2) * P:(q % 2 + 1) * P], ident[:])
                        mm.then_inc(s_zT, 1)
                        pe.wait_ge(s_zTc, i + 1)
                        pe.wait_ge(s_y, i)
                        for dc in range(DC):
                            nc.tensor.matmul(R[:, 0:D], zT[:, 2 + dc, :], wsa[:, dc, :], start=dc == 0, stop=dc == DC - 1)
                        for dc in range(DC):
                            nc.tensor.matmul(R[:, D:2 * D], zT[:, dc, :], wgcn[:, dc, :], start=dc == 0, stop=dc == DC - 1)
                        for dc in range(DC):
                            mm = nc.tensor.matmul(O[:, 0:2], zT[:, dc, :], wab[:, dc, :], start=dc == 0, stop=dc == DC - 1)
                        mm.then_inc(s_f, 1)

            @block.scalar
            def _(act):
                with act.Fori(0, NHP) as hp:
                    act.wait_ge(s_taken, hp * PER_HP + PROJ + 4)
                    with act.Fori(0, NT) as i:
                        it = hp * NT + i
                        act.wait_ge(s_chunk, hp * PER_HP + i * (2 * NCH) + PROJ)
                        nc.scalar.activation(qtile[:], QT[:, bass.ds(i * P, P)], ACT.Copy, scale=KD ** -0.5).then_inc(s_q, 1)
                        for h in range(2):
                            act.wait_ge(s_max, it * 2 + h + 1)
                            nc.scalar.activation(prob[h][:], prob[h][:], ACT.Exp, bias=negmax[:, h:h + 1],
                                                 accum_out=rowsum[:, h:h + 1]).then_inc(s_exp, 1)
                        for h in range(2):
                            for g in range(0, 8, 2):
                                act.wait_ge(s_tr[0], it * 8 + h * 4 + g // 2 + 1)
                                w = GROUPS[g] * P
                                nc.scalar.activation(PT[h][:, START[g] * P:START[g] * P + w], T[0][:, 0:w], ACT.Copy).then_inc(s_cp[0], 1)
                            act.wait_ge(s_pv, it * 2 + h + 1)
                            nc.scalar.activation(oT[h * KD:(h + 1) * KD, :], O[h * KD:(h + 1) * KD, 0:P], ACT.Copy).then_inc(s_oT, 1)

                act.wait_ge(s_var, 1)
                nc.scalar.activation(std[:], std[:], ACT.Sqrt).then_inc(s_std, 1)
                with act.Fori(0, NT // 2) as t2:
                    for u in range(2):
                        i = t2 * 2 + u
                        it = NHP * NT + t2 * 2 + u
                        for h in range(2):
                            if h == 1:
                                act.wait_ge(s_leak, i + 1)
                                nc.scalar.activation(prob[1][:], prob[1][:], ACT.Exp, scale=-1.0).then_inc(s_ee, 1)
                            for g in range(0, 8, 2):
                                act.wait_ge(s_tr[0], it * 8 + h * 4 + g // 2 + 1)
                                w = GROUPS[g] * P
                                nc.scalar.activation(PT[h][:, START[g] * P:START[g] * P + w], T[0][:, 0:w], ACT.Copy).then_inc(s_cp[0], 1)
                        act.wait_ge(s_zT, i + 1)
                        nc.scalar.activation(zT[:].rearrange("p a b -> p (a b)"), S[2][:], ACT.Copy).then_inc(s_zTc, 1)
                        act.wait_ge(s_gz, i + 1)
                        nc.scalar.activation(gate[:], gate[:], ACT.Exp, scale=-1.0).then_inc(s_ge, 1)
                        act.wait_ge(s_y, i + 1)
                        nc.scalar.activation(yt[:], yt[:], ACT.Exp, scale=-1.0).then_inc(s_ye, 1)
                act.wait_ge(s_var, 2)
                nc.scalar.activation(std[:], std[:], ACT.Sqrt).then_inc(s_std, 1)

            @block.vector
            def _(dve):
                for b in range(4):
                    nc.vector.memset(S[b][:], 0.0).then_inc(s_taken, 1)
                dve.wait_ge(s_x, 32)
                dve.wait_ge(s_id, 4)
                with dve.Fori(0, NHP) as hp:
                    n = 0
                    for buf in (QT, KT):
                        for c in range(NCH):
                            dve.wait_ge(s_chunk, hp * PER_HP + n + 1)
                            nc.vector.tensor_copy(buf[:, c * CW:(c + 1) * CW], S[n % 4][:, 0:CW]).then_inc(s_taken, 1)
                            n += 1
                    for g in range(8):
                        dve.wait_ge(s_chunk, hp * PER_HP + n + 1)
                        w = GROUPS[g] * P
                        nc.vector.tensor_copy(V[:, START[g]:START[g] + GROUPS[g], :].rearrange("p a b -> p (a b)"),
                                              S[n % 4][:, 0:w]).then_inc(s_taken, 1)
                        n += 1
                    with dve.Fori(0, NT // 2) as t2:
                        for u in range(2):
                            it = hp * NT + t2 * 2 + u
                            base = hp * PER_HP + t2 * (4 * NCH) + u * 2 * NCH + PROJ
                            it2 = hp * (NT // 2) + t2
                            dve.wait_ge(s_adj[u], it2 * 16 + 16)
                            nc.vector.tensor_scalar(bias[u][:], bias[u][:], BIG, -BIG, ALU.mult, ALU.add).then_inc(s_bias[u], 1)
                            dve.wait_ge(s_bias[u], it2 * 2 + 1)
                            diag = bias[u][:, bass.ds((t2 * 2 + u) * P, P)]
                            nc.vector.tensor_tensor(diag, diag, eye_bias[:], ALU.max).then_inc(s_bias[u], 1)
                            dve.wait_ge(s_bias[u], it2 * 2 + 2)
                            for h in range(2):
                                for c in range(NCH):
                                    m = h * NCH + c
                                    dve.wait_ge(s_chunk, base + m + 1)
                                    nc.vector.tensor_tensor(prob[h][:, c * CW:(c + 1) * CW], S[m % 4][:, 0:CW],
                                                            bias[u][:, c * CW:(c + 1) * CW], ALU.add).then_inc(s_taken, 1)
                                dve.wait_ge(s_taken, base + h * NCH + NCH + 4)
                                top = nc.vector.reduce_max(rowmax[:, h:h + 1], prob[h][:], AX_X)
                                if h == 0:
                                    top.then_inc(s_dve, 1)
                                    dve.wait_ge(s_dve, it + 1)
                                else:
                                    top.then_inc(s_bias_used[u], 1)
                                    dve.wait_ge(s_bias_used[u], hp * (NT // 2) + t2 + 1)
                                nc.vector.tensor_scalar(negmax[:, h:h + 1], rowmax[:, h:h + 1], -1.0, None,
                                                        ALU.mult).then_inc(s_max, 1)
                            for h in range(2):
                                for g in range(1, 8, 2):
                                    dve.wait_ge(s_tr[1], it * 8 + h * 4 + g // 2 + 1)
                                    w = GROUPS[g] * P
                                    nc.vector.tensor_copy(PT[h][:, START[g] * P:START[g] * P + w], T[1][:, 0:w]).then_inc(s_cp[1], 1)
                                dve.wait_ge(s_exp, it * 2 + h + 1)
                                nc.vector.reciprocal(rinv[:, h:h + 1], rowsum[:, h:h + 1]).then_inc(s_att, 1)
                                dve.wait_ge(s_att, it * 2 + h + 1)
                                dve.wait_ge(s_res, it * 2 + h + 1)
                                row = xs[:, bass.ds(t2 * 2 + u, 1), :].rearrange("p a d -> p (a d)")
                                nc.vector.scalar_tensor_tensor(out=row, in0=R[:, 0:D], scalar=rinv[:, h:h + 1], in1=row,
                                                               op0=ALU.mult, op1=ALU.add).then_inc(s_acc, 1)
                                dve.wait_ge(s_acc, it * 2 + h + 1)

                def layernorm(buf, n0, k):
                    with dve.Fori(0, NT) as t:
                        nc.vector.bn_stats(stats[:, bass.ds(t, 1), :].rearrange("p a d -> p (a d)"),
                                           buf[:, bass.ds(t, 1), :].rearrange("p a d -> p (a d)")).then_inc(s_v, 1)
                    dve.wait_ge(s_v, n0 + NT)
                    for t in range(NT):
                        nc.vector.bn_aggr(mv[:, t, :], stats[:, t, :]).then_inc(s_v, 1)
                    dve.wait_ge(s_v, n0 + 2 * NT)
                    nc.vector.tensor_scalar(std[:], mv[:, :, 1], EPS, None, ALU.add).then_inc(s_var, 1)
                    dve.wait_ge(s_std, k + 1)
                    nc.vector.reciprocal(rstd[:], std[:]).then_inc(s_v, 1)
                    dve.wait_ge(s_v, n0 + 2 * NT + 1)
                    with dve.Fori(0, NT) as t:
                        row = buf[:, bass.ds(t, 1), :].rearrange("p a d -> p (a d)")
                        nc.vector.tensor_scalar(row, row, mv[:, bass.ds(t, 1), 0], rstd[:, bass.ds(t, 1)], ALU.subtract,
                                                ALU.mult).then_inc(s_v, 1)

                layernorm(xs, 0, 0)
                dve.wait_ge(s_coef, 1)
                nc.vector.tensor_copy(coef[:, :, 0:2], R[:, 0:2 * DC].rearrange("p (c k) -> p c k", k=2)).then_inc(s_v, 1)
                nc.vector.tensor_copy(coef[:, :, 2:4], wab[:, DC:2 * DC, :]).then_inc(s_v, 1)
                nc.vector.memset(ones[:], 1.0).then_inc(s_v, 1)
                dve.wait_ge(s_v, NORM0 + 3)
                for dc in range(DC):
                    nc.vector.tensor_scalar(wr_b[:, dc, :], ones[:], coef[:, dc, 1:2], None, ALU.mult).then_inc(s_coef, 1)
                for t in range(NT):
                    dve.wait_ge(s_xT, t + 1)
                    nc.vector.tensor_copy(xTs[:, :, t * P:(t + 1) * P],
                                          S[0][:, 0:D].rearrange("p (c n) -> p c n", c=DC)).then_inc(s_xTc, 1)
                for c in range(NCH):
                    dve.wait_ge(s_sr, c + 1)
                    nc.vector.tensor_copy(SR[:, c * CW:(c + 1) * CW], S[1][:, 0:CW]).then_inc(s_xTc, 1)
                dve.wait_ge(s_node, 1)
                nc.vector.tensor_copy(node[:].rearrange("p t k -> p (t k)"), S[2][:, 0:NT * 4]).then_inc(s_node, 1)
                dve.wait_ge(s_node, 2)
                for k in range(2):
                    nc.vector.tensor_scalar(node[:, :, 2 + k], node[:, :, 2 + k], bab_b[:, k:k + 1], None, ALU.add).then_inc(s_v, 1)
                dve.wait_ge(s_v, HEAD1)
                dve.wait_ge(s_xTc, NT + NCH)
                with dve.Fori(0, NT // 2) as t2:
                    for u in range(2):
                        i = t2 * 2 + u
                        it = NHP * NT + t2 * 2 + u
                        n = 0

                        def step(ins):
                            nonlocal n
                            n += 1
                            ins.then_inc(s_v, 1)
                            dve.wait_ge(s_v, i * STEPS + (HEAD1 + n))

                        def copies(h):
                            for g in range(1, 8, 2):
                                dve.wait_ge(s_tr[1], it * 8 + h * 4 + g // 2 + 1)
                                w = GROUPS[g] * P
                                nc.vector.tensor_copy(PT[h][:, START[g] * P:START[g] * P + w], T[1][:, 0:w]).then_inc(s_cp[1], 1)

                        step(nc.vector.tensor_scalar(prob[1][:], SR[:], node[:, bass.ds(i, 1), 0], None, ALU.add))
                        step(nc.vector.scalar_tensor_tensor(out=prob[1][:], in0=prob[1][:], scalar=0.01, in1=prob[1][:],
                                                            op0=ALU.mult, op1=ALU.max))
                        dve.wait_ge(s_adj1[u], t2 * 16 + 16)
                        nc.vector.tensor_tensor(prob[1][:], prob[1][:], bias[u][:], ALU.mult).then_inc(s_leak, 1)
                        copies(0)
                        dve.wait_ge(s_ee, i * 2 + 1)
                        nc.vector.tensor_tensor_reduce(out=prob[0][:], in0=prob[1][:], in1=bias[u][:], scale=1.0, scalar=0.0,
                                                       op0=ALU.mult, op1=ALU.add, accum_out=esum[:]).then_inc(s_ee, 1)
                        copies(1)
                        dve.wait_ge(s_ee, i * 2 + 2)
                        step(nc.vector.tensor_scalar(esum[:], esum[:], 1e-5, None, ALU.add))
                        step(nc.vector.reciprocal(esum[:], esum[:]))
                        dve.wait_ge(s_z, i * 2 + 2)
                        step(nc.vector.tensor_copy(zs[:, 0, :], S[0][:, 0:D]))
                        nc.vector.tensor_scalar(zs[:, 1, :], S[1][:, 0:D], esum[:, 0:1], None, ALU.mult).then_inc(s_zs, 1)
                        dve.wait_ge(s_f, i + 1)
                        nc.vector.tensor_tensor(gate[:], O[:, 0:2], node[:, bass.ds(i, 1), 2:4].rearrange("p a k -> p (a k)"),
                                                ALU.add).then_inc(s_gz, 1)
                        step(nc.vector.tensor_tensor(yt[:], R[:, D:2 * D], bg_b[:], ALU.add))
                        dve.wait_ge(s_ge, i + 1)
                        step(nc.vector.tensor_scalar(gate[:], gate[:], 1.0, None, ALU.add))
                        step(nc.vector.reciprocal(gate[:], gate[:]))
                        step(nc.vector.tensor_scalar(yt[:], yt[:], gate[:, 1:2], None, ALU.mult))
                        nc.vector.scalar_tensor_tensor(out=yt[:], in0=R[:, 0:D], scalar=gate[:, 0:1], in1=yt[:],
                                                       op0=ALU.mult, op1=ALU.add).then_inc(s_y, 1)
                        dve.wait_ge(s_ye, i + 1)
                        step(nc.vector.tensor_scalar(yt[:], yt[:], 1.0, None, ALU.add))
                        step(nc.vector.reciprocal(yt[:], yt[:]))
                        step(nc.vector.tensor_tensor(ys[:, bass.ds(i, 1), :].rearrange("p a d -> p (a d)"), yt[:],
                                                     xs[:, bass.ds(i, 1), :].rearrange("p a d -> p (a d)"), ALU.add))
                        assert n == STEPS
                layernorm(ys, HEAD1 + NT * STEPS, 1)




def adj_resnorm(nc, x, xT, adj, Wq, Wk, Wv, Wo, W_sa, W_saT, a_sa, W_gcn, b_gcn, Wab, bab, out):
    NP, D = x.shape
    HK = Wq.shape[1]
    kv_table = nc.dram_tensor("kv_table", (NP, 2 * HK), F32, kind="Internal").ap()
    x_table = nc.dram_tensor("x_table", (NP, D + 4), F32, kind="Internal").ap()
    dram = {"x": x, "xT": xT, "adj": adj, "Wq": Wq, "Wk": Wk, "Wv": Wv, "Wo": Wo, "W_sa": W_sa, "W_saT": W_saT, "a_sa": a_sa,
            "W_gcn": W_gcn, "b_gcn": b_gcn, "Wab": Wab, "bab": bab}
    with nc.sbuf_tensor("flag", [P, 1], I32) as flag:
        sparse_path(nc, dram, (kv_table, x_table), flag, out)
        overflow = nc.values_load(flag[0:1, 0:1], min_val=0, max_val=1, skip_runtime_bounds_check_because="it is a comparison's result")
        with nc.If(overflow > 0):
            dense_path(nc, x, xT, adj, Wq, Wk, Wv, Wo, W_sa, W_saT, a_sa, W_gcn, b_gcn, Wab, bab, out)


def kernel(**inputs):
    import numpy as _np
    import concourse.bacc as _bacc
    from concourse import mybir as _mybir
    from concourse.bass_utils import run_bass_kernel_spmd as _run

    a = {k: _np.asarray(v) for k, v in inputs.items()}
    N, D = a["x"].shape
    NP = -(-N // 128) * 128
    x = _np.zeros((NP, D), a["x"].dtype)
    x[:N] = a["x"]
    adj = _np.zeros((NP, NP), a["adj"].dtype)
    adj[:N, :N] = a["adj"]

    def heads_last(w):
        return w.transpose(1, 0, 2).reshape(D, -1)

    laid = {
        "x": x, "xT": x.T, "adj": adj,
        "Wq": heads_last(a["L0_gnn_Wqs"]), "Wk": heads_last(a["L0_gnn_Wks"]), "Wv": heads_last(a["L0_gnn_Wvs"]),
        "Wo": a["L0_gnn_Wo"].reshape(-1, D),
        "W_sa": a["L1_gnn_W_sa"], "W_saT": a["L1_gnn_W_sa"].T, "a_sa": a["L1_gnn_a_sa"].reshape(2, D).T,
        "W_gcn": a["L1_gnn_W_gcnb"], "b_gcn": a["L1_gnn_b_gcnb"],
        "Wab": _np.concatenate([a["L1_gnn_Wa"], a["L1_gnn_Wb"]], 0).T,
        "bab": _np.concatenate([a["L1_gnn_ba"], a["L1_gnn_bb"]]),
    }
    nc = _bacc.Bacc("TRN2", target_bir_lowering=False, num_devices=1)
    arrays, args = {}, []
    for name, v in laid.items():
        v = _np.ascontiguousarray(v)
        arrays[f"in_{name}"] = v
        args.append(nc.dram_tensor(f"in_{name}", v.shape, _mybir.dt.from_np(v.dtype), kind="ExternalInput").ap())
    args.append(nc.dram_tensor("out_0", (NP, D), _mybir.dt.float32, kind="ExternalOutput").ap())
    adj_resnorm(nc, *args)
    r = _run(nc, [arrays], core_ids=[0])
    return r.results[0]["out_0"][:N]
```
